# Optimizing a Trainium2 kernel written in Bass

```python
import numpy as np
import jax
import jax.numpy as jnp

def _softmax(x, axis=-1):
    return jax.nn.softmax(x, axis=axis)

def _gelu(x):
    return jax.nn.gelu(x, approximate=True)

def _silu(x):
    return jax.nn.silu(x)

def _sigmoid(x):
    return jax.nn.sigmoid(x)

def _layernorm(x, axis=-1, eps=1e-05):
    m = jnp.mean(x, axis=axis, keepdims=True)
    v = jnp.var(x, axis=axis, keepdims=True)
    return (x - m) / jnp.sqrt(v + eps)

def _scatter_add(tgt, idx, src, axis=0):
    return tgt.at[idx].add(src)

def _segment_sum(src, seg, n):
    return jax.ops.segment_sum(src, seg, n)
kernel_name = 'mk_early_fusion_d1_tok_img1024_r4_ef8edb'

def setup_inputs(seed: int=0):
    np.random.seed(seed)
    _w = jnp.asarray

    def _rec_inputs():
        import jax
        import jax.numpy as jnp
        _rk = jax.random.key(seed)
        x = -0.00016672 + 0.999947 * jax.random.normal(jax.random.fold_in(_rk, 1), (8, 3, 96, 96), jnp.float32)
        txt = -0.000312475 + 0.578156 * jax.random.normal(jax.random.fold_in(_rk, 2), (8, 128, 256), jnp.float32)
        return (x, txt)
    x, txt = _rec_inputs()

    def _L0_tok_setup():
        import jax, jax.numpy as jnp
        import numpy as np
        IMAGE_SIZE = 96
        PATCH = 16
        N_EMBD = 256
        C = 3
        N_PATCHES = (IMAGE_SIZE // PATCH) ** 2
        PATCH_DIM = C * PATCH * PATCH
        key = jax.random.key(seed)
        kx, kw, kb, kp = jax.random.split(key, 4)
        B = 64
        x = jax.random.normal(kx, (B, C, IMAGE_SIZE, IMAGE_SIZE), dtype=jnp.float32)
        bound = 1.0 / np.sqrt(PATCH_DIM)
        W = jax.random.uniform(kw, (N_EMBD, PATCH_DIM), minval=-bound, maxval=bound, dtype=jnp.float32)
        b = jax.random.uniform(kb, (N_EMBD,), minval=-bound, maxval=bound, dtype=jnp.float32)
        pos_embd = jax.random.normal(kp, (1, N_PATCHES, N_EMBD), dtype=jnp.float32) * 0.02
        return {'x': x, 'W': W, 'b': b, 'pos_embd': pos_embd}
    _L0_tok_all = _L0_tok_setup()
    _L0_tok_in = {k: v for k, v in _L0_tok_all.items() if k in ('W', 'b', 'pos_embd')}
    del _L0_tok_all

    def _L0_attn_setup():
        import jax, jax.numpy as jnp
        import numpy as np
        B, T, D, H = (2, 512, 256, 16)
        HD = D // H
        key = jax.random.key(seed)
        ks = jax.random.split(key, 9)
        w = lambda k, shp: jax.random.normal(k, shp, jnp.float32) * 0.02
        return {'x': jax.random.normal(ks[0], (B, T, D), jnp.float32), 'Wq': w(ks[1], (D, D)), 'bq': jnp.zeros((D,), jnp.float32), 'Wk': w(ks[2], (D, D)), 'bk': jnp.zeros((D,), jnp.float32), 'Wv': w(ks[3], (D, D)), 'bv': jnp.zeros((D,), jnp.float32), 'Wo': w(ks[4], (D, D)), 'bo': jnp.zeros((D,), jnp.float32), 'Wqs': w(ks[5], (3, HD)), 'bqs': jnp.zeros((3,), jnp.float32), 'Wks': w(ks[6], (3, HD)), 'bks': jnp.zeros((3,), jnp.float32), 'Wvs': w(ks[7], (3, HD)), 'bvs': jnp.zeros((3,), jnp.float32), 'temp': jnp.float32(1.0)}
    _L0_attn_all = _L0_attn_setup()
    _L0_attn_in = {k: v for k, v in _L0_attn_all.items() if k in ('Wq', 'bq', 'Wk', 'bk', 'Wv', 'bv', 'Wo', 'bo', 'Wqs', 'bqs', 'Wks', 'bks', 'Wvs', 'bvs', 'temp')}
    del _L0_attn_all

    def _L0_ffn_setup():
        import jax, jax.numpy as jnp
        import numpy as np
        D_MODEL = 256
        D_HIDDEN = 1024
        NUM_EXPERTS = 8
        B, T = (2, 512)
        key = jax.random.key(seed)
        ks = jax.random.split(key, 8)
        s = 0.02
        x = jax.random.normal(ks[0], (B, T, D_MODEL), dtype=jnp.float32)
        Wg = jax.random.normal(ks[1], (D_MODEL, NUM_EXPERTS), dtype=jnp.float32) * s
        bg = jnp.zeros((NUM_EXPERTS,), dtype=jnp.float32)
        W1 = jax.random.normal(ks[2], (NUM_EXPERTS, D_MODEL, D_HIDDEN), dtype=jnp.float32) * s
        b1 = jnp.zeros((NUM_EXPERTS, D_HIDDEN), dtype=jnp.float32)
        W2 = jax.random.normal(ks[3], (NUM_EXPERTS, D_HIDDEN, D_MODEL), dtype=jnp.float32) * s
        b2 = jnp.zeros((NUM_EXPERTS, D_MODEL), dtype=jnp.float32)
        return {'x': x, 'Wg': Wg, 'bg': bg, 'W1': W1, 'b1': b1, 'W2': W2, 'b2': b2}
    _L0_ffn_all = _L0_ffn_setup()
    _L0_ffn_in = {k: v for k, v in _L0_ffn_all.items() if k in ('Wg', 'bg', 'W1', 'b1', 'W2', 'b2')}
    del _L0_ffn_all
    return {'x': x, 'txt': txt, 'L0_tok_W': _L0_tok_in['W'], 'L0_tok_b': _L0_tok_in['b'], 'L0_tok_pos_embd': _L0_tok_in['pos_embd'], 'L0_attn_Wq': _L0_attn_in['Wq'], 'L0_attn_bq': _L0_attn_in['bq'], 'L0_attn_Wk': _L0_attn_in['Wk'], 'L0_attn_bk': _L0_attn_in['bk'], 'L0_attn_Wv': _L0_attn_in['Wv'], 'L0_attn_bv': _L0_attn_in['bv'], 'L0_attn_Wo': _L0_attn_in['Wo'], 'L0_attn_bo': _L0_attn_in['bo'], 'L0_attn_Wqs': _L0_attn_in['Wqs'], 'L0_attn_bqs': _L0_attn_in['bqs'], 'L0_attn_Wks': _L0_attn_in['Wks'], 'L0_attn_bks': _L0_attn_in['bks'], 'L0_attn_Wvs': _L0_attn_in['Wvs'], 'L0_attn_bvs': _L0_attn_in['bvs'], 'L0_attn_temp': _L0_attn_in['temp'], 'L0_ffn_Wg': _L0_ffn_in['Wg'], 'L0_ffn_bg': _L0_ffn_in['bg'], 'L0_ffn_W1': _L0_ffn_in['W1'], 'L0_ffn_b1': _L0_ffn_in['b1'], 'L0_ffn_W2': _L0_ffn_in['W2'], 'L0_ffn_b2': _L0_ffn_in['b2']}

def reference(x, txt, L0_tok_W, L0_tok_b, L0_tok_pos_embd, L0_attn_Wq, L0_attn_bq, L0_attn_Wk, L0_attn_bk, L0_attn_Wv, L0_attn_bv, L0_attn_Wo, L0_attn_bo, L0_attn_Wqs, L0_attn_bqs, L0_attn_Wks, L0_attn_bks, L0_attn_Wvs, L0_attn_bvs, L0_attn_temp, L0_ffn_Wg, L0_ffn_bg, L0_ffn_W1, L0_ffn_b1, L0_ffn_W2, L0_ffn_b2):
    import jax
    import jax.numpy as jnp

    def _L0_tok_ref(x, W, b, pos_embd):
        import jax, jax.numpy as jnp
        import numpy as np
        IMAGE_SIZE = 96
        PATCH = 16
        N_EMBD = 256
        C = 3
        N_PATCHES = (IMAGE_SIZE // PATCH) ** 2
        PATCH_DIM = C * PATCH * PATCH
        B, Cc, H, Wd = x.shape
        p = PATCH
        Hp, Wp = (H // p, Wd // p)
        patches = x.reshape(B, Cc, Hp, p, Wp, p)
        patches = patches.transpose(0, 2, 4, 1, 3, 5)
        patches = patches.reshape(B, Hp * Wp, Cc * p * p)
        out = jnp.einsum('bnd,ed->bne', patches, W) + b + pos_embd
        return out

    def _L0_attn_ref(x, Wq, bq, Wk, bk, Wv, bv, Wo, bo, Wqs, bqs, Wks, bks, Wvs, bvs, temp):
        import jax, jax.numpy as jnp
        import numpy as np
        B, T, D, H = (2, 512, 256, 16)
        HD = D // H
        Bx, Tx, Dx = x.shape
        split = lambda y: y.reshape(Bx, Tx, H, HD).transpose(0, 2, 1, 3)
        q = split(x @ Wq.T + bq)
        k = split(x @ Wk.T + bk)
        v = split(x @ Wv.T + bv)
        q_stp = q @ Wqs.T + bqs
        k3 = k @ Wks.T + bks
        v3 = v @ Wvs.T + bvs
        cross_kv = jnp.cross(k3, v3, axis=-1)
        scores = (jnp.einsum('bhqd,bhkd->bhqk', q, k) + jnp.einsum('bhqc,bhkc->bhqk', q_stp, cross_kv)) * temp
        attn = jax.nn.softmax(scores, axis=-1)
        out = jnp.einsum('bhqk,bhkd->bhqd', attn, v)
        out = out.transpose(0, 2, 1, 3).reshape(Bx, Tx, Dx)
        return out @ Wo.T + bo

    def _L0_ffn_ref(x, Wg, bg, W1, b1, W2, b2):
        import jax, jax.numpy as jnp
        import numpy as np
        D_MODEL = 256
        D_HIDDEN = 1024
        NUM_EXPERTS = 8
        B, T = (2, 512)
        gate_logits = jnp.einsum('btd,de->bte', x, Wg) + bg
        gate_scores = jax.nn.softmax(gate_logits, axis=-1)
        top1_idx = jnp.argmax(gate_scores, axis=-1)
        top1_mask = jax.nn.one_hot(top1_idx, NUM_EXPERTS, dtype=x.dtype)
        top1_weight = jnp.sum(gate_scores * top1_mask, axis=-1, keepdims=True)
        h = jax.nn.silu(jnp.einsum('btd,edh->bteh', x, W1) + b1)
        o = jnp.einsum('bteh,ehd->bted', h, W2) + b2
        y = jnp.sum(o * top1_mask[..., None], axis=2) * top1_weight
        return y
    h = _L0_tok_ref(x, L0_tok_W, L0_tok_b, L0_tok_pos_embd)
    h = jnp.concatenate([h, txt], axis=1)
    h = h + _L0_attn_ref(_layernorm(h, axis=-1), L0_attn_Wq, L0_attn_bq, L0_attn_Wk, L0_attn_bk, L0_attn_Wv, L0_attn_bv, L0_attn_Wo, L0_attn_bo, L0_attn_Wqs, L0_attn_bqs, L0_attn_Wks, L0_attn_bks, L0_attn_Wvs, L0_attn_bvs, L0_attn_temp)
    h = h + _L0_ffn_ref(_layernorm(h, axis=-1), L0_ffn_Wg, L0_ffn_bg, L0_ffn_W1, L0_ffn_b1, L0_ffn_W2, L0_ffn_b2)
    return h

_drawn_inputs = setup_inputs


def setup_inputs(seed=0):
    import zlib

    import numpy as np

    out = dict(_drawn_inputs(seed))
    spreads = {'L0_attn_bq': (0.0, 0.8),
     'L0_attn_bk': (0.0, 0.8),
     'L0_attn_bv': (0.0, 0.1),
     'L0_attn_bo': (0.0, 0.1),
     'L0_attn_bqs': (0.0, 0.8),
     'L0_attn_bks': (0.0, 0.8),
     'L0_attn_bvs': (0.0, 0.8),
     'L0_ffn_bg': (0.0, 0.314),
     'L0_ffn_b1': (0.0, 0.685),
     'L0_ffn_b2': (0.0, 0.1)}
    factors = {'L0_tok_b': 3.19,
     'L0_tok_pos_embd': 3.462,
     'L0_attn_Wq': 4.165,
     'L0_attn_Wk': 4.922,
     'L0_attn_Wv': 2.87,
     'L0_attn_Wqs': 8.0,
     'L0_attn_Wks': 8.0,
     'L0_attn_Wvs': 8.0}
    for name, (base, spread) in spreads.items():
        noise = np.random.default_rng([zlib.crc32(name.encode()), seed]).standard_normal(out[name].shape)
        drawn = base * np.exp(spread * noise) if base else spread * noise
        out[name] = jnp.asarray(drawn.astype(out[name].dtype))
    for name, factor in factors.items():
        out[name] = (out[name] * factor).astype(out[name].dtype)
    return out
```

```python
from contextlib import ExitStack

import numpy as np

import concourse.bass as bass
from concourse import mybir

F32 = mybir.dt.float32
F32R = mybir.dt.float32r
I32 = mybir.dt.int32
ACT = mybir.ActivationFunctionType
ALU = mybir.AluOpType
AX = mybir.AxisListType

B, NIMG, NTXT, D, H, HD = 8, 36, 128, 256, 16, 16
PATCH, CH, IMG = 16, 3, 96
PD = CH * PATCH * PATCH
T = NIMG + NTXT
C = T // 2
NBLK = 2 * B
NTOK = B * T
E, HID = 8, 1024
P = 128
SLOTS = 128
TILES = (NTOK - E) // SLOTS + E
G = 4
DC = D // P
KC = PD // P
HC = HID // P
EB = 3
EPS = 1e-5

CONST = {}
SMALL = {}


def _columns(table, *items):
    at = 0
    for name, width in items:
        table[name] = (at, at + width)
        at += width
    return at


CONST_W = _columns(CONST, ("ident", P), ("before", P), ("iota", P), ("sel", G * P), ("restart", P),
                   ("tile_start", 32), ("full", P), ("tokid", NBLK), ("backward", E))
SMALL_W = _columns(SMALL, ("bq", 2), ("bk", 2), ("bv", 2), ("bk_rows", G), ("bqs_rows", 1),
                   ("bks_rows", 1), ("bvs_rows", 1), ("temp", 1), ("b1", E * HC), ("wg", DC * E))


def host_constants():
    c = np.zeros((P, CONST_W), np.float32)

    def put(name, value):
        a, b = CONST[name]
        c[:value.shape[0], a:b] = value.reshape(value.shape[0], b - a)

    put("ident", np.eye(P, dtype=np.float32))
    put("before", np.triu(np.ones((P, P), np.float32), 1))
    put("iota", np.tile(np.arange(P, dtype=np.float32), (P, 1)))
    sel = np.zeros((P, G, P), np.float32)
    for h in range(H):
        for k in range(3):
            row = 32 * (h % 4) + HD + k
            sel[3 * h + k, h // 4, row] = 1.0
            sel[64 + 3 * h + k, h // 4, row] = -1.0
    put("sel", sel)
    restart = np.ones((P, E, NBLK), np.float32)
    restart[:, :, 0] = 0.0
    put("restart", restart)
    put("tile_start", np.tile(SLOTS * np.arange(32, dtype=np.float32), (P, 1)))
    put("full", np.ones((P, P), np.float32))
    tok = C * np.arange(NBLK, dtype=np.float32)[None, :] + np.arange(P, dtype=np.float32)[:, None] - NTOK
    put("tokid", tok)
    put("backward", np.tile(E - np.arange(E, dtype=np.float32), (P, 1)))
    return c


def program(nc, patches, tok_wt, tok_b, pos3, txt, const, small, wq, wk, wv, wk_pad, wv_t, wo_t, wo_pad, mq, ma, mb,
            bo, bg, w1, w2, b2, out):
    x2_dram = nc.dram_tensor("normed_rows", [NTOK + 1, D], F32).ap()
    h2_dram = nc.dram_tensor("residual_rows", [NTOK + 1, D], F32).ap()
    out_rows = out.rearrange("b t d -> (b t) d")

    with ExitStack() as ctx:
        def sb(name, shape, dt=F32, scope=ctx):
            return scope.enter_context(nc.sbuf_tensor(name, shape, dt))

        def sem(name):
            return ctx.enter_context(nc.semaphore(name))

        bank = [ctx.enter_context(nc.psum_tensor(f"bank{i}", [P, 512], F32)) for i in range(8)]

        Hs = sb("Hs", [C, NBLK, D])
        cst = sb("cst", [P, CONST_W])
        sml = sb("sml", [P, SMALL_W])
        stats = sb("stats", [C, NBLK, 6])
        mv = sb("mv", [C, NBLK, 2])
        sd = sb("sd", [C, NBLK])
        rstd = sb("rstd", [C, NBLK])

        with ExitStack() as st:
            pat_s = sb("pat_s", [P, KC, B * NIMG], F32, st)
            tokw_s = sb("tokw_s", [P, KC, D], F32, st)
            pos_s = sb("pos_s", [EB * NIMG, D], F32, st)
            tokb_s = sb("tokb_s", [EB * NIMG, D], F32, st)
            emb = sb("emb", [EB * NIMG, 3, D], F32, st)
            wq_s = sb("wq_s", [P, 2, D], F32, st)
            wk_s = sb("wk_s", [P, 2, D], F32, st)
            wv_s = sb("wv_s", [P, 2, D], F32, st)
            wkp_s = sb("wkp_s", [P, DC, 512], F32, st)
            wvt_s = sb("wvt_s", [P, DC, D], F32, st)
            wot_s = sb("wot_s", [P, 2, D], F32, st)
            bv_cols = sb("bv_cols", [P, 2, C], F32, st)
            mq_s = sb("mq_s", [P, D], F32, st)
            ma_s = sb("ma_s", [P, 2, P], F32, st)
            mb_s = sb("mb_s", [P, 2, P], F32, st)
            bo_s = sb("bo_s", [C, D], F32, st)
        W1s = sb("W1s", [P, E, DC, HID])

        with ExitStack() as at:
            wqh, wql = (sb(n, [P, DC, 512], F32R, at) for n in ("wqh", "wql"))
            wkh, wkl = (sb(n, [P, DC, 512], F32R, at) for n in ("wkh", "wkl"))
            wch, wcl = (sb(n, [P, DC, 2, P], F32R, at) for n in ("wch", "wcl"))
            wvh, wvl = (sb(n, [P, DC, D], F32R, at) for n in ("wvh", "wvl"))
            wo_s = sb("wo_s", [P, G, D], F32, at)
            sel_r = sb("sel_r", [P, G, P], F32R, at)
            qbias = sb("qbias", [P, G], F32, at)
            cbias = sb("cbias", [P, 2], F32, at)
            obias = sb("obias", [C, D], F32, at)
            xhat = sb("xhat", [P, 2, D], F32, at)
            xth, xtl = (sb(n, [P, DC, T], F32R, at) for n in ("xth", "xtl"))
            crossa = sb("crossa", [P, T], F32, at)
            prod = sb("prod", [P, T], F32, at)
            prodh, prodl = (sb(n, [P, T], F32R, at) for n in ("prodh", "prodl"))
            qh, ql = (sb(n, [P, 2, G, T], F32R, at) for n in ("qh", "ql"))
            kh, kl = (sb(n, [P, G, T], F32R, at) for n in ("kh", "kl"))
            kbh, kbl = (sb(n, [P, 2, G, 4, T], F32R, at) for n in ("kbh", "kbl"))
            V = sb("V", [P, 2, 2, H, 32], F32, at)
            mx = sb("mx", [C, 8, 2, 2], F32, at)
            pr = sb("pr", [P, 4, 2, 2, T], F32, at)
            prt = sb("prt", [P, 4, 2, T], F32, at)
            den = sb("den", [P, T], F32, at)
            rden = sb("rden", [P, T], F32, at)
            AO = sb("AO", [P, G, T], F32, at)

        W2s = sb("W2s", [P, E, HC, D])
        X2 = sb("X2", [C, NBLK, D])
        x2t = sb("x2t", [P, 2, 4, C])
        bg_s = sb("bg_s", [C, E])
        b2_s = sb("b2_s", [P, E, D])
        lg = sb("lg", [C, NBLK, E])
        lgmax = sb("lgmax", [C, NBLK])
        ex = sb("ex", [C, NBLK, E])
        exsum = sb("exsum", [C, NBLK])
        wtop = sb("wtop", [C, NBLK])
        hit = sb("hit", [C, NBLK, E])
        firsthit = sb("firsthit", [C, NBLK])
        onehot = sb("onehot", [C, E, NBLK])
        upto = sb("upto", [C, E, NBLK])
        earlier = sb("earlier", [C, E, NBLK])
        ntiles_cmp = sb("ntiles_cmp", [P, E, 11])
        ntiles = sb("ntiles", [P, E])
        tiles_upto = sb("tiles_upto", [P, E])
        base = sb("base", [P, E])
        posn = sb("posn", [C, E, NBLK])
        pos = sb("pos", [C, NBLK])
        tile_cmp = sb("tile_cmp", [C, NBLK, 17])
        tile_of = sb("tile_of", [C, NBLK])
        slot_of = sb("slot_of", [C, NBLK])
        slot_hot = sb("slot_hot", [C, NBLK, SLOTS])
        tile_hot = sb("tile_hot", [C, NBLK, 2, TILES])
        ids = sb("ids", [P, TILES], I32)
        wslot = sb("wslot", [P, TILES])
        et_cmp = sb("et_cmp", [1, TILES, E])
        et_f = sb("et_f", [1, TILES])
        et = sb("et", [1, TILES], I32)
        gx = sb("gx", [P, D])
        gh = sb("gh", [P, D])
        xt = sb("xt", [P, DC, P])
        z = sb("z", [P, HID])
        b1c = sb("b1c", [P, HC])
        ht = sb("ht", [P, HC, P])
        y1 = sb("y1", [P, D])
        Y = sb("Y", [P, D])

        def con(name, rows=P):
            a, b = CONST[name]
            return cst[0:rows, a:b]

        def smal(name):
            a, b = SMALL[name]
            return sml[:, a:b]

        ident = con("ident")

        ld_pat, ld_const, ld_txt, ld_small, ld_w, ld_img = (sem(n) for n in (
            "ld_pat", "ld_const", "ld_txt", "ld_small", "ld_w", "ld_img"))
        ld_w1, ld_w2, ld_b2, rows_out = (sem(n) for n in ("ld_w1", "ld_w2", "ld_b2", "rows_out"))
        pads_zero = sem("pads_zero")
        emb_ps, emb_done, posb_done = sem("emb_ps"), sem("emb_done"), sem("posb_done")
        fold_ps = sem("fold_ps")
        stats_done, aggr_done, sd_done, rstd_done = (sem(n) for n in ("stats_done", "aggr_done", "sd_done", "rstd_done"))
        parts_hi, parts_done = sem("parts_hi"), sem("parts_done")
        xhat_ok = sem("xhat_ok")
        xt_ps, xth_ok, xtl_ok = sem("xt_ps"), sem("xth_ok"), sem("xtl_ok")
        cr_ps, cra_ok, prod_ok, prodh_ok, prods_ok = (sem(n) for n in ("cr_ps", "cra_ok", "prod_ok", "prodh_ok", "prods_ok"))
        q_ps, qh_ok, ql_ok = sem("q_ps"), sem("qh_ok"), sem("ql_ok")
        k_ps, kh_ok, kl_ok = sem("k_ps"), sem("kh_ok"), sem("kl_ok")
        v_ps, v_ok = sem("v_ps"), sem("v_ok")
        kb_ok = [sem("kb_ok0"), sem("kb_ok1")]
        s_ps, mx_ok, sub_ok, exp_ok = sem("s_ps"), sem("mx_ok"), sem("sub_ok"), sem("exp_ok")
        t_ps, prt_ok, pv_ps = sem("t_ps"), sem("prt_ok"), sem("pv_ps")
        den_ok, rden_ok, ao_ok = sem("den_ok"), sem("rden_ok"), sem("ao_ok")
        o_ps, hb_ok, h_ok = sem("o_ps"), sem("hb_ok"), sem("h_ok")
        dve_step, aggr1, v_zero, bv_spread = sem("dve_step"), sem("aggr1"), sem("v_zero"), sem("bv_spread")
        hot_ok, rank_ps, slots_hot, slots_ps, lgsub_ok, ex_ok = (sem(n) for n in (
            "hot_ok", "rank_ps", "slots_hot", "slots_ps", "lgsub_ok", "ex_ok"))
        x2_ok, g_ps, g_ok, lg_ps = sem("x2_ok"), sem("g_ps"), sem("g_ok"), sem("lg_ps")
        ids_ok, et_ok = sem("ids_ok"), sem("et_ok")
        gx_in, gh_in, sc_out = sem("gx_in"), sem("gh_in"), sem("sc_out")
        tx_ps, tx_ok, l1_ps, z_ok, zt_ps, silu_ok, b1_ok, l2_ps, y1_ok, y_ok = (sem(n) for n in (
            "tx_ps", "tx_ok", "l1_ps", "z_ok", "zt_ps", "silu_ok", "b1_ok", "l2_ps", "y1_ok", "y_ok"))

        NW = 11
        PARTS = [(0, 80), (80, C)]

        def first(b):
            return isinstance(b, int) and b == 0

        def few(b):
            return isinstance(b, int) and b < 2

        def kb_count(b, u):
            return 64 * (b - u) + 128

        block = ctx.enter_context(nc.Block())

        @block.sync
        def _(sp):
            sp.dma_start(pat_s[:, :, :], patches.rearrange("(k p) n -> p k n", p=P)).then_inc(ld_pat, 16)
            sp.dma_start(tokw_s[:, :, :], tok_wt.rearrange("(k p) e -> p k e", p=P)).then_inc(ld_pat, 16)
            sp.dma_start(pos_s[:, :], pos3).then_inc(ld_pat, 16)
            sp.dma_start(tokb_s[:, :], tok_b.partition_broadcast(EB * NIMG)).then_inc(ld_pat, 16)
            for a, b in ((NIMG, 68), (68, C)):
                sp.dma_start(Hs[a:b, 0:NBLK:2, :],
                             txt[:, a - NIMG:b - NIMG, :].rearrange("b p d -> p b d")).then_inc(ld_txt, 16)
            for a, b in PARTS:
                sp.dma_start(Hs[a:b, 1:NBLK:2, :],
                             txt[:, C - NIMG + a:C - NIMG + b, :].rearrange("b p d -> p b d")).then_inc(ld_txt, 16)
            sp.dma_start(cst[:, :], const).then_inc(ld_const, 16)
            sp.dma_start(sml[:, :], small).then_inc(ld_small, 16)
            for dst, src in ((wq_s, wq), (wk_s, wk), (wv_s, wv)):
                sp.dma_start(dst[:, :, :], src.rearrange("(k p) e -> p k e", p=P)).then_inc(ld_w, 16)
            for dst, src in ((wkp_s, wk_pad), (wvt_s, wv_t), (wot_s, wo_t)):
                sp.dma_start(dst[:, :, :], src.rearrange("(k p) e -> p k e", p=P)).then_inc(ld_w, 16)
            sp.dma_start(wo_s[:, :, :], wo_pad.rearrange("(k p) e -> p k e", p=P)).then_inc(ld_w, 16)
            sp.dma_start(mq_s[:, :], mq).then_inc(ld_w, 16)
            sp.dma_start(ma_s[:, :, :], ma).then_inc(ld_w, 16)
            sp.dma_start(mb_s[:, :, :], mb).then_inc(ld_w, 16)
            sp.dma_start(bo_s[:, :], bo.partition_broadcast(C)).then_inc(ld_w, 16)
            for b in range(B):
                m, k = b // EB, b % EB
                if k == 0:
                    sp.wait_ge(emb_done, m + 1)
                sp.dma_start(Hs[0:NIMG, 2 * b, :], emb[NIMG * k:NIMG * (k + 1), m, :]).then_inc(ld_img, 16)

            def k_blocks(pb, u):
                sp.wait_ge(kh_ok, 2 * pb + 2)
                for j in range(4):
                    sp.dma_start(kbh[32 * j:32 * j + 32, u, :, j, :].bitcast(F32),
                                 kh[32 * j:32 * j + 32, :, :].bitcast(F32)).then_inc(kb_ok[u], 16)
                sp.wait_ge(kl_ok, 2 * pb + 2)
                for j in range(4):
                    sp.dma_start(kbl[32 * j:32 * j + 32, u, :, j, :].bitcast(F32),
                                 kl[32 * j:32 * j + 32, :, :].bitcast(F32)).then_inc(kb_ok[u], 16)

            sp.wait_ge(pads_zero, 1)
            k_blocks(0, 0)
            k_blocks(1, 1)
            w1_rows = w1.rearrange("e (k p) n -> e p k n", p=P)
            sp.wait_ge(ld_img, 16 * B)
            for e in range(2):
                sp.dma_start(W1s[:, e, :, :], w1_rows[e]).then_inc(ld_w1, 16)
            with sp.Fori(0, (B - 2) // 2) as i:
                for u in range(2):
                    k_blocks(2 * i + 2 + u, u)
                    sp.dma_start(W1s[:, bass.ds(2 * i + 2 + u, 1), :, :],
                                 w1_rows[bass.ds(2 * i + 2 + u, 1)].rearrange("e p k n -> p e k n")).then_inc(ld_w1, 16)
            sp.wait_ge(h_ok, B)
            for e in range(E):
                sp.dma_start(W2s[:, e, :, :], w2[e].rearrange("(k p) n -> p k n", p=P)).then_inc(ld_w2, 16)
                if e == 0:
                    sp.dma_start(bg_s[:, :], bg.partition_broadcast(C)).then_inc(ld_b2, 16)
                    sp.dma_start(b2_s[:, :, :], b2.partition_broadcast(P)).then_inc(ld_b2, 16)
                    sp.wait_ge(x2_ok, NBLK)
                    for dst, src in ((x2_dram, X2), (h2_dram, Hs)):
                        rows = dst[0:NTOK, :].rearrange("(b p) d -> p b d", p=C)
                        for a, b in PARTS:
                            sp.dma_start(rows[a:b], src[a:b, :, :]).then_inc(rows_out, 16)
                        sp.dma_start(dst[NTOK:NTOK + 1, :], X2[0:1, 0, :]).then_inc(rows_out, 16)

        @block.tensor
        def _(pe):
            mm = nc.tensor.matmul
            pe.wait_ge(ld_pat, 64)
            for m in range(3):
                rows = min(EB, B - EB * m) * NIMG
                for k in range(KC):
                    last = mm(bank[m][0:rows, 0:D], pat_s[:, k, EB * NIMG * m:EB * NIMG * m + rows], tokw_s[:, k, :],
                              start=(k == 0), stop=(k == KC - 1))
                last.then_inc(emb_ps, 1)
            pe.wait_ge(ld_w, 16 * NW)
            pe.wait_ge(ld_small, 16)
            for d in range(DC):
                for i in range(2):
                    mm(bank[3 + d][:, D * i:D * i + D], wq_s[:, i, P * d:P * d + P], mq_s[:, :], start=True, stop=True)
            for d in range(DC):
                for x, (w, m_) in enumerate(((wk_s, ma_s), (wv_s, mb_s))):
                    for i in range(2):
                        mm(bank[5][:, 256 * d + P * x:256 * d + P * x + P], w[:, i, P * d:P * d + P], m_[:, i, :],
                           start=(i == 0), stop=(i == 1))
            for g in range(G):
                mm(bank[6][:, g:g + 1], mq_s[:, P * (g % 2):P * (g % 2) + P], smal("bq")[:, g // 2:g // 2 + 1],
                   start=True, stop=True)
            for x, (m_, b_) in enumerate(((ma_s, "bk"), (mb_s, "bv"))):
                for i in range(2):
                    mm(bank[6][:, 4 + x:5 + x], m_[:, i, :], smal(b_)[:, i:i + 1], start=(i == 0), stop=(i == 1))
            pe.wait_ge(bv_spread, 1)
            for i in range(2):
                last = mm(bank[7][0:C, 0:D], bv_cols[:, i, :], wot_s[:, i, :], start=(i == 0), stop=(i == 1))
            last.then_inc(fold_ps, 1)

            def passes(out_ap, w_hi, w_lo, x_hi, x_lo, more=False):
                terms = [(w, x, d) for w, x in ((w_hi, x_hi), (w_lo, x_hi), (w_hi, x_lo)) for d in range(DC)]
                for n, (w, x, d) in enumerate(terms):
                    last = mm(out_ap, w(d), x(d), start=(n == 0), stop=(not more and n == len(terms) - 1))
                return last

            def turn_x(pb):
                pe.wait_ge(xhat_ok, pb + 1)
                if not first(pb):
                    pe.wait_ge(kl_ok, 2 * pb)
                for c in range(2):
                    for d in range(DC):
                        last = nc.tensor.transpose(bank[6][:, P * (2 * d + c):P * (2 * d + c) + P],
                                                   xhat[:, c, P * d:P * d + P], ident)
                last.then_inc(xt_ps, 1)

            def cross_operands(pb):
                pe.wait_ge(xtl_ok, pb + 1)
                if not first(pb):
                    pe.wait_ge(v_ok, pb)
                for x in range(2):
                    last = passes(bank[7][:, T * x:T * x + T], lambda d: wch[:, d, x, :], lambda d: wcl[:, d, x, :],
                                  lambda d: xth[:, d, :], lambda d: xtl[:, d, :])
                last.then_inc(cr_ps, 1)

            def out_projection(ob):
                pe.wait_ge(ao_ok, G * ob + G)
                for c in range(2):
                    for g in range(G):
                        last = mm(bank[6][0:C, D * c:D * c + D], AO[:, g, C * c:C * c + C], wo_s[:, g, :],
                                  start=(g == 0), stop=(g == G - 1))
                last.then_inc(o_ps, 1)

            def q_groups(pb, half):
                if half == 0:
                    pe.wait_ge(prod_ok, pb + 1)
                elif not few(pb):
                    pe.wait_ge(h_ok, pb - 1)
                for x in range(2):
                    g = 2 * half + x
                    last = passes(bank[7 - half][:, T * x:T * x + T], lambda d: wqh[:, d, P * g:P * g + P],
                                  lambda d: wql[:, d, P * g:P * g + P], lambda d: xth[:, d, :], lambda d: xtl[:, d, :])
                last.then_inc(q_ps, 1)

            def k_groups(pb, half):
                pe.wait_ge(ql_ok, 2 * pb + half + 1)
                if half == 0:
                    pe.wait_ge(prods_ok, pb + 1)
                for x in range(2):
                    g = 2 * half + x
                    o = bank[7 - half][:, T * x:T * x + T]
                    passes(o, lambda d: wkh[:, d, P * g:P * g + P], lambda d: wkl[:, d, P * g:P * g + P],
                           lambda d: xth[:, d, :], lambda d: xtl[:, d, :], more=True)
                    mm(o, sel_r[:, g, :], prodh[:, :], start=False, stop=False)
                    last = mm(o, sel_r[:, g, :], prodl[:, :], start=False, stop=True)
                last.then_inc(k_ps, 1)

            def v_rows(pb):
                pe.wait_ge(kl_ok, 2 * pb + 1)
                for c in range(2):
                    last = passes(bank[7][0:C, D * c:D * c + D], lambda d: xth[:, d, C * c:C * c + C],
                                  lambda d: xtl[:, d, C * c:C * c + C], lambda d: wvh[:, d, :], lambda d: wvl[:, d, :])
                last.then_inc(v_ps, 1)

            def piece(k, pb):
                if k == 0:
                    turn_x(pb)
                elif k == 1:
                    cross_operands(pb)
                elif k == 2:
                    if not few(pb):
                        out_projection(pb - 2)
                elif k in (3, 4):
                    q_groups(pb, k - 3)
                elif k in (5, 6):
                    k_groups(pb, k - 5)
                else:
                    v_rows(pb)

            def scores(b, u, p):
                if p == 0:
                    pe.wait_ge(kb_ok[u], kb_count(b, u))
                g, j = p // 2, 2 * (p % 2)
                for c in range(2):
                    if not (isinstance(b, int) and b == 0 and p == 0):
                        pe.wait_ge(sub_ok, 16 * b + 2 * p + c - 1)
                    for n, (q, kb) in enumerate(((qh, kbh), (ql, kbh), (qh, kbl))):
                        last = mm(bank[c][0:C, 0:2 * T], q[:, u, g, C * c:C * c + C], kb[:, u, g, j:j + 2, :],
                                  start=(n == 0), stop=(n == 2))
                    last.then_inc(s_ps, 1)

            def turn_probs(b, h):
                p = h // 2
                if h % 2 == 0:
                    pe.wait_ge(exp_ok, 8 * b + p + 1)
                if not (isinstance(b, int) and b == 0 and h < 2):
                    pe.wait_ge(prt_ok, 16 * b + h - 1)
                for k in range(2):
                    for c in range(2):
                        at_ = P * (2 * k + c)
                        last = nc.tensor.transpose(bank[2 + h % 2][0:C, at_:at_ + P],
                                                   pr[:, p % 4, c, h % 2, C * k:C * k + C], ident)
                last.then_inc(t_ps, 1)

            def weigh_values(b, u, h):
                g, j = h // 4, h % 4
                if h == 0:
                    pe.wait_ge(v_ok, b + 1)
                if j == 0 and not (isinstance(b, int) and b == 0 and g == 0):
                    pe.wait_ge(ao_ok, G * b + g)
                pe.wait_ge(prt_ok, 16 * b + h + 1)
                for k in range(2):
                    last = mm(bank[4][32 * j:32 * j + 32, 0:T], V[:, u, k, h, :], prt[:, h % 4, k, :],
                              start=(k == 0), stop=(k == 1))
                last.then_inc(pv_ps, 1)

            def batch(b, u, project=True):
                for s in range(11):
                    if s < 8:
                        scores(b, u, s)
                        if project:
                            piece(s, b + 1)
                        elif s == 2:
                            pe.wait_ge(kl_ok, 2 * B)
                            out_projection(b - 1)
                    if 2 <= s < 10:
                        turn_probs(b, 2 * (s - 2))
                        turn_probs(b, 2 * (s - 2) + 1)
                    if s >= 3:
                        weigh_values(b, u, 2 * (s - 3))
                        weigh_values(b, u, 2 * (s - 3) + 1)

            pe.wait_ge(parts_done, 1)
            pe.wait_ge(pads_zero, 1)
            for k in range(8):
                piece(k, 0)
            batch(0, 0)
            with pe.Fori(0, (B - 2) // 2) as i:
                batch(2 * i + 1, 1)
                batch(2 * i + 2, 0)
            batch(B - 1, 1, project=False)
            pe.wait_ge(h_ok, B - 1)
            out_projection(B - 1)

            def turn_rows(q):
                pe.wait_ge(x2_ok, 2 * q + 2)
                if q >= 2:
                    pe.wait_ge(g_ok, q - 1)
                for x in range(2):
                    for d in range(DC):
                        n = 2 * x + d
                        last = nc.tensor.transpose(bank[q % 2][:, C * n:C * n + C], X2[:, 2 * q + x, P * d:P * d + P],
                                                   ident[0:C, 0:C])
                last.then_inc(g_ps, 1)

            def gate(q):
                pe.wait_ge(g_ok, q + 1)
                for x in range(2):
                    blk = 2 * q + x
                    for d in range(DC):
                        last = mm(bank[2][0:C, E * blk:E * blk + E], x2t[:, q % 2, 2 * x + d, :],
                                  smal("wg")[:, E * d:E * d + E], start=(d == 0), stop=(d == DC - 1))
                last.then_inc(lg_ps, 1)

            for q in range(NBLK // 2 + 1):
                if q < NBLK // 2:
                    turn_rows(q)
                if q >= 1:
                    gate(q - 1)
            pe.wait_ge(hot_ok, 1)
            mm(bank[3][0:C, 0:E * NBLK], con("before", C)[:, 0:C], onehot[:, :, :], start=True, stop=False)
            mm(bank[3][0:C, 0:E * NBLK], con("full", C)[:, 0:C], earlier[:, :, :], start=False, stop=True)
            mm(bank[4][:, 0:E], con("full", C), upto[:, :, NBLK - 1], start=True, stop=True).then_inc(rank_ps, 1)
            pe.wait_ge(slots_hot, 1)
            for blk in range(NBLK):
                last = mm(bank[5][:, 0:2 * TILES], slot_hot[:, blk, :], tile_hot[:, blk, :, :],
                          start=(blk == 0), stop=(blk == NBLK - 1))
            last.then_inc(slots_ps, 1)

            def turn_tile(t):
                pe.wait_ge(gx_in, 16 * t + 16)
                for d in range(DC):
                    last = nc.tensor.transpose(bank[6][:, P * d:P * d + P], gx[:, P * d:P * d + P], ident)
                last.then_inc(tx_ps, 1)

            def first_product(t, e):
                pe.wait_ge(tx_ok, t + 1)
                for n in range(2):
                    for d in range(DC):
                        last = mm(bank[n][:, :], xt[:, d, :], W1s[:, bass.ds(e, 1), d, 512 * n:512 * n + 512],
                                  start=(d == 0), stop=(d == DC - 1))
                    last.then_inc(l1_ps, 1)

            def turn_hidden(t):
                pe.wait_ge(z_ok, 2 * t + 2)
                for k in range(HC):
                    last = nc.tensor.transpose(bank[2 + k // 4][:, P * (k % 4):P * (k % 4) + P], z[:, P * k:P * k + P], ident)
                    if k % 4 == 3:
                        last.then_inc(zt_ps, 1)

            def second_product(t, e):
                pe.wait_ge(silu_ok, HC * t + HC)
                if not first(t):
                    pe.wait_ge(y1_ok, t)
                for k in range(HC):
                    last = mm(bank[4][:, 0:D], ht[:, k, :], W2s[:, bass.ds(e, 1), k, :], start=(k == 0), stop=(k == HC - 1))
                last.then_inc(l2_ps, 1)

            def expert(t):
                return pe.value_load(et[0:1, bass.ds(t, 1)], min_val=0, max_val=E - 1)

            pe.wait_ge(et_ok, 1)
            turn_tile(0)
            pe.wait_ge(ld_w1, 16 * E)
            first_product(0, expert(0))
            turn_tile(1)
            pe.wait_ge(ld_w2, 16 * E)
            with pe.Fori(1, TILES - 1) as t:
                turn_hidden(t - 1)
                first_product(t, expert(t))
                turn_tile(t + 1)
                second_product(t - 1, expert(t - 1))
            turn_hidden(TILES - 2)
            first_product(TILES - 1, expert(TILES - 1))
            second_product(TILES - 2, expert(TILES - 2))
            turn_hidden(TILES - 1)
            second_product(TILES - 1, expert(TILES - 1))

        @block.scalar
        def _(act):
            fn = nc.scalar.activation
            act.wait_ge(aggr_done, 1)
            fn(sd[:, :], mv[:, :, 1], ACT.Sqrt).then_inc(sd_done, 1)

            def high_x(pb):
                act.wait_ge(xt_ps, pb + 1)
                fn(xth[:, :, :].rearrange("p d (c t) -> p (d c) t", c=2),
                   bank[6][:, :].rearrange("p (n t) -> p n t", t=P)[:, :, 0:C], ACT.Copy).then_inc(xth_ok, 1)

            def cross_a(pb):
                act.wait_ge(cr_ps, pb + 1)
                fn(crossa[:, :], bank[7][:, 0:T], ACT.Identity, bias=cbias[:, 0:1]).then_inc(cra_ok, 1)

            def high_q(pb, u, half):
                act.wait_ge(q_ps, 2 * pb + half + 1)
                for x in range(2):
                    g = 2 * half + x
                    last = fn(qh[:, u, g, :], bank[7 - half][:, T * x:T * x + T], ACT.Identity, bias=qbias[:, g:g + 1])
                last.then_inc(qh_ok, 1)

            def high_k(pb, u, half):
                if half == 0 and not first(pb):
                    act.wait_ge(kb_ok[1 - u], kb_count(pb - 1, 1 - u))
                act.wait_ge(k_ps, 2 * pb + half + 1)
                for x in range(2):
                    g = 2 * half + x
                    last = fn(kh[:, g, :], bank[7 - half][:, T * x:T * x + T], ACT.Identity,
                              bias=smal("bk_rows")[:, g:g + 1])
                last.then_inc(kh_ok, 1)

            def values(pb, u):
                act.wait_ge(v_ps, pb + 1)
                fn(V[0:C, u, :, :, 0:HD], bank[7][0:C, :].rearrange("p (k h f) -> p k h f", k=2, h=H),
                   ACT.Copy).then_inc(v_ok, 1)

            def piece(k, pb, u):
                if k == 0:
                    high_x(pb)
                elif k == 1:
                    cross_a(pb)
                elif k in (3, 4):
                    high_q(pb, u, k - 3)
                elif k in (5, 6):
                    high_k(pb, u, k - 5)
                elif k == 7:
                    values(pb, u)

            def copy_turned(b, h):
                act.wait_ge(t_ps, 16 * b + h + 1)
                if not (isinstance(b, int) and b == 0 and h < 4):
                    act.wait_ge(pv_ps, 16 * b + h - 3)
                fn(prt[0:C, h % 4, :, :].rearrange("p k (c t) -> p (k c) t", c=2),
                   bank[2 + h % 2][0:C, :].rearrange("p (n t) -> p n t", t=P)[:, :, 0:C], ACT.Copy).then_inc(prt_ok, 1)

            def exps(b, p):
                act.wait_ge(sub_ok, 16 * b + 2 * p + 2)
                w = pr[0:C, p % 4, :, :, :]
                fn(w, w, ACT.Exp).then_inc(exp_ok, 1)

            def batch(b, u, project=True):
                for s in range(11):
                    if s < 8 and project:
                        piece(s, b + 1, 1 - u)
                    if 2 <= s < 10:
                        copy_turned(b, 2 * (s - 2))
                        copy_turned(b, 2 * (s - 2) + 1)
                    if s < 8:
                        exps(b, s)

            act.wait_ge(parts_done, 1)
            act.wait_ge(pads_zero, 1)
            for k in range(8):
                piece(k, 0, 0)
            batch(0, 0)
            with act.Fori(0, (B - 2) // 2) as i:
                batch(2 * i + 1, 1)
                batch(2 * i + 2, 0)
            batch(B - 1, 1, project=False)

            act.wait_ge(aggr_done, 2)
            fn(sd[:, :], mv[:, :, 1], ACT.Sqrt).then_inc(sd_done, 1)
            for q in range(NBLK // 2):
                act.wait_ge(g_ps, q + 1)
                if q >= 2:
                    act.wait_ge(lg_ps, q - 1)
                fn(x2t[:, q % 2, :, :], bank[q % 2][:, 0:4 * C].rearrange("p (n t) -> p n t", t=C),
                   ACT.Copy).then_inc(g_ok, 1)
            act.wait_ge(lgsub_ok, 1)
            fn(ex[:, :, :], ex[:, :, :], ACT.Exp).then_inc(ex_ok, 1)

            def copy_tile(t):
                act.wait_ge(tx_ps, t + 1)
                if not first(t):
                    act.wait_ge(l1_ps, 2 * t)
                fn(xt[:, :, :], bank[6][:, 0:D].rearrange("p (d t) -> p d t", t=P), ACT.Copy).then_inc(tx_ok, 1)

            def silu(t):
                act.wait_ge(b1_ok, t + 1)
                for k in range(HC):
                    if k % 4 == 0:
                        act.wait_ge(zt_ps, 2 * t + k // 4 + 1)
                    fn(ht[:, k, :], bank[2 + k // 4][:, P * (k % 4):P * (k % 4) + P], ACT.Silu,
                       bias=b1c[:, k:k + 1]).then_inc(silu_ok, 1)

            copy_tile(0)
            copy_tile(1)
            with act.Fori(1, TILES - 1) as t:
                silu(t - 1)
                copy_tile(t + 1)
            silu(TILES - 2)
            silu(TILES - 1)

        @block.vector
        def _(dve):
            v = nc.vector
            dve.wait_ge(ld_pat, 64)
            v.tensor_tensor(pos_s[:, :], pos_s[:, :], tokb_s[:, :], ALU.add).then_inc(posb_done, 1)
            dve.wait_ge(posb_done, 1)
            for m in range(3):
                rows = min(EB, B - EB * m) * NIMG
                dve.wait_ge(emb_ps, m + 1)
                v.tensor_tensor(emb[0:rows, m, :], bank[m][0:rows, 0:D], pos_s[0:rows, :], ALU.add).then_inc(emb_done, 1)
            dve.wait_ge(ld_const, 16)
            dve.wait_ge(ld_small, 16)
            for i in range(2):
                last = v.tensor_scalar(bv_cols[:, i, :], con("full")[:, 0:C], smal("bv")[:, i:i + 1], None, ALU.mult)
            last.then_inc(bv_spread, 1)
            dve.wait_ge(ld_w, 16 * NW)
            temp = smal("temp")
            v.tensor_copy(wkh[:, :, :], wkp_s[:, :, :]).then_inc(parts_hi, 1)
            v.tensor_copy(wvh[:, :, :], wvt_s[:, :, :]).then_inc(parts_hi, 1)
            v.tensor_copy(sel_r[:, :, :], con("sel").rearrange("p (g n) -> p g n", g=G)).then_inc(parts_hi, 1)
            dve.wait_ge(fold_ps, 1)
            for d in range(DC):
                v.tensor_scalar(wqh[:, d, :], bank[3 + d][:, :], temp, None, ALU.mult).then_inc(parts_hi, 1)
            v.tensor_copy(wch[:, :, :, :], bank[5][:, :].rearrange("p (d x n) -> p d x n", d=DC, x=2)).then_inc(parts_hi, 1)
            v.tensor_scalar(qbias[:, :], bank[6][:, 0:G], smal("bqs_rows"), temp, ALU.add, ALU.mult)
            v.tensor_tensor(cbias[:, 0:1], bank[6][:, 4:5], smal("bks_rows"), ALU.add)
            v.tensor_tensor(cbias[:, 1:2], bank[6][:, 5:6], smal("bvs_rows"), ALU.add)
            v.tensor_tensor(obias[:, :], bank[7][0:C, 0:D], bo_s[:, :], ALU.add)
            dve.wait_ge(parts_hi, 6)
            v.tensor_tensor(wkl[:, :, :], wkp_s[:, :, :], wkh[:, :, :].bitcast(F32), ALU.subtract)
            v.tensor_tensor(wvl[:, :, :], wvt_s[:, :, :], wvh[:, :, :].bitcast(F32), ALU.subtract)
            for d in range(DC):
                v.scalar_tensor_tensor(wql[:, d, :], bank[3 + d][:, :], temp, wqh[:, d, :].bitcast(F32), ALU.mult, ALU.subtract)
            v.tensor_tensor(wcl[:, :, :, :], bank[5][:, :].rearrange("p (d x n) -> p d x n", d=DC, x=2),
                            wch[:, :, :, :].bitcast(F32), ALU.subtract).then_inc(parts_done, 1)

            def row_stats(round_):
                for blk in range(NBLK):
                    last = v.bn_stats(stats[:, blk, :], Hs[:, blk, :])
                last.then_inc(stats_done, 1)
                dve.wait_ge(stats_done, round_)
                for blk in range(NBLK):
                    last = v.bn_aggr(mv[:, blk, :], stats[:, blk, :])
                last.then_inc(aggr1, 1)
                dve.wait_ge(aggr1, round_)
                v.tensor_scalar(mv[:, :, 1], mv[:, :, 1], EPS, None, ALU.add).then_inc(aggr_done, 1)
                dve.wait_ge(sd_done, round_)
                v.reciprocal(rstd[:, :], sd[:, :]).then_inc(rstd_done, 1)
                dve.wait_ge(rstd_done, round_)

            dve.wait_ge(ld_txt, 64)
            dve.wait_ge(ld_img, 16 * B)
            row_stats(1)

            def normed(pb):
                if not first(pb):
                    dve.wait_ge(xt_ps, pb)
                for c in range(2):
                    blk = 2 * pb + c
                    last = v.tensor_scalar(xhat[0:C, c:c + 1, :], Hs[:, bass.ds(blk, 1), :], mv[:, bass.ds(blk, 1), 0],
                                           rstd[:, bass.ds(blk, 1)], ALU.subtract, ALU.mult)
                last.then_inc(xhat_ok, 1)

            def low_x(pb):
                dve.wait_ge(xth_ok, pb + 1)
                v.tensor_tensor(xtl[:, :, :].rearrange("p d (c t) -> p (d c) t", c=2),
                                bank[6][:, :].rearrange("p (n t) -> p n t", t=P)[:, :, 0:C],
                                xth[:, :, :].bitcast(F32).rearrange("p d (c t) -> p (d c) t", c=2),
                                ALU.subtract).then_inc(xtl_ok, 1)

            def cross_products(pb):
                dve.wait_ge(cra_ok, pb + 1)
                v.scalar_tensor_tensor(prod[:, :], bank[7][:, T:2 * T], cbias[:, 1:2], crossa[:, :],
                                       ALU.add, ALU.mult).then_inc(prod_ok, 1)

            def low_q(pb, u, half):
                dve.wait_ge(qh_ok, 2 * pb + half + 1)
                for x in range(2):
                    g = 2 * half + x
                    last = v.scalar_tensor_tensor(ql[:, u, g, :], bank[7 - half][:, T * x:T * x + T], qbias[:, g:g + 1],
                                                  qh[:, u, g, :].bitcast(F32), ALU.add, ALU.subtract)
                last.then_inc(ql_ok, 1)

            def low_k(pb, u, half):
                if half == 0 and not first(pb):
                    dve.wait_ge(kb_ok[1 - u], kb_count(pb - 1, 1 - u))
                dve.wait_ge(kh_ok, 2 * pb + half + 1)
                for x in range(2):
                    g = 2 * half + x
                    last = v.scalar_tensor_tensor(kl[:, g, :], bank[7 - half][:, T * x:T * x + T],
                                                  smal("bk_rows")[:, g:g + 1], kh[:, g, :].bitcast(F32),
                                                  ALU.add, ALU.subtract)
                last.then_inc(kl_ok, 1)

            def add_out(ob):
                dve.wait_ge(hb_ok, ob + 1)
                dve.wait_ge(o_ps, ob + 1)
                rows = Hs[:, bass.ds(2 * ob, 2), :]
                v.tensor_tensor(rows, bank[6][0:C, :].rearrange("p (c d) -> p c d", c=2), rows, ALU.add).then_inc(h_ok, 1)

            def piece(k, pb, u):
                if k == 0:
                    low_x(pb)
                elif k == 1:
                    cross_products(pb)
                elif k == 2:
                    if not few(pb):
                        add_out(pb - 2)
                elif k in (3, 4):
                    low_q(pb, u, k - 3)
                elif k in (5, 6):
                    low_k(pb, u, k - 5)

            def shift(b, p):
                for c in range(2):
                    n = 2 * p + c
                    sc = bank[c][0:C, 0:2 * T].rearrange("p (h t) -> p h t", h=2)
                    dve.wait_ge(s_ps, 16 * b + n + 1)
                    v.tensor_reduce(mx[:, p, c, :], sc, AX.X, ALU.max).then_inc(mx_ok, 1)
                    if c == 0 and not (isinstance(b, int) and b == 0 and p < 4):
                        dve.wait_ge(t_ps, 16 * b + 2 * p - 6)
                    dve.wait_ge(mx_ok, 16 * b + n + 1)
                    v.tensor_tensor(pr[0:C, p % 4, c, :, :], sc, mx[:, p, c, :].unsqueeze(2).to_broadcast([C, 2, T]),
                                    ALU.subtract).then_inc(sub_ok, 1)

            def normalise(b, g):
                dve.wait_ge(parts_done, 1)
                dve.wait_ge(pv_ps, 16 * b + 4 * g + 4)
                v.stream_shuffle(den[:, :], bank[4][:, 0:T], [16 + (i % 16) for i in range(32)]).then_inc(den_ok, 1)
                dve.wait_ge(den_ok, G * b + g + 1)
                v.reciprocal(rden[:, :], den[:, :]).then_inc(rden_ok, 1)
                if g == 0 and not first(b):
                    dve.wait_ge(o_ps, b)
                dve.wait_ge(rden_ok, G * b + g + 1)
                v.tensor_tensor(AO[:, g, :], bank[4][:, 0:T], rden[:, :], ALU.mult).then_inc(ao_ok, 1)

            def batch(b, u, project=True, norm_next=True):
                for s in range(11):
                    if s < 8 and project:
                        piece(s, b + 1, 1 - u)
                    if s == 2 and not project:
                        add_out(b - 1)
                    if s < 8:
                        shift(b, s)
                    if s == 6 and project and norm_next:
                        normed(b + 2)
                    if s >= 4 and s % 2 == 0:
                        normalise(b, (s - 4) // 2)

            dve.wait_ge(pads_zero, 1)
            normed(0)
            for k in range(8):
                piece(k, 0, 0)
                if k == 0:
                    normed(1)
            batch(0, 0)
            with dve.Fori(0, (B - 2) // 2 - 1) as i:
                batch(2 * i + 1, 1)
                batch(2 * i + 2, 0)
            batch(B - 3, 1)
            batch(B - 2, 0, norm_next=False)
            batch(B - 1, 1, project=False)
            add_out(B - 1)

            count = [0]

            def link(ins):
                count[0] += 1
                ins.then_inc(dve_step, 1)
                dve.wait_ge(dve_step, count[0])

            dve.wait_ge(h_ok, B)
            row_stats(2)
            for blk in range(NBLK):
                v.tensor_scalar(X2[:, blk, :], Hs[:, blk, :], mv[:, blk, 0:1], rstd[:, blk:blk + 1],
                                ALU.subtract, ALU.mult).then_inc(x2_ok, 1)
            dve.wait_ge(ld_b2, 32)
            dve.wait_ge(lg_ps, NBLK // 2)
            link(v.tensor_tensor(lg[:, :, :], bank[2][0:C, 0:E * NBLK].rearrange("p (b e) -> p b e", e=E),
                                 bg_s[:, :].unsqueeze(1).to_broadcast([C, NBLK, E]), ALU.add))
            link(v.tensor_reduce(lgmax[:, :], lg[:, :, :], AX.X, ALU.max))
            wide = lgmax[:, :].unsqueeze(2).to_broadcast([C, NBLK, E])
            v.tensor_tensor(ex[:, :, :], lg[:, :, :], wide, ALU.subtract).then_inc(lgsub_ok, 1)
            link(v.tensor_tensor(hit[:, :, :], lg[:, :, :], wide, ALU.is_equal))
            link(v.tensor_tensor(hit[:, :, :], hit[:, :, :], con("backward", C).unsqueeze(1).to_broadcast([C, NBLK, E]), ALU.mult))
            link(v.tensor_reduce(firsthit[:, :], hit[:, :, :], AX.X, ALU.max))
            link(v.tensor_tensor(onehot[:, :, :].rearrange("p e b -> p b e"), hit[:, :, :],
                                 firsthit[:, :].unsqueeze(2).to_broadcast([C, NBLK, E]), ALU.is_equal))
            link(v.tensor_tensor_scan(upto[:, :, :].rearrange("p e b -> p (e b)"), con("restart", C),
                                      onehot[:, :, :].rearrange("p e b -> p (e b)"), 0.0, ALU.mult, ALU.add))
            v.tensor_tensor(earlier[:, :, :], upto[:, :, :], onehot[:, :, :], ALU.subtract).then_inc(hot_ok, 1)
            dve.wait_ge(ex_ok, 1)
            link(v.tensor_reduce(exsum[:, :], ex[:, :, :], AX.X, ALU.add))
            v.reciprocal(wtop[:, :], exsum[:, :])
            dve.wait_ge(rank_ps, 1)
            link(v.tensor_tensor(ntiles_cmp[:, :, :], bank[4][:, 0:E].unsqueeze(2).to_broadcast([P, E, 11]),
                                 con("tile_start")[:, 0:11].unsqueeze(1).to_broadcast([P, E, 11]), ALU.is_gt))
            link(v.tensor_reduce(ntiles[:, :], ntiles_cmp[:, :, :], AX.X, ALU.add))
            link(v.tensor_tensor_scan(tiles_upto[:, :], con("full")[:, 0:E], ntiles[:, :], 0.0, ALU.mult, ALU.add))
            link(v.tensor_tensor(base[:, :], tiles_upto[:, :], ntiles[:, :], ALU.subtract))
            link(v.tensor_scalar(base[:, :], base[:, :], float(SLOTS), None, ALU.mult))
            link(v.tensor_tensor(posn[:, :, :], bank[3][0:C, 0:E * NBLK].rearrange("p (e b) -> p e b", e=E),
                                 base[0:C, :].unsqueeze(2).to_broadcast([C, E, NBLK]), ALU.add))
            link(v.tensor_tensor(posn[:, :, :], posn[:, :, :], onehot[:, :, :], ALU.mult))
            link(v.tensor_reduce(pos[:, :], posn[:, :, :].rearrange("p e b -> p b e"), AX.X, ALU.add))
            link(v.tensor_tensor(tile_cmp[:, :, :], pos[:, :].unsqueeze(2).to_broadcast([C, NBLK, TILES - 1]),
                                 con("tile_start", C)[:, 1:TILES].unsqueeze(1).to_broadcast([C, NBLK, TILES - 1]), ALU.is_ge))
            link(v.tensor_reduce(tile_of[:, :], tile_cmp[:, :, :], AX.X, ALU.add))
            link(v.tensor_scalar(slot_of[:, :], tile_of[:, :], -float(SLOTS), None, ALU.mult))
            link(v.tensor_tensor(slot_of[:, :], slot_of[:, :], pos[:, :], ALU.add))
            v.tensor_tensor(slot_hot[:, :, :], con("iota", C).unsqueeze(1).to_broadcast([C, NBLK, SLOTS]),
                            slot_of[:, :].unsqueeze(2).to_broadcast([C, NBLK, SLOTS]), ALU.is_equal)
            link(v.tensor_tensor(tile_hot[:, :, 0, :], con("iota", C)[:, 0:TILES].unsqueeze(1).to_broadcast([C, NBLK, TILES]),
                                 tile_of[:, :].unsqueeze(2).to_broadcast([C, NBLK, TILES]), ALU.is_equal))
            link(v.tensor_tensor(tile_hot[:, :, 1, :], tile_hot[:, :, 0, :],
                                 wtop[:, :].unsqueeze(2).to_broadcast([C, NBLK, TILES]), ALU.mult))
            v.tensor_tensor(tile_hot[:, :, 0, :], tile_hot[:, :, 0, :],
                            con("tokid", C).unsqueeze(2).to_broadcast([C, NBLK, TILES]), ALU.mult).then_inc(slots_hot, 1)
            link(v.tensor_tensor(et_cmp[:, :, :], tiles_upto[0:1, :].unsqueeze(1).to_broadcast([1, TILES, E]),
                                 con("iota", 1)[:, 0:TILES].unsqueeze(2).to_broadcast([1, TILES, E]), ALU.is_le))
            link(v.tensor_reduce(et_f[:, :], et_cmp[:, :, :], AX.X, ALU.add))
            v.tensor_scalar(et[:, :], et_f[:, :], float(E - 1), None, ALU.min).then_inc(et_ok, 1)
            dve.wait_ge(slots_ps, 1)
            v.tensor_copy(wslot[:, :], bank[5][:, TILES:2 * TILES])
            v.tensor_scalar(ids[:, :], bank[5][:, 0:TILES], float(NTOK), None, ALU.add).then_inc(ids_ok, 1)

            def expert(t):
                return dve.value_load(et[0:1, bass.ds(t, 1)], min_val=0, max_val=E - 1)

            def tile_bias(t, e):
                if not first(t):
                    dve.wait_ge(silu_ok, HC * t)
                v.tensor_copy(b1c[:, :].unsqueeze(1), smal("b1").rearrange("p (e k) -> p e k", e=E)[:, bass.ds(e, 1), :]).then_inc(b1_ok, 1)

            def copy_hidden(t):
                if not first(t):
                    dve.wait_ge(zt_ps, 2 * t)
                for n in range(2):
                    dve.wait_ge(l1_ps, 2 * t + n + 1)
                    v.tensor_copy(z[:, 512 * n:512 * n + 512], bank[n][:, :]).then_inc(z_ok, 1)

            def finish(t, e):
                dve.wait_ge(l2_ps, t + 1)
                if not first(t):
                    dve.wait_ge(y_ok, t)
                v.tensor_tensor(y1[:, :].unsqueeze(1), bank[4][:, 0:D].unsqueeze(1), b2_s[:, bass.ds(e, 1), :], ALU.add).then_inc(y1_ok, 1)
                dve.wait_ge(gh_in, 16 * t + 16)
                if not first(t):
                    dve.wait_ge(sc_out, 16 * t)
                dve.wait_ge(y1_ok, t + 1)
                v.scalar_tensor_tensor(Y[:, :], y1[:, :], wslot[:, bass.ds(t, 1)], gh[:, :], ALU.mult, ALU.add).then_inc(y_ok, 1)

            dve.wait_ge(et_ok, 1)
            dve.wait_ge(ids_ok, 1)
            copy_hidden(0)
            tile_bias(0, expert(0))
            with dve.Fori(1, TILES) as t:
                copy_hidden(t)
                tile_bias(t, expert(t))
                finish(t - 1, expert(t - 1))
            finish(TILES - 1, expert(TILES - 1))

        @block.gpsimd
        def _(pool):
            g = nc.gpsimd
            g.memset(kbh[:, :, :, :, :].bitcast(F32), 0.0)
            g.memset(kbl[:, :, :, :, :].bitcast(F32), 0.0)
            g.memset(xhat[:, :, :], 0.0)
            g.memset(pr[:, :, :, :, :], 0.0)
            g.memset(prt[:, :, :, :], 0.0)
            g.memset(V[:, :, :, :, :], 0.0).then_inc(v_zero, 1)
            pool.wait_ge(v_zero, 1)
            g.memset(V[0:C, :, :, :, HD:32], 1.0).then_inc(pads_zero, 1)

            def parts_of_products(pb):
                pool.wait_ge(prod_ok, pb + 1)
                g.tensor_tensor(prodh[:, :], prod[:, :], con("full")[:, 0:1].to_broadcast([P, T]), ALU.mult).then_inc(prodh_ok, 1)
                pool.wait_ge(prodh_ok, pb + 1)
                g.tensor_tensor(prodl[:, :], prod[:, :], prodh[:, :].bitcast(F32), ALU.subtract).then_inc(prods_ok, 1)

            def add_out_bias(b):
                rows = Hs[:, bass.ds(2 * b, 2), :]
                g.tensor_tensor(rows, rows, obias[:, :].unsqueeze(1).to_broadcast([C, 2, D]), ALU.add).then_inc(hb_ok, 1)

            pool.wait_ge(parts_done, 1)
            parts_of_products(0)
            pool.wait_ge(xhat_ok, 1)
            add_out_bias(0)
            with pool.Fori(1, B) as b:
                parts_of_products(b)
                pool.wait_ge(xhat_ok, b + 1)
                add_out_bias(b)

            pool.wait_ge(ids_ok, 1)
            pool.wait_ge(rows_out, 16 * 6)

            def gather_normed(t):
                g.indirect_dma_start(out=gx[:, :], out_offset=None, in_=x2_dram,
                                     in_offset=bass.IndirectOffsetOnAxis(ap=ids[:, t:t + 1], axis=0)).then_inc(gx_in, 16)

            def gather_residual(t):
                g.indirect_dma_start(out=gh[:, :], out_offset=None, in_=h2_dram,
                                     in_offset=bass.IndirectOffsetOnAxis(ap=ids[:, t:t + 1], axis=0)).then_inc(gh_in, 16)

            def scatter(t):
                pool.wait_ge(y_ok, t + 1)
                g.indirect_dma_start(out=out_rows, out_offset=bass.IndirectOffsetOnAxis(ap=ids[:, t:t + 1], axis=0),
                                     in_=Y[:, :], in_offset=None, bounds_check=NTOK - 1, oob_is_err=False).then_inc(sc_out, 16)

            gather_normed(0)
            pool.wait_ge(tx_ps, 1)
            gather_normed(1)
            for t in range(TILES):
                if t >= 1:
                    pool.wait_ge(y_ok, t)
                gather_residual(t)
                if t + 2 < TILES:
                    pool.wait_ge(tx_ps, t + 2)
                    gather_normed(t + 2)
                scatter(t)
            pool.wait_ge(sc_out, 16 * TILES)


def kernel(x, txt, L0_tok_W, L0_tok_b, L0_tok_pos_embd, L0_attn_Wq, L0_attn_bq, L0_attn_Wk, L0_attn_bk, L0_attn_Wv,
           L0_attn_bv, L0_attn_Wo, L0_attn_bo, L0_attn_Wqs, L0_attn_bqs, L0_attn_Wks, L0_attn_bks, L0_attn_Wvs,
           L0_attn_bvs, L0_attn_temp, L0_ffn_Wg, L0_ffn_bg, L0_ffn_W1, L0_ffn_b1, L0_ffn_W2, L0_ffn_b2):
    import concourse.bacc as bacc
    from concourse.bass_utils import run_bass_kernel_spmd

    f = np.float32
    wq, wk, wv, wo = (np.asarray(w) for w in (L0_attn_Wq, L0_attn_Wk, L0_attn_Wv, L0_attn_Wo))
    n = IMG // PATCH
    patches = np.asarray(x).reshape(B, CH, n, PATCH, n, PATCH).transpose(1, 3, 5, 0, 2, 4).reshape(PD, B * NIMG)
    wk_pad = np.zeros((D, H, 32), f)
    wk_pad[:, :, :HD] = wk.T.reshape(D, H, HD)
    wo_pad = np.zeros((H, 32, D), f)
    wo_pad[:, :HD] = wo.T.reshape(H, HD, D)
    mq = np.zeros((8, HD, 8, 32), f)
    ma = np.zeros((2, 8, HD, P), f)
    mb = np.zeros((2, 8, HD, P), f)
    wqs, wks, wvs = (np.asarray(w) for w in (L0_attn_Wqs, L0_attn_Wks, L0_attn_Wvs))
    bqs, bks, bvs = (np.asarray(w) for w in (L0_attn_bqs, L0_attn_bks, L0_attn_bvs))
    bqs_rows, bks_rows, bvs_rows = np.zeros((4, 32), f), np.zeros(P, f), np.zeros(P, f)
    bqs_rows[:, HD:HD + 3] = bqs
    for h in range(8):
        mq[h, :, h, :HD] = np.eye(HD, dtype=f)
        mq[h, :, h, HD:HD + 3] = wqs.T
    for h in range(H):
        for c in range(3):
            c1, c2 = (c + 1) % 3, (c + 2) % 3
            lo, hi = 3 * h + c, 64 + 3 * h + c
            ma[h // 8, h % 8, :, lo], ma[h // 8, h % 8, :, hi] = wks[c1], wks[c2]
            mb[h // 8, h % 8, :, lo], mb[h // 8, h % 8, :, hi] = wvs[c2], wvs[c1]
            bks_rows[lo], bks_rows[hi] = bks[c1], bks[c2]
            bvs_rows[lo], bvs_rows[hi] = bvs[c2], bvs[c1]
    bk_rows = np.zeros((G, 4, 32), f)
    bk_rows[:, :, :HD] = np.asarray(L0_attn_bk).reshape(G, 4, HD)
    small = np.zeros((P, SMALL_W), f)
    for name, value in (
        ("bq", np.asarray(L0_attn_bq).reshape(2, P).T), ("bk", np.asarray(L0_attn_bk).reshape(2, P).T),
        ("bv", np.asarray(L0_attn_bv).reshape(2, P).T), ("bk_rows", bk_rows.reshape(G, P).T),
        ("bqs_rows", bqs_rows.reshape(P, 1)), ("bks_rows", bks_rows.reshape(P, 1)), ("bvs_rows", bvs_rows.reshape(P, 1)),
        ("temp", np.broadcast_to(np.asarray(L0_attn_temp), (P, 1))),
        ("b1", np.asarray(L0_ffn_b1).reshape(E, HC, P).transpose(2, 0, 1).reshape(P, E * HC)),
        ("wg", np.asarray(L0_ffn_Wg).reshape(DC, P, E).transpose(1, 0, 2).reshape(P, DC * E)),
    ):
        a, b = SMALL[name]
        small[:, a:b] = value
    arrays = {
        "patches": patches, "tok_wt": np.asarray(L0_tok_W).T, "tok_b": np.asarray(L0_tok_b),
        "pos3": np.concatenate([np.asarray(L0_tok_pos_embd)[0]] * EB), "txt": np.asarray(txt),
        "const": host_constants(), "small": small, "wq": wq, "wk": wk, "wv": wv,
        "wk_pad": wk_pad.reshape(D, 512), "wv_t": wv.T, "wo_t": wo.T, "wo_pad": wo_pad.reshape(512, D),
        "mq": mq.reshape(P, D), "ma": ma.reshape(2, P, P).transpose(1, 0, 2), "mb": mb.reshape(2, P, P).transpose(1, 0, 2),
        "bo": np.asarray(L0_attn_bo), "bg": np.asarray(L0_ffn_bg), "w1": np.asarray(L0_ffn_W1),
        "w2": np.asarray(L0_ffn_W2), "b2": np.asarray(L0_ffn_b2),
    }
    arrays = {k: np.ascontiguousarray(a) for k, a in arrays.items()}
    nc = bacc.Bacc("TRN2", target_bir_lowering=False, num_devices=1)
    args = {k: nc.dram_tensor(f"in_{k}", a.shape, mybir.dt.from_np(a.dtype), kind="ExternalInput").ap()
            for k, a in arrays.items()}
    out = nc.dram_tensor("out_0", (B, T, D), F32, kind="ExternalOutput").ap()
    program(nc, out=out, **args)
    r = run_bass_kernel_spmd(nc, [{f"in_{k}": a for k, a in arrays.items()}], core_ids=[0])
    return r.results[0]["out_0"]
```

```python
from contextlib import ExitStack

import numpy as np

import concourse.bass as bass
from concourse import mybir

F32 = mybir.dt.float32
F32R = mybir.dt.float32r
I32 = mybir.dt.int32
ACT = mybir.ActivationFunctionType
ALU = mybir.AluOpType
AX = mybir.AxisListType

B, NIMG, NTXT, D, H, HD = 8, 36, 128, 256, 16, 16
PATCH, CH, IMG = 16, 3, 96
PD = CH * PATCH * PATCH
T = NIMG + NTXT
C = T // 2
NBLK = 2 * B
NTOK = B * T
E, HID = 8, 1024
P = 128
SLOTS = 128
TILES = (NTOK - E) // SLOTS + E
G = 4
DC = D // P
KC = PD // P
HC = HID // P
EB = 3
EPS = 1e-5

CONST = {}
SMALL = {}


def _columns(table, *items):
    at = 0
    for name, width in items:
        table[name] = (at, at + width)
        at += width
    return at


CONST_W = _columns(CONST, ("ident", P), ("before", P), ("iota", P), ("restart", P),
                   ("tile_start", 32), ("full", P), ("tokid", NBLK), ("backward", E))
SMALL_W = _columns(SMALL, ("bq", 2), ("bk", 2), ("bv", 2), ("bk_rows", G), ("bqs_rows", 1),
                   ("bks_rows", 1), ("bvs_rows", 1), ("temp", 1), ("b1", E * HC), ("wg", DC * E))


def host_constants():
    c = np.zeros((P, CONST_W), np.float32)

    def put(name, value):
        a, b = CONST[name]
        c[:value.shape[0], a:b] = value.reshape(value.shape[0], b - a)

    put("ident", np.eye(P, dtype=np.float32))
    put("before", np.triu(np.ones((P, P), np.float32), 1))
    put("iota", np.tile(np.arange(P, dtype=np.float32), (P, 1)))
    restart = np.ones((P, E, NBLK), np.float32)
    restart[:, :, 0] = 0.0
    put("restart", restart)
    put("tile_start", np.tile(SLOTS * np.arange(32, dtype=np.float32), (P, 1)))
    put("full", np.ones((P, P), np.float32))
    tok = C * np.arange(NBLK, dtype=np.float32)[None, :] + np.arange(P, dtype=np.float32)[:, None] - NTOK
    put("tokid", tok)
    put("backward", np.tile(E - np.arange(E, dtype=np.float32), (P, 1)))
    return c


def host_selection():
    sel = np.zeros((P, G, P), np.float32)
    for h in range(H):
        for k in range(3):
            row = 32 * (h % 4) + HD + k
            sel[3 * h + k, h // 4, row] = 1.0
            sel[64 + 3 * h + k, h // 4, row] = -1.0
    return sel


def program(nc, patches, tok_wt, tok_b, pos3, txt, const, small, sel, wq, wk, wv, wk_pad, wv_t, wo_t, wo_pad, mq, ma, mb,
            bo, bg, w1, w2, b2, out):
    x2_dram = nc.dram_tensor("normed_rows", [NTOK + 1, D], F32).ap()
    h2_dram = nc.dram_tensor("residual_rows", [NTOK + 1, D], F32).ap()
    out_rows = out.rearrange("b t d -> (b t) d")

    with ExitStack() as ctx:
        def sb(name, shape, dt=F32, scope=ctx):
            return scope.enter_context(nc.sbuf_tensor(name, shape, dt))

        def sem(name):
            return ctx.enter_context(nc.semaphore(name))

        pair01 = ctx.enter_context(nc.psum_tensor("bank01", [P, 2, 512], F32))
        pair23 = ctx.enter_context(nc.psum_tensor("bank23", [P, 2, 512], F32))
        bank = [pair01[:, 0, :], pair01[:, 1, :], pair23[:, 0, :], pair23[:, 1, :]]
        bank += [ctx.enter_context(nc.psum_tensor(f"bank{i}", [P, 512], F32)) for i in range(4, 8)]

        Hs = sb("Hs", [C, NBLK, D])
        cst = sb("cst", [P, CONST_W])
        sml = sb("sml", [P, SMALL_W])
        stats = sb("stats", [C, NBLK, 6])
        mv = sb("mv", [C, NBLK, 2])
        sd = sb("sd", [C, NBLK])
        rstd = sb("rstd", [C, NBLK])

        with ExitStack() as st:
            pat_s = sb("pat_s", [P, KC, B * NIMG], F32, st)
            tokw_s = sb("tokw_s", [P, KC, D], F32, st)
            pos_s = sb("pos_s", [EB * NIMG, D], F32, st)
            tokb_s = sb("tokb_s", [EB * NIMG, D], F32, st)
            emb = sb("emb", [EB * NIMG, 3, D], F32, st)
            wq_s = sb("wq_s", [P, 2, D], F32, st)
            wk_s = sb("wk_s", [P, 2, D], F32, st)
            wv_s = sb("wv_s", [P, 2, D], F32, st)
            wkp_s = sb("wkp_s", [P, DC, 512], F32, st)
            wvt_s = sb("wvt_s", [P, DC, D], F32, st)
            wot_s = sb("wot_s", [P, 2, D], F32, st)
            bv_cols = sb("bv_cols", [P, 2, C], F32, st)
            mq_s = sb("mq_s", [P, D], F32, st)
            ma_s = sb("ma_s", [P, 2, P], F32, st)
            mb_s = sb("mb_s", [P, 2, P], F32, st)
            bo_s = sb("bo_s", [C, D], F32, st)
            sel_s = sb("sel_s", [P, G, P], F32, st)
        W1s = sb("W1s", [P, E, DC, HID])

        with ExitStack() as at:
            wqh, wql = (sb(n, [P, DC, 512], F32R, at) for n in ("wqh", "wql"))
            wkh, wkl = (sb(n, [P, DC, 512], F32R, at) for n in ("wkh", "wkl"))
            wch, wcl = (sb(n, [P, DC, 2, P], F32R, at) for n in ("wch", "wcl"))
            wvh, wvl = (sb(n, [P, DC, D], F32R, at) for n in ("wvh", "wvl"))
            wo_s = sb("wo_s", [P, G, D], F32, at)
            sel_r = sb("sel_r", [P, G, P], F32R, at)
            qbias = sb("qbias", [P, G], F32, at)
            cbias = sb("cbias", [P, 2], F32, at)
            obias = sb("obias", [C, D], F32, at)
            xhat = sb("xhat", [P, 2, D], F32, at)
            xth, xtl = (sb(n, [P, DC, T], F32R, at) for n in ("xth", "xtl"))
            crossa = sb("crossa", [P, T], F32, at)
            prod = sb("prod", [P, T], F32, at)
            prodh, prodl = (sb(n, [P, T], F32R, at) for n in ("prodh", "prodl"))
            qh, ql = (sb(n, [P, 2, G, T], F32R, at) for n in ("qh", "ql"))
            kh, kl = (sb(n, [P, G, T], F32R, at) for n in ("kh", "kl"))
            kbh, kbl = (sb(n, [P, 2, G, 4, T], F32R, at) for n in ("kbh", "kbl"))
            V = sb("V", [P, 2, 2, H, 32], F32, at)
            mx = sb("mx", [C, 8, 2, 2], F32, at)
            pr = sb("pr", [P, 4, 2, 2, T], F32, at)
            prt = sb("prt", [P, 4, 2, T], F32, at)
            den = sb("den", [P, T], F32, at)
            AO = sb("AO", [P, 2, G, T], F32, at)

        W2s = sb("W2s", [P, E, HC, D])
        X2 = sb("X2", [C, NBLK, D])
        x2t = sb("x2t", [P, 2, 4, C])
        bg_s = sb("bg_s", [C, E])
        b2_s = sb("b2_s", [P, E, D])
        lg = sb("lg", [C, NBLK, E])
        lgmax = sb("lgmax", [C, NBLK])
        ex = sb("ex", [C, NBLK, E])
        exsum = sb("exsum", [C, NBLK])
        wtop = sb("wtop", [C, NBLK])
        hit = sb("hit", [C, NBLK, E])
        firsthit = sb("firsthit", [C, NBLK])
        onehot = sb("onehot", [C, E, NBLK])
        upto = sb("upto", [C, E, NBLK])
        earlier = sb("earlier", [C, E, NBLK])
        ntiles_cmp = sb("ntiles_cmp", [P, E, 11])
        ntiles = sb("ntiles", [P, E])
        tiles_upto = sb("tiles_upto", [P, E])
        base = sb("base", [P, E])
        posn = sb("posn", [C, E, NBLK])
        pos = sb("pos", [C, NBLK])
        tile_cmp = sb("tile_cmp", [C, NBLK, 17])
        tile_of = sb("tile_of", [C, NBLK])
        slot_of = sb("slot_of", [C, NBLK])
        slot_hot = sb("slot_hot", [C, NBLK, SLOTS])
        tile_hot = sb("tile_hot", [C, NBLK, 2, TILES])
        ids = sb("ids", [P, TILES], I32)
        wslot = sb("wslot", [P, TILES])
        et_cmp = sb("et_cmp", [1, TILES, E])
        et_f = sb("et_f", [1, TILES])
        et = sb("et", [1, TILES], I32)
        gx = sb("gx", [P, D])
        gh = sb("gh", [P, D])
        xt = sb("xt", [P, DC, P])
        z = sb("z", [P, HID])
        b1c = sb("b1c", [P, HC])
        ht = sb("ht", [P, HC, P])
        y1 = sb("y1", [P, D])
        Y = sb("Y", [P, D])

        def con(name, rows=P):
            a, b = CONST[name]
            return cst[0:rows, a:b]

        def smal(name):
            a, b = SMALL[name]
            return sml[:, a:b]

        ident = con("ident")

        ld_pat, ld_const, ld_txt, ld_small, ld_w, ld_img = (sem(n) for n in (
            "ld_pat", "ld_const", "ld_txt", "ld_small", "ld_w", "ld_img"))
        ld_w1, ld_w2, ld_b2, rows_out = (sem(n) for n in ("ld_w1", "ld_w2", "ld_b2", "rows_out"))
        pads_zero = sem("pads_zero")
        emb_ps, emb_done, posb_done = sem("emb_ps"), sem("emb_done"), sem("posb_done")
        fold_ps = sem("fold_ps")
        stats_done, aggr_done, sd_done, rstd_done = (sem(n) for n in ("stats_done", "aggr_done", "sd_done", "rstd_done"))
        parts_hi, parts_done = sem("parts_hi"), sem("parts_done")
        xhat_ok = sem("xhat_ok")
        xt_ps, xth_ok, xtl_ok = sem("xt_ps"), sem("xth_ok"), sem("xtl_ok")
        cr_ps, cra_ok, prod_ok, prodh_ok, prods_ok = (sem(n) for n in ("cr_ps", "cra_ok", "prod_ok", "prodh_ok", "prods_ok"))
        q_ps, qh_ok, ql_ok = sem("q_ps"), sem("qh_ok"), sem("ql_ok")
        k_ps, kh_ok, kl_ok = sem("k_ps"), sem("kh_ok"), sem("kl_ok")
        v_ps, v_ok = sem("v_ps"), sem("v_ok")
        kb_ok = [sem("kb_ok0"), sem("kb_ok1")]
        s_ps, mx_ok, sub_ok, exp_ok = sem("s_ps"), sem("mx_ok"), sem("sub_ok"), sem("exp_ok")
        t_ps, prt_ok, pv_ps = sem("t_ps"), sem("prt_ok"), sem("pv_ps")
        den_ok, rden_ok, ao_ok = sem("den_ok"), sem("rden_ok"), sem("ao_ok")
        o_ps, hb_ok, h_ok = sem("o_ps"), sem("hb_ok"), sem("h_ok")
        dve_step, aggr1, v_zero, bv_spread = sem("dve_step"), sem("aggr1"), sem("v_zero"), sem("bv_spread")
        hot_ok, rank_ps, slots_hot, slots_ps, lgsub_ok, ex_ok = (sem(n) for n in (
            "hot_ok", "rank_ps", "slots_hot", "slots_ps", "lgsub_ok", "ex_ok"))
        x2_ok, g_ps, g_ok, lg_ps = sem("x2_ok"), sem("g_ps"), sem("g_ok"), sem("lg_ps")
        ids_ok, et_ok = sem("ids_ok"), sem("et_ok")
        gx_in, gh_in, sc_out = sem("gx_in"), sem("gh_in"), sem("sc_out")
        tx_ps, tx_ok, l1_ps, z_ok, zt_ps, silu_ok, b1_ok, l2_ps, y1_ok, y_ok = (sem(n) for n in (
            "tx_ps", "tx_ok", "l1_ps", "z_ok", "zt_ps", "silu_ok", "b1_ok", "l2_ps", "y1_ok", "y_ok"))

        NW = 12
        PARTS = [(0, 80), (80, C)]

        def first(b):
            return isinstance(b, int) and b == 0

        def few(b):
            return isinstance(b, int) and b < 2

        def piece_bank(pb, piece_):
            alone = {"x": 0, "cross": 1, "q0": 2, "q1": 3, "k0": 4, "k1": 5, "v": 7}
            shared = {"x": 6, "cross": 7, "q0": 6, "k0": 7, "k1": 6, "q1": 6, "v": 7}
            return bank[(alone if first(pb) else shared)[piece_]]

        def kb_count(b, u):
            return 64 * (b - u) + 128

        block = ctx.enter_context(nc.Block())

        @block.sync
        def _(sp):
            sp.dma_start(pat_s[:, :, :], patches.rearrange("(k p) n -> p k n", p=P)).then_inc(ld_pat, 16)
            sp.dma_start(tokw_s[:, :, :], tok_wt.rearrange("(k p) e -> p k e", p=P)).then_inc(ld_pat, 16)
            sp.dma_start(pos_s[:, :], pos3).then_inc(ld_pat, 16)
            sp.dma_start(tokb_s[:, :], tok_b.partition_broadcast(EB * NIMG)).then_inc(ld_pat, 16)
            for a, b in ((NIMG, 68), (68, C)):
                sp.dma_start(Hs[a:b, 0:NBLK:2, :],
                             txt[:, a - NIMG:b - NIMG, :].rearrange("b p d -> p b d")).then_inc(ld_txt, 16)
            for a, b in PARTS:
                sp.dma_start(Hs[a:b, 1:NBLK:2, :],
                             txt[:, C - NIMG + a:C - NIMG + b, :].rearrange("b p d -> p b d")).then_inc(ld_txt, 16)
            sp.dma_start(cst[:, :], const).then_inc(ld_const, 16)
            sp.dma_start(sml[:, :], small).then_inc(ld_small, 16)
            for dst, src in ((wq_s, wq), (wk_s, wk), (wv_s, wv)):
                sp.dma_start(dst[:, :, :], src.rearrange("(k p) e -> p k e", p=P)).then_inc(ld_w, 16)
            for dst, src in ((wkp_s, wk_pad), (wvt_s, wv_t), (wot_s, wo_t)):
                sp.dma_start(dst[:, :, :], src.rearrange("(k p) e -> p k e", p=P)).then_inc(ld_w, 16)
            sp.dma_start(wo_s[:, :, :], wo_pad.rearrange("(k p) e -> p k e", p=P)).then_inc(ld_w, 16)
            sp.dma_start(mq_s[:, :], mq).then_inc(ld_w, 16)
            sp.dma_start(ma_s[:, :, :], ma).then_inc(ld_w, 16)
            sp.dma_start(mb_s[:, :, :], mb).then_inc(ld_w, 16)
            sp.dma_start(bo_s[:, :], bo.partition_broadcast(C)).then_inc(ld_w, 16)
            sp.dma_start(sel_s[:, :, :], sel).then_inc(ld_w, 16)
            for b in range(B):
                m, k = b // EB, b % EB
                if k == 0:
                    sp.wait_ge(emb_done, m + 1)
                sp.dma_start(Hs[0:NIMG, 2 * b, :], emb[NIMG * k:NIMG * (k + 1), m, :]).then_inc(ld_img, 16)

            def k_blocks(pb, u):
                sp.wait_ge(kh_ok, 2 * pb + 2)
                for j in range(4):
                    sp.dma_start(kbh[32 * j:32 * j + 32, u, :, j, :].bitcast(F32),
                                 kh[32 * j:32 * j + 32, :, :].bitcast(F32)).then_inc(kb_ok[u], 16)
                sp.wait_ge(kl_ok, 2 * pb + 2)
                for j in range(4):
                    sp.dma_start(kbl[32 * j:32 * j + 32, u, :, j, :].bitcast(F32),
                                 kl[32 * j:32 * j + 32, :, :].bitcast(F32)).then_inc(kb_ok[u], 16)

            sp.wait_ge(pads_zero, 1)
            k_blocks(0, 0)
            k_blocks(1, 1)
            w1_rows = w1.rearrange("e (k p) n -> e p k n", p=P)
            sp.wait_ge(ld_img, 16 * B)
            for e in range(2):
                sp.dma_start(W1s[:, e, :, :], w1_rows[e]).then_inc(ld_w1, 16)
            with sp.Fori(0, (B - 2) // 2) as i:
                for u in range(2):
                    k_blocks(2 * i + 2 + u, u)
                    sp.dma_start(W1s[:, bass.ds(2 * i + 2 + u, 1), :, :],
                                 w1_rows[bass.ds(2 * i + 2 + u, 1)].rearrange("e p k n -> p e k n")).then_inc(ld_w1, 16)
            sp.wait_ge(h_ok, B)
            for e in range(E):
                sp.dma_start(W2s[:, e, :, :], w2[e].rearrange("(k p) n -> p k n", p=P)).then_inc(ld_w2, 16)
                if e == 0:
                    sp.dma_start(bg_s[:, :], bg.partition_broadcast(C)).then_inc(ld_b2, 16)
                    sp.dma_start(b2_s[:, :, :], b2.partition_broadcast(P)).then_inc(ld_b2, 16)
                    sp.wait_ge(x2_ok, NBLK)
                    for dst, src in ((x2_dram, X2), (h2_dram, Hs)):
                        rows = dst[0:NTOK, :].rearrange("(b p) d -> p b d", p=C)
                        for a, b in PARTS:
                            sp.dma_start(rows[a:b], src[a:b, :, :]).then_inc(rows_out, 16)
                        sp.dma_start(dst[NTOK:NTOK + 1, :], X2[0:1, 0, :]).then_inc(rows_out, 16)

        @block.tensor
        def _(pe):
            mm = nc.tensor.matmul
            pe.wait_ge(ld_pat, 64)
            for m in range(3):
                rows = min(EB, B - EB * m) * NIMG
                for k in range(KC):
                    last = mm(bank[m][0:rows, 0:D], pat_s[:, k, EB * NIMG * m:EB * NIMG * m + rows], tokw_s[:, k, :],
                              start=(k == 0), stop=(k == KC - 1))
                last.then_inc(emb_ps, 1)
            pe.wait_ge(ld_w, 16 * NW)
            pe.wait_ge(ld_small, 16)
            for d in range(DC):
                for i in range(2):
                    mm(bank[3 + d][:, D * i:D * i + D], wq_s[:, i, P * d:P * d + P], mq_s[:, :], start=True, stop=True)
            for d in range(DC):
                for x, (w, m_) in enumerate(((wk_s, ma_s), (wv_s, mb_s))):
                    for i in range(2):
                        mm(bank[5][:, 256 * d + P * x:256 * d + P * x + P], w[:, i, P * d:P * d + P], m_[:, i, :],
                           start=(i == 0), stop=(i == 1))
            for g in range(G):
                mm(bank[6][:, g:g + 1], mq_s[:, P * (g % 2):P * (g % 2) + P], smal("bq")[:, g // 2:g // 2 + 1],
                   start=True, stop=True)
            for x, (m_, b_) in enumerate(((ma_s, "bk"), (mb_s, "bv"))):
                for i in range(2):
                    mm(bank[6][:, 4 + x:5 + x], m_[:, i, :], smal(b_)[:, i:i + 1], start=(i == 0), stop=(i == 1))
            pe.wait_ge(bv_spread, 1)
            for i in range(2):
                last = mm(bank[7][0:C, 0:D], bv_cols[:, i, :], wot_s[:, i, :], start=(i == 0), stop=(i == 1))
            last.then_inc(fold_ps, 1)

            def passes(out_ap, w_hi, w_lo, x_hi, x_lo, more=False):
                terms = [(w, x, d) for w, x in ((w_hi, x_hi), (w_lo, x_hi), (w_hi, x_lo)) for d in range(DC)]
                for n, (w, x, d) in enumerate(terms):
                    last = mm(out_ap, w(d), x(d), start=(n == 0), stop=(not more and n == len(terms) - 1))
                return last

            def turn_x(pb):
                pe.wait_ge(xhat_ok, pb + 1)
                if not few(pb):
                    pe.wait_ge(ql_ok, 2 * pb)
                for c in range(2):
                    for d in range(DC):
                        last = nc.tensor.transpose(piece_bank(pb, "x")[:, P * (2 * d + c):P * (2 * d + c) + P],
                                                   xhat[:, c, P * d:P * d + P], ident)
                last.then_inc(xt_ps, 1)

            def cross_operands(pb):
                pe.wait_ge(xtl_ok, pb + 1)
                if not first(pb):
                    pe.wait_ge(v_ok, pb)
                for x in range(2):
                    last = passes(piece_bank(pb, "cross")[:, T * x:T * x + T], lambda d: wch[:, d, x, :], lambda d: wcl[:, d, x, :],
                                  lambda d: xth[:, d, :], lambda d: xtl[:, d, :])
                last.then_inc(cr_ps, 1)

            def out_projection(ob, u):
                pe.wait_ge(ao_ok, G * ob + G)
                if isinstance(ob, int) and ob == B - 1:
                    pe.wait_ge(h_ok, B - 1)
                elif isinstance(ob, int) and ob == B - 2:
                    pe.wait_ge(v_ok, B)
                else:
                    pe.wait_ge(kl_ok, 2 * ob + 5)
                for c in range(2):
                    for g in range(G):
                        last = mm(bank[7][0:C, D * c:D * c + D], AO[:, u, g, C * c:C * c + C], wo_s[:, g, :],
                                  start=(g == 0), stop=(g == G - 1))
                last.then_inc(o_ps, 1)

            def q_groups(pb, half):
                if half == 1 and not first(pb):
                    pe.wait_ge(kl_ok, 2 * pb + 2)
                for x in range(2):
                    g = 2 * half + x
                    last = passes(piece_bank(pb, f"q{half}")[:, T * x:T * x + T], lambda d: wqh[:, d, P * g:P * g + P],
                                  lambda d: wql[:, d, P * g:P * g + P], lambda d: xth[:, d, :], lambda d: xtl[:, d, :])
                last.then_inc(q_ps, 1)

            def k_groups(pb, half):
                if half == 1 and not first(pb):
                    pe.wait_ge(ql_ok, 2 * pb + 1)
                if half == 0:
                    pe.wait_ge(prods_ok, pb + 1)
                for x in range(2):
                    g = 2 * half + x
                    o = piece_bank(pb, f"k{half}")[:, T * x:T * x + T]
                    passes(o, lambda d: wkh[:, d, P * g:P * g + P], lambda d: wkl[:, d, P * g:P * g + P],
                           lambda d: xth[:, d, :], lambda d: xtl[:, d, :], more=True)
                    mm(o, sel_r[:, g, :], prodh[:, :], start=False, stop=False)
                    last = mm(o, sel_r[:, g, :], prodl[:, :], start=False, stop=True)
                last.then_inc(k_ps, 1)

            def v_rows(pb):
                if not few(pb):
                    pe.wait_ge(h_ok, pb - 1)
                for c in range(2):
                    last = passes(piece_bank(pb, "v")[0:C, D * c:D * c + D], lambda d: xth[:, d, C * c:C * c + C],
                                  lambda d: xtl[:, d, C * c:C * c + C], lambda d: wvh[:, d, :], lambda d: wvl[:, d, :])
                last.then_inc(v_ps, 1)

            def piece(k, pb, u):
                if k == 0:
                    turn_x(pb)
                elif k == 1:
                    cross_operands(pb)
                elif k == 2:
                    q_groups(pb, 0)
                elif k in (3, 4):
                    k_groups(pb, k - 3)
                elif k == 5:
                    if not few(pb):
                        out_projection(pb - 2, u)
                elif k == 6:
                    q_groups(pb, 1)
                else:
                    v_rows(pb)

            def scores(b, u, p):
                if p == 0:
                    pe.wait_ge(kb_ok[u], kb_count(b, u))
                if not (isinstance(b, int) and b == 0 and p == 0):
                    pe.wait_ge(sub_ok, 8 * b + p)
                g, j = p // 2, 2 * (p % 2)
                for c in range(2):
                    for n, (q, kb) in enumerate(((qh, kbh), (ql, kbh), (qh, kbl))):
                        last = mm(bank[c][0:C, 0:2 * T], q[:, u, g, C * c:C * c + C], kb[:, u, g, j:j + 2, :],
                                  start=(n == 0), stop=(n == 2))
                last.then_inc(s_ps, 1)

            def turn_probs(b, p):
                pe.wait_ge(exp_ok, 8 * b + p + 1)
                if not (isinstance(b, int) and b == 0 and p == 0):
                    pe.wait_ge(prt_ok, 8 * b + p)
                for x in range(2):
                    for k in range(2):
                        for c in range(2):
                            at_ = P * (2 * k + c)
                            last = nc.tensor.transpose(bank[2 + x][0:C, at_:at_ + P],
                                                       pr[:, p % 4, c, x, C * k:C * k + C], ident)
                last.then_inc(t_ps, 1)

            def weigh_values(b, u, p):
                g = p // 2
                if p == 0:
                    pe.wait_ge(v_ok, b + 1)
                if p % 2 == 0 and not (isinstance(b, int) and b == 0 and g < 2):
                    pe.wait_ge(ao_ok, G * b + g - 1)
                pe.wait_ge(prt_ok, 8 * b + p + 1)
                for h in (2 * p, 2 * p + 1):
                    j = h % 4
                    for k in range(2):
                        last = mm(bank[4 + g % 2][32 * j:32 * j + 32, 0:T], V[:, u, k, h, :], prt[:, h % 4, k, :],
                                  start=(k == 0), stop=(k == 1))
                last.then_inc(pv_ps, 1)

            def batch(b, u, project=True):
                for s in range(8):
                    scores(b, u, s)
                    tb, tu, tp = (b, u, s - 2) if s >= 2 else (b - 1, 1 - u, s + 6)
                    if s >= 2 or not first(b):
                        turn_probs(tb, tp)
                    if project:
                        piece(s, b + 1, 1 - u)
                    elif s == 5:
                        out_projection(b - 1, 1 - u)
                    if s >= 2 or not first(b):
                        weigh_values(tb, tu, tp)

            pe.wait_ge(parts_done, 1)
            pe.wait_ge(pads_zero, 1)
            for k in range(8):
                piece(k, 0, 0)
            batch(0, 0)
            with pe.Fori(0, (B - 2) // 2) as i:
                batch(2 * i + 1, 1)
                batch(2 * i + 2, 0)
            batch(B - 1, 1, project=False)
            for p in (6, 7):
                turn_probs(B - 1, p)
                weigh_values(B - 1, 1, p)
            out_projection(B - 1, 1)

            def turn_rows(q):
                pe.wait_ge(x2_ok, 2 * q + 2)
                if q >= 2:
                    pe.wait_ge(g_ok, q - 1)
                for x in range(2):
                    for d in range(DC):
                        n = 2 * x + d
                        last = nc.tensor.transpose(bank[q % 2][:, C * n:C * n + C], X2[:, 2 * q + x, P * d:P * d + P],
                                                   ident[0:C, 0:C])
                last.then_inc(g_ps, 1)

            def gate(q):
                pe.wait_ge(g_ok, q + 1)
                for x in range(2):
                    blk = 2 * q + x
                    for d in range(DC):
                        last = mm(bank[2][0:C, E * blk:E * blk + E], x2t[:, q % 2, 2 * x + d, :],
                                  smal("wg")[:, E * d:E * d + E], start=(d == 0), stop=(d == DC - 1))
                last.then_inc(lg_ps, 1)

            for q in range(NBLK // 2 + 1):
                if q < NBLK // 2:
                    turn_rows(q)
                if q >= 1:
                    gate(q - 1)
            pe.wait_ge(hot_ok, 1)
            mm(bank[3][0:C, 0:E * NBLK], con("before", C)[:, 0:C], onehot[:, :, :], start=True, stop=False)
            mm(bank[3][0:C, 0:E * NBLK], con("full", C)[:, 0:C], earlier[:, :, :], start=False, stop=True)
            mm(bank[4][:, 0:E], con("full", C), upto[:, :, NBLK - 1], start=True, stop=True).then_inc(rank_ps, 1)
            pe.wait_ge(slots_hot, 1)
            for blk in range(NBLK):
                last = mm(bank[5][:, 0:2 * TILES], slot_hot[:, blk, :], tile_hot[:, blk, :, :],
                          start=(blk == 0), stop=(blk == NBLK - 1))
            last.then_inc(slots_ps, 1)

            def turn_tile(t):
                pe.wait_ge(gx_in, 16 * t + 16)
                for d in range(DC):
                    last = nc.tensor.transpose(bank[6][:, P * d:P * d + P], gx[:, P * d:P * d + P], ident)
                last.then_inc(tx_ps, 1)

            def first_product(t, e):
                pe.wait_ge(tx_ok, t + 1)
                for n in range(2):
                    for d in range(DC):
                        last = mm(bank[n][:, :], xt[:, d, :], W1s[:, bass.ds(e, 1), d, 512 * n:512 * n + 512],
                                  start=(d == 0), stop=(d == DC - 1))
                    last.then_inc(l1_ps, 1)

            def turn_hidden(t):
                pe.wait_ge(z_ok, 2 * t + 2)
                for k in range(HC):
                    last = nc.tensor.transpose(bank[2 + k // 4][:, P * (k % 4):P * (k % 4) + P], z[:, P * k:P * k + P], ident)
                    if k % 4 == 3:
                        last.then_inc(zt_ps, 1)

            def second_product(t, e):
                pe.wait_ge(silu_ok, HC * t + HC)
                if not first(t):
                    pe.wait_ge(y1_ok, t)
                for k in range(HC):
                    last = mm(bank[4][:, 0:D], ht[:, k, :], W2s[:, bass.ds(e, 1), k, :], start=(k == 0), stop=(k == HC - 1))
                last.then_inc(l2_ps, 1)

            def expert(t):
                return pe.value_load(et[0:1, bass.ds(t, 1)], min_val=0, max_val=E - 1)

            pe.wait_ge(et_ok, 1)
            turn_tile(0)
            pe.wait_ge(ld_w1, 16 * E)
            first_product(0, expert(0))
            turn_tile(1)
            pe.wait_ge(ld_w2, 16 * E)
            with pe.Fori(1, TILES - 1) as t:
                turn_hidden(t - 1)
                first_product(t, expert(t))
                turn_tile(t + 1)
                second_product(t - 1, expert(t - 1))
            turn_hidden(TILES - 2)
            first_product(TILES - 1, expert(TILES - 1))
            second_product(TILES - 2, expert(TILES - 2))
            turn_hidden(TILES - 1)
            second_product(TILES - 1, expert(TILES - 1))

        @block.scalar
        def _(act):
            fn = nc.scalar.activation
            act.wait_ge(aggr_done, 1)
            fn(sd[:, :], mv[:, :, 1], ACT.Sqrt).then_inc(sd_done, 1)

            def high_x(pb):
                act.wait_ge(xt_ps, pb + 1)
                fn(xth[:, :, :].rearrange("p d (c t) -> p (d c) t", c=2),
                   piece_bank(pb, "x")[:, :].rearrange("p (n t) -> p n t", t=P)[:, :, 0:C], ACT.Copy).then_inc(xth_ok, 1)

            def cross_a(pb):
                act.wait_ge(cr_ps, pb + 1)
                fn(crossa[:, :], piece_bank(pb, "cross")[:, 0:T], ACT.Identity, bias=cbias[:, 0:1]).then_inc(cra_ok, 1)

            def high_q(pb, u, half):
                act.wait_ge(q_ps, 2 * pb + half + 1)
                for x in range(2):
                    g = 2 * half + x
                    last = fn(qh[:, u, g, :], piece_bank(pb, f"q{half}")[:, T * x:T * x + T], ACT.Identity, bias=qbias[:, g:g + 1])
                last.then_inc(qh_ok, 1)

            def high_k(pb, u, half):
                if half == 0 and not first(pb):
                    act.wait_ge(kb_ok[1 - u], kb_count(pb - 1, 1 - u))
                act.wait_ge(k_ps, 2 * pb + half + 1)
                for x in range(2):
                    g = 2 * half + x
                    last = fn(kh[:, g, :], piece_bank(pb, f"k{half}")[:, T * x:T * x + T], ACT.Identity,
                              bias=smal("bk_rows")[:, g:g + 1])
                last.then_inc(kh_ok, 1)

            def values(pb, u):
                act.wait_ge(v_ps, pb + 1)
                fn(V[0:C, u, :, :, 0:HD], piece_bank(pb, "v")[0:C, :].rearrange("p (k h f) -> p k h f", k=2, h=H),
                   ACT.Copy).then_inc(v_ok, 1)

            def piece(k, pb, u):
                if k == 0:
                    high_x(pb)
                elif k == 1:
                    cross_a(pb)
                elif k in (2, 6):
                    high_q(pb, u, k // 4)
                elif k in (3, 4):
                    high_k(pb, u, k - 3)
                elif k == 7:
                    values(pb, u)

            def copy_turned(b, p):
                act.wait_ge(t_ps, 8 * b + p + 1)
                if not (isinstance(b, int) and b == 0 and p < 2):
                    act.wait_ge(pv_ps, 8 * b + p - 1)
                r = 2 * (p % 2)
                fn(prt[0:C, r:r + 2, :, :].rearrange("p h k (c t) -> p h (k c) t", c=2),
                   pair23[0:C, :, :].rearrange("p h (n t) -> p h n t", t=P)[:, :, :, 0:C], ACT.Copy).then_inc(prt_ok, 1)

            def exps(b, p):
                act.wait_ge(sub_ok, 8 * b + p + 1)
                w = pr[0:C, p % 4, :, :, :]
                fn(w, w, ACT.Exp).then_inc(exp_ok, 1)

            def batch(b, u, project=True):
                for s in range(8):
                    if s >= 2:
                        copy_turned(b, s - 2)
                    elif not first(b):
                        copy_turned(b - 1, s + 6)
                    exps(b, s)
                    if project:
                        piece(s, b + 1, 1 - u)

            act.wait_ge(parts_done, 1)
            act.wait_ge(pads_zero, 1)
            for k in range(8):
                piece(k, 0, 0)
            batch(0, 0)
            with act.Fori(0, (B - 2) // 2) as i:
                batch(2 * i + 1, 1)
                batch(2 * i + 2, 0)
            batch(B - 1, 1, project=False)
            for p in (6, 7):
                copy_turned(B - 1, p)

            act.wait_ge(aggr_done, 2)
            fn(sd[:, :], mv[:, :, 1], ACT.Sqrt).then_inc(sd_done, 1)
            for q in range(NBLK // 2):
                act.wait_ge(g_ps, q + 1)
                if q >= 2:
                    act.wait_ge(lg_ps, q - 1)
                fn(x2t[:, q % 2, :, :], bank[q % 2][:, 0:4 * C].rearrange("p (n t) -> p n t", t=C),
                   ACT.Copy).then_inc(g_ok, 1)
            act.wait_ge(lgsub_ok, 1)
            fn(ex[:, :, :], ex[:, :, :], ACT.Exp).then_inc(ex_ok, 1)

            def copy_tile(t):
                act.wait_ge(tx_ps, t + 1)
                if not first(t):
                    act.wait_ge(l1_ps, 2 * t)
                fn(xt[:, :, :], bank[6][:, 0:D].rearrange("p (d t) -> p d t", t=P), ACT.Copy).then_inc(tx_ok, 1)

            def silu(t):
                act.wait_ge(b1_ok, t + 1)
                for k in range(HC):
                    if k % 4 == 0:
                        act.wait_ge(zt_ps, 2 * t + k // 4 + 1)
                    fn(ht[:, k, :], bank[2 + k // 4][:, P * (k % 4):P * (k % 4) + P], ACT.Silu,
                       bias=b1c[:, k:k + 1]).then_inc(silu_ok, 1)

            copy_tile(0)
            copy_tile(1)
            with act.Fori(1, TILES - 1) as t:
                silu(t - 1)
                copy_tile(t + 1)
            silu(TILES - 2)
            silu(TILES - 1)

        @block.vector
        def _(dve):
            v = nc.vector
            dve.wait_ge(ld_pat, 64)
            v.tensor_tensor(pos_s[:, :], pos_s[:, :], tokb_s[:, :], ALU.add).then_inc(posb_done, 1)
            dve.wait_ge(posb_done, 1)
            for m in range(3):
                rows = min(EB, B - EB * m) * NIMG
                dve.wait_ge(emb_ps, m + 1)
                v.tensor_tensor(emb[0:rows, m, :], bank[m][0:rows, 0:D], pos_s[0:rows, :], ALU.add).then_inc(emb_done, 1)
            dve.wait_ge(ld_const, 16)
            dve.wait_ge(ld_small, 16)
            for i in range(2):
                last = v.tensor_scalar(bv_cols[:, i, :], con("full")[:, 0:C], smal("bv")[:, i:i + 1], None, ALU.mult)
            last.then_inc(bv_spread, 1)
            dve.wait_ge(ld_w, 16 * NW)
            temp = smal("temp")
            v.tensor_copy(wkh[:, :, :], wkp_s[:, :, :]).then_inc(parts_hi, 1)
            v.tensor_copy(wvh[:, :, :], wvt_s[:, :, :]).then_inc(parts_hi, 1)
            v.tensor_copy(sel_r[:, :, :], sel_s[:, :, :]).then_inc(parts_hi, 1)
            dve.wait_ge(fold_ps, 1)
            for d in range(DC):
                v.tensor_scalar(wqh[:, d, :], bank[3 + d][:, :], temp, None, ALU.mult).then_inc(parts_hi, 1)
            v.tensor_copy(wch[:, :, :, :], bank[5][:, :].rearrange("p (d x n) -> p d x n", d=DC, x=2)).then_inc(parts_hi, 1)
            v.tensor_scalar(qbias[:, :], bank[6][:, 0:G], smal("bqs_rows"), temp, ALU.add, ALU.mult)
            v.tensor_tensor(cbias[:, 0:1], bank[6][:, 4:5], smal("bks_rows"), ALU.add)
            v.tensor_tensor(cbias[:, 1:2], bank[6][:, 5:6], smal("bvs_rows"), ALU.add)
            v.tensor_tensor(obias[:, :], bank[7][0:C, 0:D], bo_s[:, :], ALU.add)
            dve.wait_ge(parts_hi, 6)
            v.tensor_tensor(wkl[:, :, :], wkp_s[:, :, :], wkh[:, :, :].bitcast(F32), ALU.subtract)
            v.tensor_tensor(wvl[:, :, :], wvt_s[:, :, :], wvh[:, :, :].bitcast(F32), ALU.subtract)
            for d in range(DC):
                v.scalar_tensor_tensor(wql[:, d, :], bank[3 + d][:, :], temp, wqh[:, d, :].bitcast(F32), ALU.mult, ALU.subtract)
            v.tensor_tensor(wcl[:, :, :, :], bank[5][:, :].rearrange("p (d x n) -> p d x n", d=DC, x=2),
                            wch[:, :, :, :].bitcast(F32), ALU.subtract).then_inc(parts_done, 1)

            def row_stats(round_):
                for blk in range(NBLK):
                    last = v.bn_stats(stats[:, blk, :], Hs[:, blk, :])
                last.then_inc(stats_done, 1)
                dve.wait_ge(stats_done, round_)
                for blk in range(NBLK):
                    last = v.bn_aggr(mv[:, blk, :], stats[:, blk, :])
                last.then_inc(aggr1, 1)
                dve.wait_ge(aggr1, round_)
                v.tensor_scalar(mv[:, :, 1], mv[:, :, 1], EPS, None, ALU.add).then_inc(aggr_done, 1)
                dve.wait_ge(sd_done, round_)
                v.reciprocal(rstd[:, :], sd[:, :]).then_inc(rstd_done, 1)
                dve.wait_ge(rstd_done, round_)

            dve.wait_ge(ld_txt, 64)
            dve.wait_ge(ld_img, 16 * B)
            row_stats(1)

            def normed(pb):
                if not first(pb):
                    dve.wait_ge(xt_ps, pb)
                for c in range(2):
                    blk = 2 * pb + c
                    last = v.tensor_scalar(xhat[0:C, c:c + 1, :], Hs[:, bass.ds(blk, 1), :], mv[:, bass.ds(blk, 1), 0],
                                           rstd[:, bass.ds(blk, 1)], ALU.subtract, ALU.mult)
                last.then_inc(xhat_ok, 1)

            def low_x(pb):
                dve.wait_ge(xth_ok, pb + 1)
                v.tensor_tensor(xtl[:, :, :].rearrange("p d (c t) -> p (d c) t", c=2),
                                piece_bank(pb, "x")[:, :].rearrange("p (n t) -> p n t", t=P)[:, :, 0:C],
                                xth[:, :, :].bitcast(F32).rearrange("p d (c t) -> p (d c) t", c=2),
                                ALU.subtract).then_inc(xtl_ok, 1)

            def cross_products(pb):
                dve.wait_ge(cra_ok, pb + 1)
                v.scalar_tensor_tensor(prod[:, :], piece_bank(pb, "cross")[:, T:2 * T], cbias[:, 1:2], crossa[:, :],
                                       ALU.add, ALU.mult).then_inc(prod_ok, 1)

            def low_q(pb, u, half):
                dve.wait_ge(qh_ok, 2 * pb + half + 1)
                for x in range(2):
                    g = 2 * half + x
                    last = v.scalar_tensor_tensor(ql[:, u, g, :], piece_bank(pb, f"q{half}")[:, T * x:T * x + T], qbias[:, g:g + 1],
                                                  qh[:, u, g, :].bitcast(F32), ALU.add, ALU.subtract)
                last.then_inc(ql_ok, 1)

            def low_k(pb, u, half):
                if half == 0 and not first(pb):
                    dve.wait_ge(kb_ok[1 - u], kb_count(pb - 1, 1 - u))
                dve.wait_ge(kh_ok, 2 * pb + half + 1)
                for x in range(2):
                    g = 2 * half + x
                    last = v.scalar_tensor_tensor(kl[:, g, :], piece_bank(pb, f"k{half}")[:, T * x:T * x + T],
                                                  smal("bk_rows")[:, g:g + 1], kh[:, g, :].bitcast(F32),
                                                  ALU.add, ALU.subtract)
                last.then_inc(kl_ok, 1)

            def add_out(ob):
                dve.wait_ge(hb_ok, ob + 1)
                dve.wait_ge(o_ps, ob + 1)
                rows = Hs[:, bass.ds(2 * ob, 2), :]
                v.tensor_tensor(rows, bank[7][0:C, :].rearrange("p (c d) -> p c d", c=2), rows, ALU.add).then_inc(h_ok, 1)

            def piece(k, pb, u):
                if k == 0:
                    low_x(pb)
                elif k == 1:
                    cross_products(pb)
                elif k == 5:
                    if not few(pb):
                        add_out(pb - 2)
                elif k in (2, 6):
                    low_q(pb, u, k // 4)
                elif k in (3, 4):
                    low_k(pb, u, k - 3)

            def find_max(b, p):
                dve.wait_ge(s_ps, 8 * b + p + 1)
                v.tensor_reduce(mx[:, p, :, :], scored, AX.X, ALU.max).then_inc(mx_ok, 1)

            def shift(b, p):
                if not (isinstance(b, int) and b == 0 and p < 4):
                    dve.wait_ge(t_ps, 8 * b + p - 3)
                dve.wait_ge(mx_ok, 8 * b + p + 1)
                v.tensor_tensor(pr[0:C, p % 4, :, :, :], scored, mx[:, p, :, :].unsqueeze(3).to_broadcast([C, 2, 2, T]),
                                ALU.subtract).then_inc(sub_ok, 1)

            scored = pair01[0:C, :, 0:2 * T].rearrange("p c (h t) -> p c h t", h=2)

            def take_sums(g):
                v.stream_shuffle(den[:, :], bank[4 + g % 2][:, 0:T], [16 + (i % 16) for i in range(32)]).then_inc(den_ok, 1)

            def normalise(b, u, g):
                dve.wait_ge(den_ok, G * b + g + 1)
                v.reciprocal(den[:, :], den[:, :]).then_inc(rden_ok, 1)
                if g == 0 and not few(b):
                    dve.wait_ge(o_ps, b - 1)
                dve.wait_ge(rden_ok, G * b + g + 1)
                v.tensor_tensor(AO[:, u, g, :], bank[4 + g % 2][:, 0:T], den[:, :], ALU.mult).then_inc(ao_ok, 1)

            def batch(b, u, project=True, norm_next=True):
                for s in range(8):
                    find_max(b, s)
                    complete = s in (4, 6) or (s in (0, 2) and not first(b))
                    of, of_u, g = (b, u, s // 2 - 2) if s >= 4 else (b - 1, 1 - u, s // 2 + 2)
                    if complete:
                        take_sums(g)
                    shift(b, s)
                    if complete:
                        normalise(of, of_u, g)
                    if s == 6 and project and norm_next:
                        normed(b + 2)
                    if project:
                        piece(s, b + 1, 1 - u)
                    elif s == 5:
                        add_out(b - 1)

            dve.wait_ge(pads_zero, 1)
            normed(0)
            for k in range(8):
                piece(k, 0, 0)
                if k == 0:
                    normed(1)
            batch(0, 0)
            with dve.Fori(0, (B - 2) // 2 - 1) as i:
                batch(2 * i + 1, 1)
                batch(2 * i + 2, 0)
            batch(B - 3, 1)
            batch(B - 2, 0, norm_next=False)
            batch(B - 1, 1, project=False)
            for g in (2, 3):
                dve.wait_ge(ao_ok, G * (B - 1) + g)
                dve.wait_ge(pv_ps, 8 * (B - 1) + 2 * g + 2)
                take_sums(g)
                normalise(B - 1, 1, g)
            add_out(B - 1)

            count = [0]

            def link(ins):
                count[0] += 1
                ins.then_inc(dve_step, 1)
                dve.wait_ge(dve_step, count[0])

            dve.wait_ge(h_ok, B)
            row_stats(2)
            for blk in range(NBLK):
                v.tensor_scalar(X2[:, blk, :], Hs[:, blk, :], mv[:, blk, 0:1], rstd[:, blk:blk + 1],
                                ALU.subtract, ALU.mult).then_inc(x2_ok, 1)
            dve.wait_ge(ld_b2, 32)
            dve.wait_ge(lg_ps, NBLK // 2)
            link(v.tensor_tensor(lg[:, :, :], bank[2][0:C, 0:E * NBLK].rearrange("p (b e) -> p b e", e=E),
                                 bg_s[:, :].unsqueeze(1).to_broadcast([C, NBLK, E]), ALU.add))
            link(v.tensor_reduce(lgmax[:, :], lg[:, :, :], AX.X, ALU.max))
            wide = lgmax[:, :].unsqueeze(2).to_broadcast([C, NBLK, E])
            v.tensor_tensor(ex[:, :, :], lg[:, :, :], wide, ALU.subtract).then_inc(lgsub_ok, 1)
            link(v.tensor_tensor(hit[:, :, :], lg[:, :, :], wide, ALU.is_equal))
            link(v.tensor_tensor(hit[:, :, :], hit[:, :, :], con("backward", C).unsqueeze(1).to_broadcast([C, NBLK, E]), ALU.mult))
            link(v.tensor_reduce(firsthit[:, :], hit[:, :, :], AX.X, ALU.max))
            link(v.tensor_tensor(onehot[:, :, :].rearrange("p e b -> p b e"), hit[:, :, :],
                                 firsthit[:, :].unsqueeze(2).to_broadcast([C, NBLK, E]), ALU.is_equal))
            link(v.tensor_tensor_scan(upto[:, :, :].rearrange("p e b -> p (e b)"), con("restart", C),
                                      onehot[:, :, :].rearrange("p e b -> p (e b)"), 0.0, ALU.mult, ALU.add))
            v.tensor_tensor(earlier[:, :, :], upto[:, :, :], onehot[:, :, :], ALU.subtract).then_inc(hot_ok, 1)
            dve.wait_ge(ex_ok, 1)
            link(v.tensor_reduce(exsum[:, :], ex[:, :, :], AX.X, ALU.add))
            v.reciprocal(wtop[:, :], exsum[:, :])
            dve.wait_ge(rank_ps, 1)
            link(v.tensor_tensor(ntiles_cmp[:, :, :], bank[4][:, 0:E].unsqueeze(2).to_broadcast([P, E, 11]),
                                 con("tile_start")[:, 0:11].unsqueeze(1).to_broadcast([P, E, 11]), ALU.is_gt))
            link(v.tensor_reduce(ntiles[:, :], ntiles_cmp[:, :, :], AX.X, ALU.add))
            link(v.tensor_tensor_scan(tiles_upto[:, :], con("full")[:, 0:E], ntiles[:, :], 0.0, ALU.mult, ALU.add))
            link(v.tensor_tensor(base[:, :], tiles_upto[:, :], ntiles[:, :], ALU.subtract))
            link(v.tensor_scalar(base[:, :], base[:, :], float(SLOTS), None, ALU.mult))
            link(v.tensor_tensor(posn[:, :, :], bank[3][0:C, 0:E * NBLK].rearrange("p (e b) -> p e b", e=E),
                                 base[0:C, :].unsqueeze(2).to_broadcast([C, E, NBLK]), ALU.add))
            link(v.tensor_tensor(posn[:, :, :], posn[:, :, :], onehot[:, :, :], ALU.mult))
            link(v.tensor_reduce(pos[:, :], posn[:, :, :].rearrange("p e b -> p b e"), AX.X, ALU.add))
            link(v.tensor_tensor(tile_cmp[:, :, :], pos[:, :].unsqueeze(2).to_broadcast([C, NBLK, TILES - 1]),
                                 con("tile_start", C)[:, 1:TILES].unsqueeze(1).to_broadcast([C, NBLK, TILES - 1]), ALU.is_ge))
            link(v.tensor_reduce(tile_of[:, :], tile_cmp[:, :, :], AX.X, ALU.add))
            link(v.tensor_scalar(slot_of[:, :], tile_of[:, :], -float(SLOTS), None, ALU.mult))
            link(v.tensor_tensor(slot_of[:, :], slot_of[:, :], pos[:, :], ALU.add))
            v.tensor_tensor(slot_hot[:, :, :], con("iota", C).unsqueeze(1).to_broadcast([C, NBLK, SLOTS]),
                            slot_of[:, :].unsqueeze(2).to_broadcast([C, NBLK, SLOTS]), ALU.is_equal)
            link(v.tensor_tensor(tile_hot[:, :, 0, :], con("iota", C)[:, 0:TILES].unsqueeze(1).to_broadcast([C, NBLK, TILES]),
                                 tile_of[:, :].unsqueeze(2).to_broadcast([C, NBLK, TILES]), ALU.is_equal))
            link(v.tensor_tensor(tile_hot[:, :, 1, :], tile_hot[:, :, 0, :],
                                 wtop[:, :].unsqueeze(2).to_broadcast([C, NBLK, TILES]), ALU.mult))
            v.tensor_tensor(tile_hot[:, :, 0, :], tile_hot[:, :, 0, :],
                            con("tokid", C).unsqueeze(2).to_broadcast([C, NBLK, TILES]), ALU.mult).then_inc(slots_hot, 1)
            link(v.tensor_tensor(et_cmp[:, :, :], tiles_upto[0:1, :].unsqueeze(1).to_broadcast([1, TILES, E]),
                                 con("iota", 1)[:, 0:TILES].unsqueeze(2).to_broadcast([1, TILES, E]), ALU.is_le))
            link(v.tensor_reduce(et_f[:, :], et_cmp[:, :, :], AX.X, ALU.add))
            v.tensor_scalar(et[:, :], et_f[:, :], float(E - 1), None, ALU.min).then_inc(et_ok, 1)
            dve.wait_ge(slots_ps, 1)
            v.tensor_copy(wslot[:, :], bank[5][:, TILES:2 * TILES])
            v.tensor_scalar(ids[:, :], bank[5][:, 0:TILES], float(NTOK), None, ALU.add).then_inc(ids_ok, 1)

            def expert(t):
                return dve.value_load(et[0:1, bass.ds(t, 1)], min_val=0, max_val=E - 1)

            def tile_bias(t, e):
                if not first(t):
                    dve.wait_ge(silu_ok, HC * t)
                v.tensor_copy(b1c[:, :].unsqueeze(1), smal("b1").rearrange("p (e k) -> p e k", e=E)[:, bass.ds(e, 1), :]).then_inc(b1_ok, 1)

            def copy_hidden(t):
                if not first(t):
                    dve.wait_ge(zt_ps, 2 * t)
                for n in range(2):
                    dve.wait_ge(l1_ps, 2 * t + n + 1)
                    v.tensor_copy(z[:, 512 * n:512 * n + 512], bank[n][:, :]).then_inc(z_ok, 1)

            def finish(t, e):
                dve.wait_ge(l2_ps, t + 1)
                if not first(t):
                    dve.wait_ge(y_ok, t)
                v.tensor_tensor(y1[:, :].unsqueeze(1), bank[4][:, 0:D].unsqueeze(1), b2_s[:, bass.ds(e, 1), :], ALU.add).then_inc(y1_ok, 1)
                dve.wait_ge(gh_in, 16 * t + 16)
                if not first(t):
                    dve.wait_ge(sc_out, 16 * t)
                dve.wait_ge(y1_ok, t + 1)
                v.scalar_tensor_tensor(Y[:, :], y1[:, :], wslot[:, bass.ds(t, 1)], gh[:, :], ALU.mult, ALU.add).then_inc(y_ok, 1)

            dve.wait_ge(et_ok, 1)
            dve.wait_ge(ids_ok, 1)
            copy_hidden(0)
            tile_bias(0, expert(0))
            with dve.Fori(1, TILES) as t:
                copy_hidden(t)
                tile_bias(t, expert(t))
                finish(t - 1, expert(t - 1))
            finish(TILES - 1, expert(TILES - 1))

        @block.gpsimd
        def _(pool):
            g = nc.gpsimd
            g.memset(kbh[:, :, :, :, :].bitcast(F32), 0.0)
            g.memset(kbl[:, :, :, :, :].bitcast(F32), 0.0)
            g.memset(xhat[:, :, :], 0.0)
            g.memset(pr[:, :, :, :, :], 0.0)
            g.memset(prt[:, :, :, :], 0.0)
            g.memset(V[:, :, :, :, :], 0.0).then_inc(v_zero, 1)
            pool.wait_ge(v_zero, 1)
            g.memset(V[0:C, :, :, :, HD:32], 1.0).then_inc(pads_zero, 1)

            def parts_of_products(pb):
                pool.wait_ge(prod_ok, pb + 1)
                g.tensor_tensor(prodh[:, :], prod[:, :], con("full")[:, 0:1].to_broadcast([P, T]), ALU.mult).then_inc(prodh_ok, 1)
                pool.wait_ge(prodh_ok, pb + 1)
                g.tensor_tensor(prodl[:, :], prod[:, :], prodh[:, :].bitcast(F32), ALU.subtract).then_inc(prods_ok, 1)

            def add_out_bias(b):
                rows = Hs[:, bass.ds(2 * b, 2), :]
                g.tensor_tensor(rows, rows, obias[:, :].unsqueeze(1).to_broadcast([C, 2, D]), ALU.add).then_inc(hb_ok, 1)

            pool.wait_ge(parts_done, 1)
            parts_of_products(0)
            pool.wait_ge(xhat_ok, 1)
            add_out_bias(0)
            with pool.Fori(1, B) as b:
                parts_of_products(b)
                pool.wait_ge(xhat_ok, b + 1)
                add_out_bias(b)

            pool.wait_ge(ids_ok, 1)
            pool.wait_ge(rows_out, 16 * 6)

            def gather_normed(t):
                g.indirect_dma_start(out=gx[:, :], out_offset=None, in_=x2_dram,
                                     in_offset=bass.IndirectOffsetOnAxis(ap=ids[:, t:t + 1], axis=0)).then_inc(gx_in, 16)

            def gather_residual(t):
                g.indirect_dma_start(out=gh[:, :], out_offset=None, in_=h2_dram,
                                     in_offset=bass.IndirectOffsetOnAxis(ap=ids[:, t:t + 1], axis=0)).then_inc(gh_in, 16)

            def scatter(t):
                pool.wait_ge(y_ok, t + 1)
                g.indirect_dma_start(out=out_rows, out_offset=bass.IndirectOffsetOnAxis(ap=ids[:, t:t + 1], axis=0),
                                     in_=Y[:, :], in_offset=None, bounds_check=NTOK - 1, oob_is_err=False).then_inc(sc_out, 16)

            gather_normed(0)
            pool.wait_ge(tx_ps, 1)
            gather_normed(1)
            for t in range(TILES):
                if t >= 1:
                    pool.wait_ge(y_ok, t)
                gather_residual(t)
                if t + 2 < TILES:
                    pool.wait_ge(tx_ps, t + 2)
                    gather_normed(t + 2)
                scatter(t)
            pool.wait_ge(sc_out, 16 * TILES)


def kernel(x, txt, L0_tok_W, L0_tok_b, L0_tok_pos_embd, L0_attn_Wq, L0_attn_bq, L0_attn_Wk, L0_attn_bk, L0_attn_Wv,
           L0_attn_bv, L0_attn_Wo, L0_attn_bo, L0_attn_Wqs, L0_attn_bqs, L0_attn_Wks, L0_attn_bks, L0_attn_Wvs,
           L0_attn_bvs, L0_attn_temp, L0_ffn_Wg, L0_ffn_bg, L0_ffn_W1, L0_ffn_b1, L0_ffn_W2, L0_ffn_b2):
    import concourse.bacc as bacc
    from concourse.bass_utils import run_bass_kernel_spmd

    f = np.float32
    wq, wk, wv, wo = (np.asarray(w) for w in (L0_attn_Wq, L0_attn_Wk, L0_attn_Wv, L0_attn_Wo))
    n = IMG // PATCH
    patches = np.asarray(x).reshape(B, CH, n, PATCH, n, PATCH).transpose(1, 3, 5, 0, 2, 4).reshape(PD, B * NIMG)
    wk_pad = np.zeros((D, H, 32), f)
    wk_pad[:, :, :HD] = wk.T.reshape(D, H, HD)
    wo_pad = np.zeros((H, 32, D), f)
    wo_pad[:, :HD] = wo.T.reshape(H, HD, D)
    mq = np.zeros((8, HD, 8, 32), f)
    ma = np.zeros((2, 8, HD, P), f)
    mb = np.zeros((2, 8, HD, P), f)
    wqs, wks, wvs = (np.asarray(w) for w in (L0_attn_Wqs, L0_attn_Wks, L0_attn_Wvs))
    bqs, bks, bvs = (np.asarray(w) for w in (L0_attn_bqs, L0_attn_bks, L0_attn_bvs))
    bqs_rows, bks_rows, bvs_rows = np.zeros((4, 32), f), np.zeros(P, f), np.zeros(P, f)
    bqs_rows[:, HD:HD + 3] = bqs
    for h in range(8):
        mq[h, :, h, :HD] = np.eye(HD, dtype=f)
        mq[h, :, h, HD:HD + 3] = wqs.T
    for h in range(H):
        for c in range(3):
            c1, c2 = (c + 1) % 3, (c + 2) % 3
            lo, hi = 3 * h + c, 64 + 3 * h + c
            ma[h // 8, h % 8, :, lo], ma[h // 8, h % 8, :, hi] = wks[c1], wks[c2]
            mb[h // 8, h % 8, :, lo], mb[h // 8, h % 8, :, hi] = wvs[c2], wvs[c1]
            bks_rows[lo], bks_rows[hi] = bks[c1], bks[c2]
            bvs_rows[lo], bvs_rows[hi] = bvs[c2], bvs[c1]
    bk_rows = np.zeros((G, 4, 32), f)
    bk_rows[:, :, :HD] = np.asarray(L0_attn_bk).reshape(G, 4, HD)
    small = np.zeros((P, SMALL_W), f)
    for name, value in (
        ("bq", np.asarray(L0_attn_bq).reshape(2, P).T), ("bk", np.asarray(L0_attn_bk).reshape(2, P).T),
        ("bv", np.asarray(L0_attn_bv).reshape(2, P).T), ("bk_rows", bk_rows.reshape(G, P).T),
        ("bqs_rows", bqs_rows.reshape(P, 1)), ("bks_rows", bks_rows.reshape(P, 1)), ("bvs_rows", bvs_rows.reshape(P, 1)),
        ("temp", np.broadcast_to(np.asarray(L0_attn_temp), (P, 1))),
        ("b1", np.asarray(L0_ffn_b1).reshape(E, HC, P).transpose(2, 0, 1).reshape(P, E * HC)),
        ("wg", np.asarray(L0_ffn_Wg).reshape(DC, P, E).transpose(1, 0, 2).reshape(P, DC * E)),
    ):
        a, b = SMALL[name]
        small[:, a:b] = value
    arrays = {
        "patches": patches, "tok_wt": np.asarray(L0_tok_W).T, "tok_b": np.asarray(L0_tok_b),
        "pos3": np.concatenate([np.asarray(L0_tok_pos_embd)[0]] * EB), "txt": np.asarray(txt),
        "const": host_constants(), "sel": host_selection(), "small": small, "wq": wq, "wk": wk, "wv": wv,
        "wk_pad": wk_pad.reshape(D, 512), "wv_t": wv.T, "wo_t": wo.T, "wo_pad": wo_pad.reshape(512, D),
        "mq": mq.reshape(P, D), "ma": ma.reshape(2, P, P).transpose(1, 0, 2), "mb": mb.reshape(2, P, P).transpose(1, 0, 2),
        "bo": np.asarray(L0_attn_bo), "bg": np.asarray(L0_ffn_bg), "w1": np.asarray(L0_ffn_W1),
        "w2": np.asarray(L0_ffn_W2), "b2": np.asarray(L0_ffn_b2),
    }
    arrays = {k: np.ascontiguousarray(a) for k, a in arrays.items()}
    nc = bacc.Bacc("TRN2", target_bir_lowering=False, num_devices=1)
    args = {k: nc.dram_tensor(f"in_{k}", a.shape, mybir.dt.from_np(a.dtype), kind="ExternalInput").ap()
            for k, a in arrays.items()}
    out = nc.dram_tensor("out_0", (B, T, D), F32, kind="ExternalOutput").ap()
    program(nc, out=out, **args)
    r = run_bass_kernel_spmd(nc, [{f"in_{k}": a for k, a in arrays.items()}], core_ids=[0])
    return r.results[0]["out_0"]
```

```python
from contextlib import ExitStack

import numpy as np

import concourse.bass as bass
from concourse import mybir

F32 = mybir.dt.float32
F32R = mybir.dt.float32r
I32 = mybir.dt.int32
ACT = mybir.ActivationFunctionType
ALU = mybir.AluOpType
AX = mybir.AxisListType

B, NIMG, NTXT, D, H, HD = 8, 36, 128, 256, 16, 16
PATCH, CH, IMG = 16, 3, 96
PD = CH * PATCH * PATCH
T = NIMG + NTXT
C = T // 2
NBLK = 2 * B
NTOK = B * T
E, HID = 8, 1024
P = 128
SLOTS = 128
TILES = (NTOK - E) // SLOTS + E
G = 4
DC = D // P
KC = PD // P
HC = HID // P
EB = 3
ROW = D + 3
RING = 4
EPS = 1e-5

CONST = {}
LATE = {}
SMALL = {}


def _columns(table, *items):
    at = 0
    for name, width in items:
        table[name] = (at, at + width)
        at += width
    return at


CONST_W = _columns(CONST, ("ident", P), ("full", P))
LATE_W = _columns(LATE, ("before", P), ("iota", P), ("restart", P), ("tile_start", 32), ("tokid", NBLK),
                  ("backward", E))
SMALL_W = _columns(SMALL, ("bq", 2), ("bk", 2), ("bv", 2), ("bk_rows", G), ("bqs_rows", 1),
                   ("bks_rows", 1), ("bvs_rows", 1), ("temp", 1), ("b1", E * HC), ("wg", DC * E))


def host_constants():
    early, late = np.zeros((P, CONST_W), np.float32), np.zeros((P, LATE_W), np.float32)

    def put(name, value):
        table, c = (CONST, early) if name in CONST else (LATE, late)
        a, b = table[name]
        c[:value.shape[0], a:b] = value.reshape(value.shape[0], b - a)

    put("ident", np.eye(P, dtype=np.float32))
    put("before", np.triu(np.ones((P, P), np.float32), 1))
    put("iota", np.tile(np.arange(P, dtype=np.float32), (P, 1)))
    restart = np.ones((P, E, NBLK), np.float32)
    restart[:, :, 0] = 0.0
    put("restart", restart)
    put("tile_start", np.tile(SLOTS * np.arange(32, dtype=np.float32), (P, 1)))
    put("full", np.ones((P, P), np.float32))
    tok = C * np.arange(NBLK, dtype=np.float32)[None, :] + np.arange(P, dtype=np.float32)[:, None] - NTOK
    put("tokid", tok)
    put("backward", np.tile(E - np.arange(E, dtype=np.float32), (P, 1)))
    return early, late


def host_selection():
    sel = np.zeros((P, G, P), np.float32)
    for h in range(H):
        for k in range(3):
            row = 32 * (h % 4) + HD + k
            sel[3 * h + k, h // 4, row] = 1.0
            sel[64 + 3 * h + k, h // 4, row] = -1.0
    return sel


def program(nc, patches, tok_wt, tok_b, pos3, txt, const, late, small, sel, wq, wk, wv, wk_pad, wv_t, wo_t, wo_pad, mq, ma, mb,
            bo, bg, w1, w2, b2, out):
    rows_dram = nc.dram_tensor("rows_dram", [NTOK + 1, ROW], F32).ap()
    out_rows = out.rearrange("b t d -> (b t) d")

    with ExitStack() as ctx:
        def sb(name, shape, dt=F32, scope=ctx):
            return scope.enter_context(nc.sbuf_tensor(name, shape, dt))

        def sem(name):
            return ctx.enter_context(nc.semaphore(name))

        pair01 = ctx.enter_context(nc.psum_tensor("bank01", [P, 2, 512], F32))
        pair23 = ctx.enter_context(nc.psum_tensor("bank23", [P, 2, 512], F32))
        bank = [pair01[:, 0, :], pair01[:, 1, :], pair23[:, 0, :], pair23[:, 1, :]]
        bank += [ctx.enter_context(nc.psum_tensor(f"bank{i}", [P, 512], F32)) for i in range(4, 8)]

        Hs = sb("Hs", [C, NBLK, D])
        cst = sb("cst", [P, CONST_W])
        sml = sb("sml", [P, SMALL_W])
        stats = sb("stats", [C, NBLK, 6])
        mv = sb("mv", [C, NBLK, 2])
        stats2 = sb("stats2", [C, 2, 6])
        mv2 = sb("mv2", [C, 2, 2])
        lgraw = sb("lgraw", [C, NBLK, E])
        sd = sb("sd", [C, NBLK])
        rstd = sb("rstd", [C, NBLK])

        with ExitStack() as st:
            pat_s = sb("pat_s", [P, KC, B * NIMG], F32, st)
            tokw_s = sb("tokw_s", [P, KC, D], F32, st)
            pos_s = sb("pos_s", [EB * NIMG, D], F32, st)
            tokb_s = sb("tokb_s", [EB * NIMG, D], F32, st)
            emb = sb("emb", [EB * NIMG, 3, D], F32, st)
            wq_s = sb("wq_s", [P, 2, D], F32, st)
            wk_s = sb("wk_s", [P, 2, D], F32, st)
            wv_s = sb("wv_s", [P, 2, D], F32, st)
            wkp_s = sb("wkp_s", [P, DC, 512], F32, st)
            wvt_s = sb("wvt_s", [P, DC, D], F32, st)
            wot_s = sb("wot_s", [P, 2, D], F32, st)
            bv_cols = sb("bv_cols", [P, 2, C], F32, st)
            mq_s = sb("mq_s", [P, D], F32, st)
            ma_s = sb("ma_s", [P, 2, P], F32, st)
            mb_s = sb("mb_s", [P, 2, P], F32, st)
            bo_s = sb("bo_s", [C, D], F32, st)
            sel_s = sb("sel_s", [P, G, P], F32, st)
        W1s = sb("W1s", [P, E, DC, HID])

        with ExitStack() as at:
            wqh, wql = (sb(n, [P, DC, 512], F32R, at) for n in ("wqh", "wql"))
            wkh, wkl = (sb(n, [P, DC, 512], F32R, at) for n in ("wkh", "wkl"))
            wch, wcl = (sb(n, [P, DC, 2, P], F32R, at) for n in ("wch", "wcl"))
            wvh, wvl = (sb(n, [P, DC, D], F32R, at) for n in ("wvh", "wvl"))
            sel_r = sb("sel_r", [P, G, P], F32R, at)
            qh, ql = (sb(n, [P, G, T], F32R, at) for n in ("qh", "ql"))
            kh, kl = (sb(n, [P, G, T], F32R, at) for n in ("kh", "kl"))
            xth, xtl = (sb(n, [P, DC, T], F32R, at) for n in ("xth", "xtl"))
            prodh, prodl = (sb(n, [P, T], F32R, at) for n in ("prodh", "prodl"))
            wo_s = sb("wo_s", [P, G, D], F32, at)
            qbias = sb("qbias", [P, G], F32, at)
            cbias = sb("cbias", [P, 2], F32, at)
            obias = sb("obias", [C, D], F32, at)
            xhat = sb("xhat", [P, 2, D], F32, at)
            cross = sb("cross", [P, 2, T], F32, at)
            crossa, prod = cross[:, 0, :], cross[:, 1, :]
            hct = cross[:, :, :].rearrange("p c (x t) -> p (c x) t", x=2)
            qb = sb("qb", [P, 2, H // 2, T], F32R, at)
            kb = sb("kb", [P, 2, H // 2, 2, T], F32R, at)
            V = sb("V", [P, 2, 2, H, 32], F32, at)
            mx = sb("mx", [C, 8, 2, 2], F32, at)
            negmx = sb("negmx", [C, 8, 2, 2], F32, at)
            pr = sb("pr", [P, 4, 2, 2, T], F32, at)
            prt = sb("prt", [P, 4, 2, T], F32, at)
            den = sb("den", [P, T], F32, at)
            AO = sb("AO", [P, 2, G, T], F32, at)

        W2s = sb("W2s", [P, E, HC, D])
        late_s = sb("late_s", [P, LATE_W])
        bg_s = sb("bg_s", [C, E])
        b2_s = sb("b2_s", [P, E, D])
        lg = sb("lg", [C, NBLK, E])
        lgmax = sb("lgmax", [C, NBLK])
        ex = sb("ex", [C, NBLK, E])
        exsum = sb("exsum", [C, NBLK])
        hit = sb("hit", [C, NBLK, E])
        firsthit = sb("firsthit", [C, NBLK])
        onehot = sb("onehot", [C, E, NBLK])
        upto = sb("upto", [C, E, NBLK])
        earlier = sb("earlier", [C, E, NBLK])
        ntiles_cmp = sb("ntiles_cmp", [P, E, 11])
        ntiles = sb("ntiles", [P, E])
        tiles_upto = sb("tiles_upto", [P, E])
        base = sb("base", [P, E])
        posn = sb("posn", [C, E, NBLK])
        pos = sb("pos", [C, NBLK])
        tile_cmp = sb("tile_cmp", [C, NBLK, 17])
        tile_of = sb("tile_of", [C, NBLK])
        slot_of = sb("slot_of", [C, NBLK])
        slot_hot = sb("slot_hot", [C, NBLK, SLOTS], F32R)
        tile_hot = sb("tile_hot", [C, NBLK, TILES])
        tile_ids = sb("tile_ids", [C, NBLK, TILES], F32R)
        ids = sb("ids", [P, TILES], I32)
        et_cmp = sb("et_cmp", [1, TILES, E])
        et_f = sb("et_f", [1, TILES])
        et = sb("et", [1, TILES], I32)
        tab = sb("tab", [C, NBLK, 3])
        hrow = sb("hrow", [P, RING, ROW])
        xn = sb("xn", [P, D])
        xt = sb("xt", [P, DC, P])
        z = sb("z", [P, HID])
        b1c = sb("b1c", [P, HC])
        ht = sb("ht", [P, HC, P])
        y1 = sb("y1", [P, D])
        Y = sb("Y", [P, D])

        def con(name, rows=P):
            (a, b), held = (CONST[name], cst) if name in CONST else (LATE[name], late_s)
            return held[0:rows, a:b]

        def smal(name):
            a, b = SMALL[name]
            return sml[:, a:b]

        ident = con("ident")

        ld_pat, ld_const, ld_txt, ld_small, ld_fold, ld_split, ld_wo, ld_img = (sem(n) for n in (
            "ld_pat", "ld_const", "ld_txt", "ld_small", "ld_fold", "ld_split", "ld_wo", "ld_img"))
        ld_w1, ld_w2, ld_b2, ld_late, rows_out = (sem(n) for n in ("ld_w1", "ld_w2", "ld_b2", "ld_late", "rows_out"))
        pads_zero = sem("pads_zero")
        emb_ps, emb_done, posb_done = sem("emb_ps"), sem("emb_done"), sem("posb_done")
        fold_ps = sem("fold_ps")
        stats_done, aggr_done, sd_done, rstd_done = (sem(n) for n in ("stats_done", "aggr_done", "sd_done", "rstd_done"))
        parts_hi, parts_lo, parts_done = sem("parts_hi"), sem("parts_lo"), sem("parts_done")
        xhat_ok = sem("xhat_ok")
        xt_ps, xth_ok, xtl_ok = sem("xt_ps"), sem("xth_ok"), sem("xtl_ok")
        cr_ps, cra_ok, prod_ok, prodh_ok, prods_ok = (sem(n) for n in ("cr_ps", "cra_ok", "prod_ok", "prodh_ok", "prods_ok"))
        q_ps, qh_ok, ql_ok = sem("q_ps"), sem("qh_ok"), sem("ql_ok")
        k_ps, kh_ok, kl_ok = sem("k_ps"), sem("kh_ok"), sem("kl_ok")
        v_ps, v_ok = sem("v_ps"), sem("v_ok")
        kb_ok = [sem("kb_ok0"), sem("kb_ok1")]
        qb_ok = [[sem("qb_ok00"), sem("qb_ok01")], [sem("qb_ok10"), sem("qb_ok11")]]
        qg_ok = [sem("qg_ok0"), sem("qg_ok1")]
        s_ps, mx_ok, neg_ok, exp_ok = sem("s_ps"), sem("mx_ok"), sem("neg_ok"), sem("exp_ok")
        t_ps, prt_ok, pv_ps = sem("t_ps"), sem("prt_ok"), sem("pv_ps")
        den_ok, rden_ok, ao_ok = sem("den_ok"), sem("rden_ok"), sem("ao_ok")
        o_ps, hb_ok, h_ok = sem("o_ps"), sem("hb_ok"), sem("h_ok")
        dve_step, aggr1, v_zero, bv_spread = sem("dve_step"), sem("aggr1"), sem("v_zero"), sem("bv_spread")
        hot_ok, rank_ps, slots_hot, slots_ps, lgsub_ok, ex_ok = (sem(n) for n in (
            "hot_ok", "rank_ps", "slots_hot", "slots_ps", "lgsub_ok", "ex_ok"))
        st2_ok, mv2_ok, mv_ok, tab_ok = sem("st2_ok"), sem("mv2_ok"), sem("mv_ok"), sem("tab_ok")
        hc_ok, g_ps, g_ok, lg_ps, lg_ok = (sem(n) for n in ("hc_ok", "g_ps", "g_ok", "lg_ps", "lg_ok"))
        ids_ok, et_ok = sem("ids_ok"), sem("et_ok")
        rows_in, sc_out, xn_ok = [sem(f"rows_in{k}") for k in range(RING)], sem("sc_out"), sem("xn_ok")
        tx_ps, tx_ok, l1_ps, z_ok, zt_ps, silu_ok, b1_ok, l2_ps, y1_ok, y_ok = (sem(n) for n in (
            "tx_ps", "tx_ok", "l1_ps", "z_ok", "zt_ps", "silu_ok", "b1_ok", "l2_ps", "y1_ok", "y_ok"))

        EARLY_W2 = 5
        ROWS = 2 * B + 4
        PARTS = [(0, 80), (80, C)]

        def first(b):
            return isinstance(b, int) and b == 0

        def few(b):
            return isinstance(b, int) and b < 2

        FIRST_ORDER = (0, 1, 2, 3, 4, 6, 7)

        def piece_bank(pb, piece_):
            alone = {"x": 0, "cross": 1, "q0": 2, "q1": 3, "k0": 4, "k1": 5, "v": 7}
            shared = {"x": 6, "cross": 7, "q0": 6, "k0": 7, "k1": 6, "q1": 6, "v": 7}
            return bank[(alone if first(pb) else shared)[piece_]]

        HR = 20
        COPIES = 12

        def stacked(b, u, copies=COPIES):
            return 8 * copies * (b - u) + 16 * copies

        def wait_q_stack(eng, b, u, half):
            if half == 0:
                eng.wait_ge(qb_ok[0][u], stacked(b, u, COPIES // 2))
                eng.wait_ge(qg_ok[u], stacked(b, u, COPIES // 2))
            else:
                eng.wait_ge(qb_ok[1][u], stacked(b, u))

        def stack_q(queue, pb, u, half, quadrants=range(4)):
            done = qg_ok[u] if quadrants is BY_POOL else qb_ok[half][u]
            for j in quadrants:
                for part, src in enumerate((qh, ql, qh)):
                    row = 64 * (j % 2) + HR * part
                    queue.dma_start(qb[row:row + HR, u, 4 * half + j // 2:4 * half + 4:2, :].bitcast(F32),
                                    src[32 * j:32 * j + HR, 2 * half:2 * half + 2, :].bitcast(F32)
                                    ).then_inc(done, 16)

        BY_SP, BY_POOL = (0, 1), (2, 3)

        block = ctx.enter_context(nc.Block())

        @block.sync
        def _(sp):
            sp.dma_start(pat_s[:, :, :], patches.rearrange("(k p) n -> p k n", p=P)).then_inc(ld_pat, 16)
            sp.dma_start(tokw_s[:, :, :], tok_wt.rearrange("(k p) e -> p k e", p=P)).then_inc(ld_pat, 16)
            sp.dma_start(pos_s[:, :], pos3).then_inc(ld_pat, 16)
            sp.dma_start(tokb_s[:, :], tok_b.partition_broadcast(EB * NIMG)).then_inc(ld_pat, 16)
            for a, b in ((NIMG, 68), (68, C)):
                sp.dma_start(Hs[a:b, 0:NBLK:2, :],
                             txt[:, a - NIMG:b - NIMG, :].rearrange("b p d -> p b d")).then_inc(ld_txt, 16)
            for a, b in PARTS:
                sp.dma_start(Hs[a:b, 1:NBLK:2, :],
                             txt[:, C - NIMG + a:C - NIMG + b, :].rearrange("b p d -> p b d")).then_inc(ld_txt, 16)
            sp.dma_start(cst[:, :], const).then_inc(ld_const, 16)
            sp.dma_start(sml[:, :], small).then_inc(ld_small, 16)
            for dst, src in ((wk_s, wk), (wv_s, wv)):
                sp.dma_start(dst[:, :, :], src.rearrange("(k p) e -> p k e", p=P)).then_inc(ld_fold, 16)
            sp.dma_start(ma_s[:, :, :], ma).then_inc(ld_fold, 16)
            sp.dma_start(mb_s[:, :, :], mb).then_inc(ld_fold, 16)
            sp.dma_start(wq_s[:, :, :], wq.rearrange("(k p) e -> p k e", p=P)).then_inc(ld_fold, 16)
            sp.dma_start(mq_s[:, :], mq).then_inc(ld_fold, 16)
            for dst, src in ((wkp_s, wk_pad), (wvt_s, wv_t)):
                sp.dma_start(dst[:, :, :], src.rearrange("(k p) e -> p k e", p=P)).then_inc(ld_split, 16)
            sp.dma_start(sel_s[:, :, :], sel).then_inc(ld_split, 16)
            for dst, src in ((wot_s, wo_t), (wo_s, wo_pad)):
                sp.dma_start(dst[:, :, :], src.rearrange("(k p) e -> p k e", p=P)).then_inc(ld_wo, 16)
            sp.dma_start(bo_s[:, :], bo.partition_broadcast(C)).then_inc(ld_wo, 16)
            for b in range(B):
                m, k = b // EB, b % EB
                if k == 0:
                    sp.wait_ge(emb_done, m + 1)
                sp.dma_start(Hs[0:NIMG, 2 * b, :], emb[NIMG * k:NIMG * (k + 1), m, :]).then_inc(ld_img, 16)

            def stack_k(pb, u):
                for src, ready, parts in ((kh, kh_ok, (0, 1)), (kl, kl_ok, (2,))):
                    sp.wait_ge(ready, 2 * pb + 2)
                    for j in range(4):
                        for part in parts:
                            row = 64 * (j % 2) + HR * part
                            sp.dma_start(kb[row:row + HR, u, j // 2:H // 2:2, j % 2, :].bitcast(F32),
                                         src[32 * j:32 * j + HR, :, :].bitcast(F32)).then_inc(kb_ok[u], 16)

            sp.wait_ge(pads_zero, 1)
            for pb in range(2):
                sp.wait_ge(ql_ok, 2 * pb + 1)
                stack_q(sp, pb, pb, 0, BY_SP)
                stack_k(pb, pb)
                sp.wait_ge(ql_ok, 2 * pb + 2)
                stack_q(sp, pb, pb, 1)
            w1_rows = w1.rearrange("e (k p) n -> e p k n", p=P)
            sp.wait_ge(ld_img, 16 * B)
            for e in range(2):
                sp.dma_start(W1s[:, e, :, :], w1_rows[e]).then_inc(ld_w1, 16)
            def write_rows(ob):
                sp.wait_ge(h_ok, ob + 1)
                dst = rows_dram[bass.ds(T * ob, T), 0:D].rearrange("(c p) d -> p c d", p=C)
                for a, b in PARTS:
                    sp.dma_start(dst[a:b], Hs[a:b, bass.ds(2 * ob, 2), :]).then_inc(rows_out, 16)

            with sp.Fori(0, (B - 2) // 2) as i:
                for u in range(2):
                    sp.wait_ge(ql_ok, 2 * (2 * i + 2 + u) + 1)
                    stack_q(sp, 2 * i + 2 + u, u, 0, BY_SP)
                    stack_k(2 * i + 2 + u, u)
                    sp.dma_start(W1s[:, bass.ds(2 * i + 2 + u, 1), :, :],
                                 w1_rows[bass.ds(2 * i + 2 + u, 1)].rearrange("e p k n -> p e k n")).then_inc(ld_w1, 16)
                    write_rows(2 * i + u)
                    sp.wait_ge(ql_ok, 2 * (2 * i + 2 + u) + 2)
                    stack_q(sp, 2 * i + 2 + u, u, 1)

            def load_w2(e):
                sp.dma_start(W2s[:, e, :, :], w2[e].rearrange("(k p) n -> p k n", p=P)).then_inc(ld_w2, 16)

            sp.wait_ge(v_ok, B)
            sp.wait_ge(kb_ok[1], stacked(B - 1, 1))
            for half in range(2):
                wait_q_stack(sp, B - 1, 1, half)
            for e in range(EARLY_W2):
                load_w2(e)
            write_rows(B - 2)
            sp.dma_start(rows_dram[NTOK:NTOK + 1, 0:D], Hs[0:1, 0, :]).then_inc(rows_out, 16)
            sp.dma_start(rows_dram[NTOK:NTOK + 1, D:ROW], Hs[0:1, 0, 0:ROW - D]).then_inc(rows_out, 16)
            sp.wait_ge(o_ps, B)
            sp.dma_start(late_s[:, :], late).then_inc(ld_late, 16)
            sp.dma_start(bg_s[:, :], bg.partition_broadcast(C)).then_inc(ld_late, 16)
            write_rows(B - 1)
            sp.dma_start(b2_s[:, :, :], b2.partition_broadcast(P)).then_inc(ld_b2, 16)
            sp.wait_ge(lg_ps, B)
            load_w2(EARLY_W2)
            sp.wait_ge(tab_ok, 1)
            dst = rows_dram[0:NTOK, D:ROW].rearrange("(b p) w -> p b w", p=C)
            for a, b in PARTS:
                sp.dma_start(dst[a:b], tab[a:b, :, :]).then_inc(rows_out, 16)
            for e in range(EARLY_W2 + 1, E):
                load_w2(e)

        @block.tensor
        def _(pe):
            mm = nc.tensor.matmul
            pe.wait_ge(ld_pat, 64)
            for m in range(3):
                rows = min(EB, B - EB * m) * NIMG
                for k in range(KC):
                    last = mm(bank[m][0:rows, 0:D], pat_s[:, k, EB * NIMG * m:EB * NIMG * m + rows], tokw_s[:, k, :],
                              start=(k == 0), stop=(k == KC - 1))
                last.then_inc(emb_ps, 1)
            pe.wait_ge(ld_fold, 16 * 6)
            pe.wait_ge(ld_small, 16)
            for d in range(DC):
                for x, (w, m_) in enumerate(((wk_s, ma_s), (wv_s, mb_s))):
                    for i in range(2):
                        last = mm(bank[5][:, 256 * d + P * x:256 * d + P * x + P], w[:, i, P * d:P * d + P], m_[:, i, :],
                                  start=(i == 0), stop=(i == 1))
            last.then_inc(fold_ps, 1)
            for d in range(DC):
                for i in range(2):
                    last = mm(bank[3 + d][:, D * i:D * i + D], wq_s[:, i, P * d:P * d + P], mq_s[:, :], start=True, stop=True)
            last.then_inc(fold_ps, 1)
            for g in range(G):
                mm(bank[6][:, g:g + 1], mq_s[:, P * (g % 2):P * (g % 2) + P], smal("bq")[:, g // 2:g // 2 + 1],
                   start=True, stop=True)
            for x, (m_, b_) in enumerate(((ma_s, "bk"), (mb_s, "bv"))):
                for i in range(2):
                    mm(bank[6][:, 4 + x:5 + x], m_[:, i, :], smal(b_)[:, i:i + 1], start=(i == 0), stop=(i == 1))
            pe.wait_ge(bv_spread, 1)
            pe.wait_ge(ld_wo, 48)
            for i in range(2):
                last = mm(bank[7][0:C, 0:D], bv_cols[:, i, :], wot_s[:, i, :], start=(i == 0), stop=(i == 1))
            last.then_inc(fold_ps, 1)

            def passes(out_ap, w_hi, w_lo, x_hi, x_lo, more=False):
                terms = [(w, x, d) for w, x in ((w_hi, x_hi), (w_lo, x_hi), (w_hi, x_lo)) for d in range(DC)]
                for n, (w, x, d) in enumerate(terms):
                    last = mm(out_ap, w(d), x(d), start=(n == 0), stop=(not more and n == len(terms) - 1))
                return last

            def turn_x(pb):
                pe.wait_ge(xhat_ok, pb + 1)
                for c in range(2):
                    for d in range(DC):
                        last = nc.tensor.transpose(piece_bank(pb, "x")[:, P * (2 * d + c):P * (2 * d + c) + P],
                                                   xhat[:, c, P * d:P * d + P], ident)
                last.then_inc(xt_ps, 1)

            def cross_operands(pb):
                pe.wait_ge(xtl_ok, pb + 1)
                if not first(pb):
                    pe.wait_ge(v_ok, pb)
                for x in range(2):
                    last = passes(piece_bank(pb, "cross")[:, T * x:T * x + T], lambda d: wch[:, d, x, :], lambda d: wcl[:, d, x, :],
                                  lambda d: xth[:, d, :], lambda d: xtl[:, d, :])
                last.then_inc(cr_ps, 1)

            def out_group(g, u):
                pe.wait_ge(ao_ok, G * (B - 1) + g + 1)
                for c in range(2):
                    last = mm(bank[7 - c][0:C, 0:D], AO[:, u, g, C * c:C * c + C], wo_s[:, g, :],
                              start=(g == 0), stop=(g == G - 1))
                return last

            def out_projection(ob, u):
                if isinstance(ob, int) and ob == B - 2:
                    pe.wait_ge(v_ok, B)
                else:
                    pe.wait_ge(kl_ok, 2 * ob + 5)
                pe.wait_ge(ao_ok, G * ob + G)
                for c in range(2):
                    for g in range(G):
                        last = mm(bank[7][0:C, D * c:D * c + D], AO[:, u, g, C * c:C * c + C], wo_s[:, g, :],
                                  start=(g == 0), stop=(g == G - 1))
                last.then_inc(o_ps, 1)

            def turn_rows(ob):
                pe.wait_ge(hc_ok, ob + 1)
                if isinstance(ob, int) and ob == B - 1:
                    pe.wait_ge(ao_ok, G * B)
                else:
                    pe.wait_ge(ao_ok, G * ob + G + 2)
                for x in range(2):
                    for d in range(DC):
                        n = P * (2 * x + d)
                        last = nc.tensor.transpose(bank[5][:, n:n + P], xhat[:, x, P * d:P * d + P], ident)
                last.then_inc(g_ps, 1)

            def gate(ob):
                pe.wait_ge(g_ok, ob + 1)
                for x in range(2):
                    for d in range(DC):
                        last = mm(bank[5][0:C, E * x:E * x + E], hct[:, 2 * x + d, :], smal("wg")[:, E * d:E * d + E],
                                  start=(d == 0), stop=(d == DC - 1))
                last.then_inc(lg_ps, 1)

            def q_groups(pb, half):
                if half == 1 and not first(pb):
                    pe.wait_ge(kl_ok, 2 * pb + 2)
                for x in range(2):
                    g = 2 * half + x
                    last = passes(piece_bank(pb, f"q{half}")[:, T * x:T * x + T], lambda d: wqh[:, d, P * g:P * g + P],
                                  lambda d: wql[:, d, P * g:P * g + P], lambda d: xth[:, d, :], lambda d: xtl[:, d, :])
                last.then_inc(q_ps, 1)

            def k_groups(pb, half):
                if half == 1 and not first(pb):
                    pe.wait_ge(ql_ok, 2 * pb + 1)
                if half == 0:
                    pe.wait_ge(prods_ok, pb + 1)
                for x in range(2):
                    g = 2 * half + x
                    o = piece_bank(pb, f"k{half}")[:, T * x:T * x + T]
                    passes(o, lambda d: wkh[:, d, P * g:P * g + P], lambda d: wkl[:, d, P * g:P * g + P],
                           lambda d: xth[:, d, :], lambda d: xtl[:, d, :], more=True)
                    mm(o, sel_r[:, g, :], prodh[:, :], start=False, stop=False)
                    last = mm(o, sel_r[:, g, :], prodl[:, :], start=False, stop=True)
                last.then_inc(k_ps, 1)

            def v_rows(pb):
                if not few(pb):
                    pe.wait_ge(h_ok, pb - 1)
                for c in range(2):
                    last = passes(piece_bank(pb, "v")[0:C, D * c:D * c + D], lambda d: xth[:, d, C * c:C * c + C],
                                  lambda d: xtl[:, d, C * c:C * c + C], lambda d: wvh[:, d, :], lambda d: wvl[:, d, :])
                last.then_inc(v_ps, 1)

            def piece(k, pb, u):
                if k == 0:
                    turn_x(pb)
                elif k == 1:
                    cross_operands(pb)
                elif k == 2:
                    q_groups(pb, 0)
                elif k in (3, 4):
                    k_groups(pb, k - 3)
                elif k == 5:
                    if not few(pb):
                        out_projection(pb - 2, u)
                elif k == 6:
                    q_groups(pb, 1)
                else:
                    v_rows(pb)

            def scores(b, u, p):
                if p == 0:
                    pe.wait_ge(kb_ok[u], stacked(b, u))
                if p % 4 == 0:
                    wait_q_stack(pe, b, u, p // 4)
                for c in range(2):
                    if not (isinstance(b, int) and b == 0 and p == 0):
                        pe.wait_ge(exp_ok, 16 * b + 2 * p + c - 1)
                    mm(bank[c][0:C, 0:2 * T], qb[:, u, p, C * c:C * c + C], kb[:, u, p, :, :],
                       start=True, stop=True).then_inc(s_ps, 1)

            def turn_probs(b, p):
                pe.wait_ge(exp_ok, 16 * b + 2 * p + 2)
                if not (isinstance(b, int) and b == 0 and p == 0):
                    pe.wait_ge(prt_ok, 8 * b + p)
                for x in range(2):
                    for k in range(2):
                        for c in range(2):
                            at_ = P * (2 * k + c)
                            last = nc.tensor.transpose(bank[2 + x][0:C, at_:at_ + P],
                                                       pr[:, p % 4, c, x, C * k:C * k + C], ident)
                last.then_inc(t_ps, 1)

            def weigh_values(b, u, p):
                g = p // 2
                if p == 0:
                    pe.wait_ge(v_ok, b + 1)
                if p % 2 == 0 and not (isinstance(b, int) and b == 0 and g < 2):
                    pe.wait_ge(ao_ok, G * b + g - 1)
                if p == 6 and isinstance(b, int) and b >= B - 2:
                    pe.wait_ge(lg_ok, b)
                pe.wait_ge(prt_ok, 8 * b + p + 1)
                for h in (2 * p, 2 * p + 1):
                    j = h % 4
                    for k in range(2):
                        last = mm(bank[4 + g % 2][32 * j:32 * j + 32, 0:T], V[:, u, k, h, :], prt[:, h % 4, k, :],
                                  start=(k == 0), stop=(k == 1))
                last.then_inc(pv_ps, 1)

            def batch(b, u, project=True):
                for s in range(8):
                    tb, tu, tp = (b, u, s - 2) if s >= 2 else (b - 1, 1 - u, s + 6)
                    if s >= 2 or not first(b):
                        turn_probs(tb, tp)
                    scores(b, u, s)
                    if project:
                        piece(s, b + 1, 1 - u)
                    elif s == 5:
                        out_projection(b - 1, 1 - u)
                    if s == 7 and not first(b):
                        turn_rows(b - 1)
                    if s >= 2 or not first(b):
                        weigh_values(tb, tu, tp)
                    if s == 7 and not first(b):
                        gate(b - 1)

            pe.wait_ge(parts_done, 1)
            pe.wait_ge(pads_zero, 1)
            pe.wait_ge(parts_lo, 1)
            for k in FIRST_ORDER:
                piece(k, 0, 0)
            batch(0, 0)
            with pe.Fori(0, (B - 2) // 2) as i:
                batch(2 * i + 1, 1)
                batch(2 * i + 2, 0)
            batch(B - 1, 1, project=False)
            turn_probs(B - 1, 6)
            pe.wait_ge(h_ok, B - 1)
            pe.wait_ge(ql_ok, 2 * B)
            out_group(0, 1)
            out_group(1, 1)
            weigh_values(B - 1, 1, 6)
            turn_probs(B - 1, 7)
            out_group(2, 1)
            weigh_values(B - 1, 1, 7)
            out_group(3, 1).then_inc(o_ps, 1)
            turn_rows(B - 1)
            gate(B - 1)

            pe.wait_ge(hot_ok, 1)
            mm(bank[3][0:C, 0:E * NBLK], con("before", C)[:, 0:C], onehot[:, :, :], start=True, stop=False)
            mm(bank[3][0:C, 0:E * NBLK], con("full", C)[:, 0:C], earlier[:, :, :], start=False, stop=True)
            mm(bank[4][:, 0:E], con("full", C), upto[:, :, NBLK - 1], start=True, stop=True).then_inc(rank_ps, 1)
            for blk in range(NBLK):
                if blk % 4 == 0:
                    pe.wait_ge(slots_hot, blk // 4 + 1)
                last = mm(bank[5][:, 0:TILES], slot_hot[:, blk, :], tile_ids[:, blk, :],
                          start=(blk == 0), stop=(blk == NBLK - 1))
            last.then_inc(slots_ps, 1)

            def turn_tile(t):
                pe.wait_ge(xn_ok, t + 1)
                for d in range(DC):
                    last = nc.tensor.transpose(bank[6][:, P * d:P * d + P], xn[:, P * d:P * d + P], ident)
                last.then_inc(tx_ps, 1)

            def first_product(t, e):
                pe.wait_ge(tx_ok, t + 1)
                for n in range(2):
                    for d in range(DC):
                        last = mm(bank[n][:, :], xt[:, d, :], W1s[:, bass.ds(e, 1), d, 512 * n:512 * n + 512],
                                  start=(d == 0), stop=(d == DC - 1))
                    last.then_inc(l1_ps, 1)

            def turn_hidden(t):
                pe.wait_ge(z_ok, 2 * t + 2)
                for k in range(HC):
                    last = nc.tensor.transpose(bank[2 + k // 4][:, P * (k % 4):P * (k % 4) + P], z[:, P * k:P * k + P], ident)
                    if k % 4 == 3:
                        last.then_inc(zt_ps, 1)

            def second_product(t, e):
                pe.wait_ge(silu_ok, HC * t + HC)
                if not first(t):
                    pe.wait_ge(y1_ok, t)
                for k in range(HC):
                    last = mm(bank[4][:, 0:D], ht[:, k, :], W2s[:, bass.ds(e, 1), k, :], start=(k == 0), stop=(k == HC - 1))
                last.then_inc(l2_ps, 1)

            def expert(t):
                return pe.value_load(et[0:1, bass.ds(t, 1)], min_val=0, max_val=E - 1)

            pe.wait_ge(et_ok, 1)
            turn_tile(0)
            pe.wait_ge(ld_w1, 16 * E)
            first_product(0, expert(0))
            turn_tile(1)
            pe.wait_ge(ld_w2, 16 * E)
            with pe.Fori(1, TILES - 1) as t:
                turn_hidden(t - 1)
                first_product(t, expert(t))
                turn_tile(t + 1)
                second_product(t - 1, expert(t - 1))
            turn_hidden(TILES - 2)
            first_product(TILES - 1, expert(TILES - 1))
            second_product(TILES - 2, expert(TILES - 2))
            turn_hidden(TILES - 1)
            second_product(TILES - 1, expert(TILES - 1))

        @block.scalar
        def _(act):
            fn = nc.scalar.activation
            act.wait_ge(ld_split, 48)
            fn(wkh[:, :, :], wkp_s[:, :, :], ACT.Copy)
            fn(wvh[:, :, :], wvt_s[:, :, :], ACT.Copy)
            fn(sel_r[:, :, :], sel_s[:, :, :], ACT.Copy).then_inc(parts_hi, 1)
            act.wait_ge(fold_ps, 1)
            act.wait_ge(ld_small, 16)
            fn(wch[:, :, :, :], bank[5][:, :].rearrange("p (d x n) -> p d x n", d=DC, x=2), ACT.Copy).then_inc(parts_hi, 1)
            act.wait_ge(fold_ps, 2)
            for d in range(DC):
                last = fn(wqh[:, d, :], bank[3 + d][:, :], ACT.Copy, scale=smal("temp"))
            last.then_inc(parts_hi, 1)
            act.wait_ge(aggr_done, 1)
            fn(sd[:, :], mv[:, :, 1], ACT.Sqrt).then_inc(sd_done, 1)

            def high_x(pb):
                act.wait_ge(xt_ps, pb + 1)
                fn(xth[:, :, :].rearrange("p d (c t) -> p (d c) t", c=2),
                   piece_bank(pb, "x")[:, :].rearrange("p (n t) -> p n t", t=P)[:, :, 0:C], ACT.Copy).then_inc(xth_ok, 1)

            def cross_a(pb):
                act.wait_ge(cr_ps, pb + 1)
                fn(crossa, piece_bank(pb, "cross")[:, 0:T], ACT.Identity, bias=cbias[:, 0:1]).then_inc(cra_ok, 1)

            def high_q(pb, u, half):
                if not first(pb):
                    wait_q_stack(act, pb - 1, 1 - u, half)
                act.wait_ge(q_ps, 2 * pb + half + 1)
                for x in range(2):
                    g = 2 * half + x
                    last = fn(qh[:, g, :], piece_bank(pb, f"q{half}")[:, T * x:T * x + T], ACT.Identity, bias=qbias[:, g:g + 1])
                last.then_inc(qh_ok, 1)

            def high_k(pb, u, half):
                if half == 0 and not first(pb):
                    act.wait_ge(kb_ok[1 - u], stacked(pb - 1, 1 - u))
                act.wait_ge(k_ps, 2 * pb + half + 1)
                for x in range(2):
                    g = 2 * half + x
                    last = fn(kh[:, g, :], piece_bank(pb, f"k{half}")[:, T * x:T * x + T], ACT.Identity,
                              bias=smal("bk_rows")[:, g:g + 1])
                last.then_inc(kh_ok, 1)

            def values(pb, u):
                act.wait_ge(v_ps, pb + 1)
                fn(V[0:C, u, :, :, 0:HD], piece_bank(pb, "v")[0:C, :].rearrange("p (k h f) -> p k h f", k=2, h=H),
                   ACT.Copy).then_inc(v_ok, 1)

            def piece(k, pb, u):
                if k == 0:
                    high_x(pb)
                elif k == 1:
                    cross_a(pb)
                elif k in (2, 6):
                    high_q(pb, u, k // 4)
                elif k in (3, 4):
                    high_k(pb, u, k - 3)
                elif k == 7:
                    values(pb, u)

            def copy_rows(ob):
                act.wait_ge(g_ps, ob + 1)
                fn(hct, bank[5][:, :].rearrange("p (n t) -> p n t", t=P)[:, :, 0:C], ACT.Copy).then_inc(g_ok, 1)

            def copy_turned(b, p):
                act.wait_ge(t_ps, 8 * b + p + 1)
                if not (isinstance(b, int) and b == 0 and p < 2):
                    act.wait_ge(pv_ps, 8 * b + p - 1)
                r = 2 * (p % 2)
                fn(prt[0:C, r:r + 2, :, :].rearrange("p h k (c t) -> p h (k c) t", c=2),
                   pair23[0:C, :, :].rearrange("p h (n t) -> p h n t", t=P)[:, :, :, 0:C], ACT.Copy).then_inc(prt_ok, 1)

            def exps(b, p):
                for c in range(2):
                    act.wait_ge(neg_ok, 16 * b + 2 * p + c + 1)
                    if c == 0 and not (isinstance(b, int) and b == 0 and p < 4):
                        act.wait_ge(t_ps, 8 * b + p - 3)
                    for x in range(2):
                        last = fn(pr[0:C, p % 4, c, x, :], bank[c][0:C, T * x:T * x + T], ACT.Exp,
                                  bias=negmx[:, p, c, x:x + 1])
                    last.then_inc(exp_ok, 1)

            def batch(b, u, project=True):
                for s in range(8):
                    if s >= 2:
                        copy_turned(b, s - 2)
                    elif not first(b):
                        copy_turned(b - 1, s + 6)
                    if s == 7 and not first(b):
                        copy_rows(b - 1)
                    exps(b, s)
                    if project:
                        piece(s, b + 1, 1 - u)

            act.wait_ge(parts_done, 1)
            act.wait_ge(pads_zero, 1)
            for k in FIRST_ORDER:
                piece(k, 0, 0)
            batch(0, 0)
            with act.Fori(0, (B - 2) // 2) as i:
                batch(2 * i + 1, 1)
                batch(2 * i + 2, 0)
            batch(B - 1, 1, project=False)
            for p in (6, 7):
                copy_turned(B - 1, p)

            act.wait_ge(mv_ok, B - 1)
            fn(sd[:, 0:NBLK - 2], mv[:, 0:NBLK - 2, 1], ACT.Sqrt)
            copy_rows(B - 1)
            act.wait_ge(mv_ok, B)
            fn(sd[:, NBLK - 2:NBLK], mv[:, NBLK - 2:NBLK, 1], ACT.Sqrt).then_inc(sd_done, 1)
            act.wait_ge(lgsub_ok, 1)
            fn(ex[:, :, :], ex[:, :, :], ACT.Exp).then_inc(ex_ok, 1)

            def copy_tile(t):
                act.wait_ge(tx_ps, t + 1)
                if not first(t):
                    act.wait_ge(l1_ps, 2 * t)
                fn(xt[:, :, :], bank[6][:, 0:D].rearrange("p (d t) -> p d t", t=P), ACT.Copy).then_inc(tx_ok, 1)

            def silu(t):
                act.wait_ge(b1_ok, t + 1)
                for k in range(HC):
                    if k % 4 == 0:
                        act.wait_ge(zt_ps, 2 * t + k // 4 + 1)
                    fn(ht[:, k, :], bank[2 + k // 4][:, P * (k % 4):P * (k % 4) + P], ACT.Silu,
                       bias=b1c[:, k:k + 1]).then_inc(silu_ok, 1)

            copy_tile(0)
            copy_tile(1)
            with act.Fori(1, TILES - 1) as t:
                silu(t - 1)
                copy_tile(t + 1)
            silu(TILES - 2)
            silu(TILES - 1)

        @block.vector
        def _(dve):
            v = nc.vector
            dve.wait_ge(ld_pat, 64)
            v.tensor_tensor(pos_s[:, :], pos_s[:, :], tokb_s[:, :], ALU.add).then_inc(posb_done, 1)
            dve.wait_ge(ld_txt, 64)
            for blk in range(1, NBLK, 2):
                v.bn_stats(stats[:, blk, :], Hs[:, blk, :])
            dve.wait_ge(ld_const, 16)
            dve.wait_ge(ld_small, 16)
            for i in range(2):
                last = v.tensor_scalar(bv_cols[:, i, :], con("full")[:, 0:C], smal("bv")[:, i:i + 1], None, ALU.mult)
            last.then_inc(bv_spread, 1)
            dve.wait_ge(posb_done, 1)
            for m in range(3):
                rows = min(EB, B - EB * m) * NIMG
                dve.wait_ge(emb_ps, m + 1)
                v.tensor_tensor(emb[0:rows, m, :], bank[m][0:rows, 0:D], pos_s[0:rows, :], ALU.add).then_inc(emb_done, 1)
            dve.wait_ge(ld_img, 16 * B)
            for blk in range(0, NBLK, 2):
                last = v.bn_stats(stats[:, blk, :], Hs[:, blk, :])
            last.then_inc(stats_done, 1)
            dve.wait_ge(stats_done, 1)
            for blk in range(NBLK):
                last = v.bn_aggr(mv[:, blk, :], stats[:, blk, :])
            last.then_inc(aggr1, 1)
            dve.wait_ge(aggr1, 1)
            v.tensor_scalar(mv[:, :, 1], mv[:, :, 1], EPS, None, ALU.add).then_inc(aggr_done, 1)
            temp = smal("temp")
            dve.wait_ge(parts_hi, 2)
            v.tensor_tensor(wcl[:, :, :, :], bank[5][:, :].rearrange("p (d x n) -> p d x n", d=DC, x=2),
                            wch[:, :, :, :].bitcast(F32), ALU.subtract)
            dve.wait_ge(parts_hi, 3)
            for d in range(DC):
                v.scalar_tensor_tensor(wql[:, d, :], bank[3 + d][:, :], temp, wqh[:, d, :].bitcast(F32), ALU.mult, ALU.subtract)
            dve.wait_ge(fold_ps, 3)
            v.tensor_scalar(qbias[:, :], bank[6][:, 0:G], smal("bqs_rows"), temp, ALU.add, ALU.mult)
            v.tensor_tensor(cbias[:, 0:1], bank[6][:, 4:5], smal("bks_rows"), ALU.add)
            v.tensor_tensor(cbias[:, 1:2], bank[6][:, 5:6], smal("bvs_rows"), ALU.add)
            v.tensor_tensor(obias[:, :], bank[7][0:C, 0:D], bo_s[:, :], ALU.add).then_inc(parts_done, 1)
            dve.wait_ge(sd_done, 1)
            v.reciprocal(rstd[:, :], sd[:, :]).then_inc(rstd_done, 1)
            dve.wait_ge(rstd_done, 1)
            dve.wait_ge(parts_done, 1)

            def normed(pb):
                if not first(pb):
                    dve.wait_ge(xt_ps, pb)
                for c in range(2):
                    blk = 2 * pb + c
                    last = v.tensor_scalar(xhat[0:C, c:c + 1, :], Hs[:, bass.ds(blk, 1), :], mv[:, bass.ds(blk, 1), 0],
                                           rstd[:, bass.ds(blk, 1)], ALU.subtract, ALU.mult)
                last.then_inc(xhat_ok, 1)

            def low_x(pb):
                dve.wait_ge(xth_ok, pb + 1)
                v.tensor_tensor(xtl[:, :, :].rearrange("p d (c t) -> p (d c) t", c=2),
                                piece_bank(pb, "x")[:, :].rearrange("p (n t) -> p n t", t=P)[:, :, 0:C],
                                xth[:, :, :].bitcast(F32).rearrange("p d (c t) -> p (d c) t", c=2),
                                ALU.subtract).then_inc(xtl_ok, 1)

            def cross_products(pb):
                dve.wait_ge(cra_ok, pb + 1)
                v.scalar_tensor_tensor(prod, piece_bank(pb, "cross")[:, T:2 * T], cbias[:, 1:2], crossa,
                                       ALU.add, ALU.mult).then_inc(prod_ok, 1)

            def low_q(pb, u, half):
                if not first(pb):
                    wait_q_stack(dve, pb - 1, 1 - u, half)
                dve.wait_ge(qh_ok, 2 * pb + half + 1)
                for x in range(2):
                    g = 2 * half + x
                    last = v.scalar_tensor_tensor(ql[:, g, :], piece_bank(pb, f"q{half}")[:, T * x:T * x + T], qbias[:, g:g + 1],
                                                  qh[:, g, :].bitcast(F32), ALU.add, ALU.subtract)
                last.then_inc(ql_ok, 1)

            def low_k(pb, u, half):
                if half == 0 and not first(pb):
                    dve.wait_ge(kb_ok[1 - u], stacked(pb - 1, 1 - u))
                dve.wait_ge(kh_ok, 2 * pb + half + 1)
                for x in range(2):
                    g = 2 * half + x
                    last = v.scalar_tensor_tensor(kl[:, g, :], piece_bank(pb, f"k{half}")[:, T * x:T * x + T],
                                                  smal("bk_rows")[:, g:g + 1], kh[:, g, :].bitcast(F32),
                                                  ALU.add, ALU.subtract)
                last.then_inc(kl_ok, 1)

            def add_out(ob):
                dve.wait_ge(hb_ok, ob + 1)
                dve.wait_ge(o_ps, ob + 1)
                if isinstance(ob, int) and ob == B - 1:
                    for c in range(2):
                        rows = Hs[:, 2 * ob + c, :]
                        last = v.tensor_tensor(rows, bank[7 - c][0:C, 0:D], rows, ALU.add)
                    last.then_inc(h_ok, 1)
                    return
                rows = Hs[:, bass.ds(2 * ob, 2), :]
                v.tensor_tensor(rows, bank[7][0:C, :].rearrange("p (c d) -> p c d", c=2), rows, ALU.add).then_inc(h_ok, 1)

            def moments(ob):
                for c in range(2):
                    last = v.bn_stats(stats2[:, c:c + 1, :], Hs[:, bass.ds(2 * ob + c, 1), :])
                last.then_inc(st2_ok, 1)

            def centre(ob):
                for c in range(2):
                    last = v.bn_aggr(mv2[:, c, :], stats2[:, c, :])
                last.then_inc(mv2_ok, 1)
                dve.wait_ge(mv2_ok, ob + 1)
                for c in range(2):
                    last = v.tensor_scalar(xhat[0:C, c:c + 1, :], Hs[:, bass.ds(2 * ob + c, 1), :], mv2[:, c, 0:1],
                                           None, ALU.subtract)
                last.then_inc(hc_ok, 1)
                v.tensor_copy(mv[:, bass.ds(2 * ob, 2), 0], mv2[:, :, 0])
                v.tensor_scalar(mv[:, bass.ds(2 * ob, 2), 1], mv2[:, :, 1], EPS, None, ALU.add).then_inc(mv_ok, 1)

            def copy_gate(ob):
                dve.wait_ge(lg_ps, ob + 1)
                v.tensor_copy(lgraw[:, bass.ds(2 * ob, 2), :],
                              bank[5][0:C, 0:2 * E].rearrange("p (x e) -> p x e", x=2)).then_inc(lg_ok, 1)

            def piece(k, pb, u):
                if k == 0:
                    low_x(pb)
                elif k == 1:
                    cross_products(pb)
                elif k == 5:
                    if not few(pb):
                        add_out(pb - 2)
                elif k in (2, 6):
                    low_q(pb, u, k // 4)
                elif k in (3, 4):
                    low_k(pb, u, k - 3)

            def find_max(b, p):
                for c in range(2):
                    dve.wait_ge(s_ps, 16 * b + 2 * p + c + 1)
                    v.tensor_reduce(mx[:, p, c, :], bank[c][0:C, 0:2 * T].rearrange("p (h t) -> p h t", h=2),
                                    AX.X, ALU.max).then_inc(mx_ok, 1)

            def negate_max(b, p):
                for c in range(2):
                    dve.wait_ge(mx_ok, 16 * b + 2 * p + c + 1)
                    v.tensor_scalar(negmx[:, p, c, :], mx[:, p, c, :], -1.0, None, ALU.mult).then_inc(neg_ok, 1)

            def take_sums(g):
                v.stream_shuffle(den[:, :], bank[4 + g % 2][:, 0:T], [16 + (i % 16) for i in range(32)]).then_inc(den_ok, 1)

            def invert(b, g):
                dve.wait_ge(den_ok, G * b + g + 1)
                v.reciprocal(den[:, :], den[:, :]).then_inc(rden_ok, 1)

            def normalise(b, u, g):
                if g == 0 and not few(b):
                    dve.wait_ge(o_ps, b - 1)
                dve.wait_ge(rden_ok, G * b + g + 1)
                v.tensor_tensor(AO[:, u, g, :], bank[4 + g % 2][:, 0:T], den[:, :], ALU.mult).then_inc(ao_ok, 1)

            AFTER_MAX = (1, 2, 3, 4, 6)

            def batch(b, u, project=True, norm_next=True):
                for s in range(8):
                    if s == 6 and not first(b):
                        dve.wait_ge(h_ok, b)
                    find_max(b, s)
                    complete = s in (4, 6) or (s in (0, 2) and not first(b))
                    of, of_u, g = (b, u, s // 2 - 2) if s >= 4 else (b - 1, 1 - u, s // 2 + 2)
                    if complete:
                        take_sums(g)
                    negate_max(b, s)
                    if project and s - 1 in AFTER_MAX:
                        piece(s - 1, b + 1, 1 - u)
                    if s == 6 and not first(b):
                        moments(b - 1)
                        dve.wait_ge(st2_ok, b)
                    if complete:
                        invert(of, g)
                    if s == 6 and not first(b):
                        centre(b - 1)
                    if complete:
                        normalise(of, of_u, g)
                    if project and s not in AFTER_MAX:
                        piece(s, b + 1, 1 - u)
                    elif s == 5:
                        add_out(b - 1)
                    if s == 7 and not first(b):
                        copy_gate(b - 1)
                    if s == 7 and project and norm_next:
                        normed(b + 2)

            dve.wait_ge(pads_zero, 1)
            normed(0)
            for k in FIRST_ORDER:
                piece(k, 0, 0)
                if k == 0:
                    normed(1)
            batch(0, 0)
            with dve.Fori(0, (B - 2) // 2 - 1) as i:
                batch(2 * i + 1, 1)
                batch(2 * i + 2, 0)
            batch(B - 3, 1)
            batch(B - 2, 0, norm_next=False)
            batch(B - 1, 1, project=False)
            for g in (2, 3):
                dve.wait_ge(ao_ok, G * (B - 1) + g)
                dve.wait_ge(pv_ps, 8 * (B - 1) + 2 * g + 2)
                take_sums(g)
                invert(B - 1, g)
                normalise(B - 1, 1, g)
            add_out(B - 1)
            dve.wait_ge(h_ok, B)
            moments(B - 1)
            dve.wait_ge(st2_ok, B)
            centre(B - 1)
            copy_gate(B - 1)

            count = [0]

            def link(ins):
                count[0] += 1
                ins.then_inc(dve_step, 1)
                dve.wait_ge(dve_step, count[0])

            dve.wait_ge(sd_done, 2)
            link(v.reciprocal(rstd[:, :], sd[:, :]))
            dve.wait_ge(ld_late, 32)
            link(v.tensor_tensor(lg[:, :, :], lgraw[:, :, :], rstd[:, :].unsqueeze(2).to_broadcast([C, NBLK, E]), ALU.mult))
            link(v.tensor_tensor(lg[:, :, :], lg[:, :, :], bg_s[:, :].unsqueeze(1).to_broadcast([C, NBLK, E]), ALU.add))
            link(v.tensor_reduce(lgmax[:, :], lg[:, :, :], AX.X, ALU.max))
            wide = lgmax[:, :].unsqueeze(2).to_broadcast([C, NBLK, E])
            v.tensor_tensor(ex[:, :, :], lg[:, :, :], wide, ALU.subtract).then_inc(lgsub_ok, 1)
            link(v.tensor_tensor(hit[:, :, :], lg[:, :, :], wide, ALU.is_equal))
            link(v.tensor_tensor(hit[:, :, :], hit[:, :, :], con("backward", C).unsqueeze(1).to_broadcast([C, NBLK, E]), ALU.mult))
            link(v.tensor_reduce(firsthit[:, :], hit[:, :, :], AX.X, ALU.max))
            link(v.tensor_tensor(onehot[:, :, :].rearrange("p e b -> p b e"), hit[:, :, :],
                                 firsthit[:, :].unsqueeze(2).to_broadcast([C, NBLK, E]), ALU.is_equal))
            link(v.tensor_tensor_scan(upto[:, :, :].rearrange("p e b -> p (e b)"), con("restart", C),
                                      onehot[:, :, :].rearrange("p e b -> p (e b)"), 0.0, ALU.mult, ALU.add))
            v.tensor_tensor(earlier[:, :, :], upto[:, :, :], onehot[:, :, :], ALU.subtract).then_inc(hot_ok, 1)
            dve.wait_ge(ex_ok, 1)
            link(v.tensor_reduce(exsum[:, :], ex[:, :, :], AX.X, ALU.add))
            v.tensor_copy(tab[:, :, 1], mv[:, :, 0])
            v.tensor_copy(tab[:, :, 2], rstd[:, :])
            v.reciprocal(tab[:, :, 0], exsum[:, :]).then_inc(tab_ok, 1)
            dve.wait_ge(rank_ps, 1)
            link(v.tensor_tensor(ntiles_cmp[:, :, :], bank[4][:, 0:E].unsqueeze(2).to_broadcast([P, E, 11]),
                                 con("tile_start")[:, 0:11].unsqueeze(1).to_broadcast([P, E, 11]), ALU.is_gt))
            link(v.tensor_reduce(ntiles[:, :], ntiles_cmp[:, :, :], AX.X, ALU.add))
            link(v.tensor_tensor_scan(tiles_upto[:, :], con("full")[:, 0:E], ntiles[:, :], 0.0, ALU.mult, ALU.add))
            link(v.tensor_tensor(base[:, :], tiles_upto[:, :], ntiles[:, :], ALU.subtract))
            link(v.scalar_tensor_tensor(posn[:, :, :], base[0:C, :].unsqueeze(2).to_broadcast([C, E, NBLK]), float(SLOTS),
                                        bank[3][0:C, 0:E * NBLK].rearrange("p (e b) -> p e b", e=E), ALU.mult, ALU.add))
            link(v.tensor_tensor(posn[:, :, :], posn[:, :, :], onehot[:, :, :], ALU.mult))
            link(v.tensor_reduce(pos[:, :], posn[:, :, :].rearrange("p e b -> p b e"), AX.X, ALU.add))
            link(v.tensor_tensor(tile_cmp[:, :, :], pos[:, :].unsqueeze(2).to_broadcast([C, NBLK, TILES - 1]),
                                 con("tile_start", C)[:, 1:TILES].unsqueeze(1).to_broadcast([C, NBLK, TILES - 1]), ALU.is_ge))
            link(v.tensor_reduce(tile_of[:, :], tile_cmp[:, :, :], AX.X, ALU.add))
            link(v.scalar_tensor_tensor(slot_of[:, :], tile_of[:, :], -float(SLOTS), pos[:, :], ALU.mult, ALU.add))
            link(v.tensor_tensor(tile_hot[:, :, :], con("iota", C)[:, 0:TILES].unsqueeze(1).to_broadcast([C, NBLK, TILES]),
                                 tile_of[:, :].unsqueeze(2).to_broadcast([C, NBLK, TILES]), ALU.is_equal))
            v.tensor_tensor(tile_ids[:, :, :], tile_hot[:, :, :],
                            con("tokid", C).unsqueeze(2).to_broadcast([C, NBLK, TILES]), ALU.mult)
            for k in range(0, NBLK, 4):
                v.tensor_tensor(slot_hot[:, k:k + 4, :], con("iota", C).unsqueeze(1).to_broadcast([C, 4, SLOTS]),
                                slot_of[:, k:k + 4].unsqueeze(2).to_broadcast([C, 4, SLOTS]),
                                ALU.is_equal).then_inc(slots_hot, 1)
            link(v.tensor_tensor(et_cmp[:, :, :], tiles_upto[0:1, :].unsqueeze(1).to_broadcast([1, TILES, E]),
                                 con("iota", 1)[:, 0:TILES].unsqueeze(2).to_broadcast([1, TILES, E]), ALU.is_le))
            link(v.tensor_reduce(et_f[:, :], et_cmp[:, :, :], AX.X, ALU.add))
            v.tensor_scalar(et[:, :], et_f[:, :], float(E - 1), None, ALU.min).then_inc(et_ok, 1)
            dve.wait_ge(slots_ps, 1)
            v.tensor_scalar(ids[:, :], bank[5][:, 0:TILES], float(NTOK), None, ALU.add).then_inc(ids_ok, 1)

            def expert(t):
                return dve.value_load(et[0:1, bass.ds(t, 1)], min_val=0, max_val=E - 1)

            def tile_bias(t, e):
                if not first(t):
                    dve.wait_ge(silu_ok, HC * t)
                v.tensor_copy(b1c[:, :].unsqueeze(1), smal("b1").rearrange("p (e k) -> p e k", e=E)[:, bass.ds(e, 1), :]).then_inc(b1_ok, 1)

            def copy_hidden(t):
                if not first(t):
                    dve.wait_ge(zt_ps, 2 * t)
                for n in range(2):
                    dve.wait_ge(l1_ps, 2 * t + n + 1)
                    v.tensor_copy(z[:, 512 * n:512 * n + 512], bank[n][:, :]).then_inc(z_ok, 1)

            def norm_tile(t, i, c):
                place = hrow[:, c % RING, :]
                dve.wait_ge(rows_in[c % RING], 16 * (i + c // RING + 1))
                if not first(t):
                    dve.wait_ge(tx_ps, t)
                v.tensor_scalar(xn[:, :], place[:, 0:D], place[:, D + 1:D + 2], place[:, D + 2:D + 3],
                                ALU.subtract, ALU.mult).then_inc(xn_ok, 1)

            def finish(t, c, e):
                place = hrow[:, c % RING, :]
                dve.wait_ge(l2_ps, t + 1)
                if not first(t):
                    dve.wait_ge(y_ok, t)
                v.tensor_tensor(y1[:, :].unsqueeze(1), bank[4][:, 0:D].unsqueeze(1), b2_s[:, bass.ds(e, 1), :],
                                ALU.add).then_inc(y1_ok, 1)
                if not first(t):
                    dve.wait_ge(sc_out, 16 * t)
                dve.wait_ge(y1_ok, t + 1)
                v.scalar_tensor_tensor(Y[:, :], y1[:, :], place[:, D:D + 1], place[:, 0:D], ALU.mult, ALU.add).then_inc(y_ok, 1)

            def tile(t, i, c):
                norm_tile(t + 1, i, c + 1)
                copy_hidden(t)
                tile_bias(t, expert(t))
                finish(t - 1, c - 1, expert(t - 1))

            dve.wait_ge(et_ok, 1)
            norm_tile(0, 0, 0)
            norm_tile(1, 0, 1)
            copy_hidden(0)
            tile_bias(0, expert(0))
            dve.wait_ge(ld_b2, 16)
            LOOPS = (TILES - 2) // RING
            with dve.Fori(0, LOOPS) as i:
                for c in range(1, RING + 1):
                    tile(RING * i + c, i, c)
            for t in range(RING * LOOPS + 1, TILES):
                if t + 1 < TILES:
                    norm_tile(t + 1, 0, t + 1)
                copy_hidden(t)
                tile_bias(t, expert(t))
                finish(t - 1, t - 1, expert(t - 1))
            finish(TILES - 1, TILES - 1, expert(TILES - 1))

        @block.gpsimd
        def _(pool):
            g = nc.gpsimd
            g.memset(kb[:, :, :, :, :].bitcast(F32), 0.0)
            g.memset(qb[:, :, :, :].bitcast(F32), 0.0)
            g.memset(xhat[:, :, :], 0.0)
            g.memset(pr[:, :, :, :, :], 0.0)
            g.memset(prt[:, :, :, :], 0.0)
            g.memset(V[:, :, :, :, :], 0.0).then_inc(v_zero, 1)
            pool.wait_ge(v_zero, 1)
            g.memset(V[0:C, :, :, :, HD:32], 1.0).then_inc(pads_zero, 1)

            pool.wait_ge(parts_hi, 1)
            g.tensor_tensor(wkl[:, :, :], wkp_s[:, :, :], wkh[:, :, :].bitcast(F32), ALU.subtract)
            g.tensor_tensor(wvl[:, :, :], wvt_s[:, :, :], wvh[:, :, :].bitcast(F32), ALU.subtract).then_inc(parts_lo, 1)

            def parts_of_products(pb):
                pool.wait_ge(prod_ok, pb + 1)
                g.tensor_tensor(prodh[:, :], prod, con("full")[:, 0:1].to_broadcast([P, T]), ALU.mult).then_inc(prodh_ok, 1)
                pool.wait_ge(prodh_ok, pb + 1)
                g.tensor_tensor(prodl[:, :], prod, prodh[:, :].bitcast(F32), ALU.subtract).then_inc(prods_ok, 1)

            def add_out_bias(b):
                rows = Hs[:, bass.ds(2 * b, 2), :]
                g.tensor_tensor(rows, rows, obias[:, :].unsqueeze(1).to_broadcast([C, 2, D]), ALU.add).then_inc(hb_ok, 1)

            def prepare(pb, u):
                parts_of_products(pb)
                pool.wait_ge(xhat_ok, pb + 1)
                pool.wait_ge(ql_ok, 2 * pb + 1)
                add_out_bias(pb)
                stack_q(g, pb, u, 0, BY_POOL)

            pool.wait_ge(parts_done, 1)
            prepare(0, 0)
            with pool.Fori(0, (B - 2) // 2) as i:
                prepare(2 * i + 1, 1)
                prepare(2 * i + 2, 0)
            prepare(B - 1, 1)

            def gather(t):
                g.indirect_dma_start(out=hrow[:, t % RING, :], out_offset=None, in_=rows_dram,
                                     in_offset=bass.IndirectOffsetOnAxis(ap=ids[:, t:t + 1], axis=0)
                                     ).then_inc(rows_in[t % RING], 16)

            def scatter(t):
                pool.wait_ge(y_ok, t + 1)
                g.indirect_dma_start(out=out_rows, out_offset=bass.IndirectOffsetOnAxis(ap=ids[:, t:t + 1], axis=0),
                                     in_=Y[:, :], in_offset=None, bounds_check=NTOK - 1, oob_is_err=False).then_inc(sc_out, 16)

            pool.wait_ge(rows_out, 16 * ROWS)
            pool.wait_ge(ids_ok, 1)
            for t in range(RING):
                gather(t)
            for t in range(TILES):
                scatter(t)
                if t + RING < TILES:
                    gather(t + RING)
            pool.wait_ge(sc_out, 16 * TILES)


def kernel(x, txt, L0_tok_W, L0_tok_b, L0_tok_pos_embd, L0_attn_Wq, L0_attn_bq, L0_attn_Wk, L0_attn_bk, L0_attn_Wv,
           L0_attn_bv, L0_attn_Wo, L0_attn_bo, L0_attn_Wqs, L0_attn_bqs, L0_attn_Wks, L0_attn_bks, L0_attn_Wvs,
           L0_attn_bvs, L0_attn_temp, L0_ffn_Wg, L0_ffn_bg, L0_ffn_W1, L0_ffn_b1, L0_ffn_W2, L0_ffn_b2):
    import concourse.bacc as bacc
    from concourse.bass_utils import run_bass_kernel_spmd

    f = np.float32
    wq, wk, wv, wo = (np.asarray(w) for w in (L0_attn_Wq, L0_attn_Wk, L0_attn_Wv, L0_attn_Wo))
    n = IMG // PATCH
    patches = np.asarray(x).reshape(B, CH, n, PATCH, n, PATCH).transpose(1, 3, 5, 0, 2, 4).reshape(PD, B * NIMG)
    wk_pad = np.zeros((D, H, 32), f)
    wk_pad[:, :, :HD] = wk.T.reshape(D, H, HD)
    wo_pad = np.zeros((H, 32, D), f)
    wo_pad[:, :HD] = wo.T.reshape(H, HD, D)
    mq = np.zeros((8, HD, 8, 32), f)
    ma = np.zeros((2, 8, HD, P), f)
    mb = np.zeros((2, 8, HD, P), f)
    wqs, wks, wvs = (np.asarray(w) for w in (L0_attn_Wqs, L0_attn_Wks, L0_attn_Wvs))
    bqs, bks, bvs = (np.asarray(w) for w in (L0_attn_bqs, L0_attn_bks, L0_attn_bvs))
    bqs_rows, bks_rows, bvs_rows = np.zeros((4, 32), f), np.zeros(P, f), np.zeros(P, f)
    bqs_rows[:, HD:HD + 3] = bqs
    for h in range(8):
        mq[h, :, h, :HD] = np.eye(HD, dtype=f)
        mq[h, :, h, HD:HD + 3] = wqs.T
    for h in range(H):
        for c in range(3):
            c1, c2 = (c + 1) % 3, (c + 2) % 3
            lo, hi = 3 * h + c, 64 + 3 * h + c
            ma[h // 8, h % 8, :, lo], ma[h // 8, h % 8, :, hi] = wks[c1], wks[c2]
            mb[h // 8, h % 8, :, lo], mb[h // 8, h % 8, :, hi] = wvs[c2], wvs[c1]
            bks_rows[lo], bks_rows[hi] = bks[c1], bks[c2]
            bvs_rows[lo], bvs_rows[hi] = bvs[c2], bvs[c1]
    bk_rows = np.zeros((G, 4, 32), f)
    bk_rows[:, :, :HD] = np.asarray(L0_attn_bk).reshape(G, 4, HD)
    small = np.zeros((P, SMALL_W), f)
    for name, value in (
        ("bq", np.asarray(L0_attn_bq).reshape(2, P).T), ("bk", np.asarray(L0_attn_bk).reshape(2, P).T),
        ("bv", np.asarray(L0_attn_bv).reshape(2, P).T), ("bk_rows", bk_rows.reshape(G, P).T),
        ("bqs_rows", bqs_rows.reshape(P, 1)), ("bks_rows", bks_rows.reshape(P, 1)), ("bvs_rows", bvs_rows.reshape(P, 1)),
        ("temp", np.broadcast_to(np.asarray(L0_attn_temp), (P, 1))),
        ("b1", np.asarray(L0_ffn_b1).reshape(E, HC, P).transpose(2, 0, 1).reshape(P, E * HC)),
        ("wg", np.asarray(L0_ffn_Wg).reshape(DC, P, E).transpose(1, 0, 2).reshape(P, DC * E)),
    ):
        a, b = SMALL[name]
        small[:, a:b] = value
    arrays = {
        "patches": patches, "tok_wt": np.asarray(L0_tok_W).T, "tok_b": np.asarray(L0_tok_b),
        "pos3": np.concatenate([np.asarray(L0_tok_pos_embd)[0]] * EB), "txt": np.asarray(txt),
        "const": host_constants()[0], "late": host_constants()[1], "sel": host_selection(), "small": small, "wq": wq, "wk": wk, "wv": wv,
        "wk_pad": wk_pad.reshape(D, 512), "wv_t": wv.T, "wo_t": wo.T, "wo_pad": wo_pad.reshape(512, D),
        "mq": mq.reshape(P, D), "ma": ma.reshape(2, P, P).transpose(1, 0, 2), "mb": mb.reshape(2, P, P).transpose(1, 0, 2),
        "bo": np.asarray(L0_attn_bo), "bg": np.asarray(L0_ffn_bg), "w1": np.asarray(L0_ffn_W1),
        "w2": np.asarray(L0_ffn_W2), "b2": np.asarray(L0_ffn_b2),
    }
    arrays = {k: np.ascontiguousarray(a) for k, a in arrays.items()}
    nc = bacc.Bacc("TRN2", target_bir_lowering=False, num_devices=1)
    args = {k: nc.dram_tensor(f"in_{k}", a.shape, mybir.dt.from_np(a.dtype), kind="ExternalInput").ap()
            for k, a in arrays.items()}
    out = nc.dram_tensor("out_0", (B, T, D), F32, kind="ExternalOutput").ap()
    program(nc, out=out, **args)
    r = run_bass_kernel_spmd(nc, [{f"in_{k}": a for k, a in arrays.items()}], core_ids=[0])
    return r.results[0]["out_0"]
```
